# Optimizing a Trainium2 kernel written in Bass

```python
import numpy as np
import jax
import jax.numpy as jnp

def _softmax(x, axis=-1):
    return jax.nn.softmax(x, axis=axis)

def _gelu(x):
    return jax.nn.gelu(x, approximate=True)

def _silu(x):
    return jax.nn.silu(x)

def _sigmoid(x):
    return jax.nn.sigmoid(x)

def _layernorm(x, axis=-1, eps=1e-05):
    m = jnp.mean(x, axis=axis, keepdims=True)
    v = jnp.var(x, axis=axis, keepdims=True)
    return (x - m) / jnp.sqrt(v + eps)

def _scatter_add(tgt, idx, src, axis=0):
    return tgt.at[idx].add(src)

def _segment_sum(src, seg, n):
    return jax.ops.segment_sum(src, seg, n)
kernel_name = 'mk_xattn_ffn_d2_seqx_r4_153a5c'

def setup_inputs(seed: int=0):
    np.random.seed(seed)
    _w = jnp.asarray

    def _rec_inputs():
        import jax
        import jax.numpy as jnp
        _rk = jax.random.key(seed)
        x = -0.0002928 + 1 * jax.random.normal(jax.random.fold_in(_rk, 1), (2, 1024, 256), jnp.float32)
        _lenS = 1024 - jax.random.randint(jax.random.fold_in(_rk, 7), (2,), 0, max(1, 1024 // 4) + 1, jnp.int32)
        _lenS2 = 77 - jax.random.randint(jax.random.fold_in(_rk, 8), (2,), 0, max(1, 77 // 4) + 1, jnp.int32)
        _ctx_768P = jax.random.normal(jax.random.fold_in(_rk, 11), (2, 16, 192), jnp.float32)
        _ctx_768c = jax.random.dirichlet(jax.random.fold_in(_rk, 511), 0.3 * jnp.ones((16,), jnp.float32), (2, 77))
        _ctx_768t = jnp.einsum('bsk,bkd->bsd', _ctx_768c, _ctx_768P)
        _ctx_768t = _ctx_768t * jax.lax.rsqrt(jnp.mean(jnp.square(_ctx_768t)) + 1e-12) * 0.953939
        ctx_768 = 2.09791e-05 + 1.00001 * (_ctx_768t + 0.3 * jax.random.normal(jax.random.fold_in(_rk, 611), (2, 77, 192), jnp.float32))
        return (x, ctx_768)
    x, ctx_768 = _rec_inputs()

    def _L0_xattn_setup():
        import jax, jax.numpy as jnp
        import numpy as np
        N_HEADS = 16
        DIMS = 256
        D_CTX = 192
        HEAD = DIMS // N_HEADS
        key = jax.random.key(seed)
        ks = jax.random.split(key, 10)
        s_q = 1.0 / np.sqrt(DIMS)
        s_c = 1.0 / np.sqrt(D_CTX)
        return {'x': jax.random.normal(ks[0], (2, 512, DIMS), jnp.float32), 'context': jax.random.normal(ks[1], (2, 512, D_CTX), jnp.float32), 'w_q': jax.random.normal(ks[2], (DIMS, DIMS), jnp.float32) * s_q, 'b_q': jax.random.normal(ks[3], (DIMS,), jnp.float32) * 0.01, 'w_k': jax.random.normal(ks[4], (D_CTX, DIMS), jnp.float32) * s_c, 'b_k': jax.random.normal(ks[5], (DIMS,), jnp.float32) * 0.01, 'w_v': jax.random.normal(ks[6], (D_CTX, DIMS), jnp.float32) * s_c, 'b_v': jax.random.normal(ks[7], (DIMS,), jnp.float32) * 0.01, 'w_o': jax.random.normal(ks[8], (DIMS, DIMS), jnp.float32) * s_q, 'b_o': jax.random.normal(ks[9], (DIMS,), jnp.float32) * 0.01}
    _L0_xattn_all = _L0_xattn_setup()
    _L0_xattn_in = {k: v for k, v in _L0_xattn_all.items() if k in ('w_q', 'b_q', 'w_k', 'b_k', 'w_v', 'b_v', 'w_o', 'b_o')}
    del _L0_xattn_all

    def _L0_ffn_setup():
        import jax, jax.numpy as jnp
        import numpy as np
        B, S, D, F, E = (2, 512, 256, 1024, 8)
        LN_EPS = 1e-05

        def _xavier(key, shape, fan_in, fan_out):
            a = np.sqrt(6.0 / (fan_in + fan_out))
            return jax.random.uniform(key, shape, jnp.float32, -a, a)
        key = jax.random.key(seed)
        ks = jax.random.split(key, 8)
        tgt = jax.random.normal(ks[0], (B, S, D), jnp.float32)
        router_w = _xavier(ks[1], (E, D), D, E)
        router_b = jnp.zeros((E,), jnp.float32)
        w1 = _xavier(ks[2], (E, D, F), D, F)
        b1 = jnp.zeros((E, F), jnp.float32)
        w2 = _xavier(ks[3], (E, F, D), F, D)
        b2 = jnp.zeros((E, D), jnp.float32)
        gamma = jnp.ones((D,), jnp.float32)
        beta = jnp.zeros((D,), jnp.float32)
        return {'tgt': tgt, 'router_w': router_w, 'router_b': router_b, 'w1': w1, 'b1': b1, 'w2': w2, 'b2': b2, 'gamma': gamma, 'beta': beta}
    _L0_ffn_all = _L0_ffn_setup()
    _L0_ffn_in = {k: v for k, v in _L0_ffn_all.items() if k in ('router_w', 'router_b', 'w1', 'b1', 'w2', 'b2', 'gamma', 'beta')}
    del _L0_ffn_all

    def _L1_xattn_setup():
        import jax, jax.numpy as jnp
        import numpy as np
        EPS = 1e-05

        def layernorm(x, g, b):
            mu = jnp.mean(x, axis=-1, keepdims=True)
            var = jnp.mean(jnp.square(x - mu), axis=-1, keepdims=True)
            return (x - mu) * jax.lax.rsqrt(var + EPS) * g + b
        key = jax.random.key(seed)
        ks = jax.random.split(key, 12)
        B, L1, L2 = (8, 512, 512)
        D1, D2, E = (256, 192, 256)
        s1, s2, se = (D1 ** (-0.5), D2 ** (-0.5), E ** (-0.5))
        return {'modality1': jax.random.normal(ks[0], (B, L1, D1), jnp.float32), 'modality2': jax.random.normal(ks[1], (B, L2, D2), jnp.float32), 'ln1_g': jnp.ones((D1,), jnp.float32), 'ln1_b': jnp.zeros((D1,), jnp.float32), 'ln2_g': jnp.ones((D2,), jnp.float32), 'ln2_b': jnp.zeros((D2,), jnp.float32), 'Wq': jax.random.normal(ks[2], (D1, E), jnp.float32) * s1, 'bq': jax.random.normal(ks[3], (E,), jnp.float32) * 0.01, 'Wk': jax.random.normal(ks[4], (D2, E), jnp.float32) * s2, 'bk': jax.random.normal(ks[5], (E,), jnp.float32) * 0.01, 'Wv': jax.random.normal(ks[6], (D2, E), jnp.float32) * s2, 'bv': jax.random.normal(ks[7], (E,), jnp.float32) * 0.01, 'Wo': jax.random.normal(ks[8], (E, D1), jnp.float32) * se, 'bo': jax.random.normal(ks[9], (D1,), jnp.float32) * 0.01}
    _L1_xattn_all = _L1_xattn_setup()
    _L1_xattn_in = {k: v for k, v in _L1_xattn_all.items() if k in ('ln1_g', 'ln1_b', 'ln2_g', 'ln2_b', 'Wq', 'bq', 'Wk', 'bk', 'Wv', 'bv', 'Wo', 'bo')}
    del _L1_xattn_all

    def _L1_ffn_setup():
        import math
        import jax, jax.numpy as jnp
        import numpy as np
        D_CONTENT = 256
        D_POSITION = 32
        NUM_TILES = 8
        BATCH = 8
        SEQ = 512

        def make_pe(seq_len, d_pos):
            pos = jnp.arange(seq_len, dtype=jnp.float32)[:, None]
            div = jnp.exp(jnp.arange(0, d_pos, 2, dtype=jnp.float32) * (-math.log(10000.0) / d_pos))
            ang = pos * div
            pe = jnp.zeros((seq_len, d_pos), dtype=jnp.float32)
            pe = pe.at[:, 0::2].set(jnp.sin(ang))
            pe = pe.at[:, 1::2].set(jnp.cos(ang))
            return pe
        key = jax.random.key(seed)
        k1, k2, k3, k4 = jax.random.split(key, 4)
        x = jax.random.normal(k1, (BATCH, SEQ, D_CONTENT), dtype=jnp.float32)
        tile_sigs = jax.random.normal(k2, (NUM_TILES, D_POSITION), dtype=jnp.float32)
        lim = 1.0 / math.sqrt(D_CONTENT)
        W = jax.random.uniform(k3, (NUM_TILES, D_CONTENT, D_CONTENT), minval=-lim, maxval=lim, dtype=jnp.float32)
        b = jax.random.uniform(k4, (NUM_TILES, D_CONTENT), minval=-lim, maxval=lim, dtype=jnp.float32)
        return {'x': x, 'tile_sigs': tile_sigs, 'W': W, 'b': b}
    _L1_ffn_all = _L1_ffn_setup()
    _L1_ffn_in = {k: v for k, v in _L1_ffn_all.items() if k in ('tile_sigs', 'W', 'b')}
    del _L1_ffn_all
    return {'x': x, 'ctx_768': ctx_768, 'L0_xattn_w_q': _L0_xattn_in['w_q'], 'L0_xattn_b_q': _L0_xattn_in['b_q'], 'L0_xattn_w_k': _L0_xattn_in['w_k'], 'L0_xattn_b_k': _L0_xattn_in['b_k'], 'L0_xattn_w_v': _L0_xattn_in['w_v'], 'L0_xattn_b_v': _L0_xattn_in['b_v'], 'L0_xattn_w_o': _L0_xattn_in['w_o'], 'L0_xattn_b_o': _L0_xattn_in['b_o'], 'L0_ffn_router_w': _L0_ffn_in['router_w'], 'L0_ffn_router_b': _L0_ffn_in['router_b'], 'L0_ffn_w1': _L0_ffn_in['w1'], 'L0_ffn_b1': _L0_ffn_in['b1'], 'L0_ffn_w2': _L0_ffn_in['w2'], 'L0_ffn_b2': _L0_ffn_in['b2'], 'L0_ffn_gamma': _L0_ffn_in['gamma'], 'L0_ffn_beta': _L0_ffn_in['beta'], 'L1_xattn_ln1_g': _L1_xattn_in['ln1_g'], 'L1_xattn_ln1_b': _L1_xattn_in['ln1_b'], 'L1_xattn_ln2_g': _L1_xattn_in['ln2_g'], 'L1_xattn_ln2_b': _L1_xattn_in['ln2_b'], 'L1_xattn_Wq': _L1_xattn_in['Wq'], 'L1_xattn_bq': _L1_xattn_in['bq'], 'L1_xattn_Wk': _L1_xattn_in['Wk'], 'L1_xattn_bk': _L1_xattn_in['bk'], 'L1_xattn_Wv': _L1_xattn_in['Wv'], 'L1_xattn_bv': _L1_xattn_in['bv'], 'L1_xattn_Wo': _L1_xattn_in['Wo'], 'L1_xattn_bo': _L1_xattn_in['bo'], 'L1_ffn_tile_sigs': _L1_ffn_in['tile_sigs'], 'L1_ffn_W': _L1_ffn_in['W'], 'L1_ffn_b': _L1_ffn_in['b']}

def reference(x, ctx_768, L0_xattn_w_q, L0_xattn_b_q, L0_xattn_w_k, L0_xattn_b_k, L0_xattn_w_v, L0_xattn_b_v, L0_xattn_w_o, L0_xattn_b_o, L0_ffn_router_w, L0_ffn_router_b, L0_ffn_w1, L0_ffn_b1, L0_ffn_w2, L0_ffn_b2, L0_ffn_gamma, L0_ffn_beta, L1_xattn_ln1_g, L1_xattn_ln1_b, L1_xattn_ln2_g, L1_xattn_ln2_b, L1_xattn_Wq, L1_xattn_bq, L1_xattn_Wk, L1_xattn_bk, L1_xattn_Wv, L1_xattn_bv, L1_xattn_Wo, L1_xattn_bo, L1_ffn_tile_sigs, L1_ffn_W, L1_ffn_b):
    import jax
    import jax.numpy as jnp

    def _L0_xattn_ref(x, context, w_q, b_q, w_k, b_k, w_v, b_v, w_o, b_o):
        import jax, jax.numpy as jnp
        import numpy as np
        N_HEADS = 16
        DIMS = 256
        D_CTX = 192
        HEAD = DIMS // N_HEADS
        B, Lq, D = x.shape
        q = x @ w_q + b_q
        k = context @ w_k + b_k
        v = context @ w_v + b_v
        q = q.reshape(B, Lq, N_HEADS, HEAD)
        k = k.reshape(B, -1, N_HEADS, HEAD)
        v = v.reshape(B, -1, N_HEADS, HEAD)
        scale = 1.0 / np.sqrt(HEAD).astype(np.float32)
        scores = jnp.einsum('bqhd,bkhd->bhqk', q, k) * scale
        weights = jax.nn.softmax(scores, axis=-1)
        out = jnp.einsum('bhqk,bkhd->bqhd', weights, v).reshape(B, Lq, D)
        return out @ w_o + b_o

    def _L0_ffn_ref(tgt, router_w, router_b, w1, b1, w2, b2, gamma, beta):
        import jax, jax.numpy as jnp
        import numpy as np
        B, S, D, F, E = (2, 512, 256, 1024, 8)
        LN_EPS = 1e-05

        def _xavier(key, shape, fan_in, fan_out):
            a = np.sqrt(6.0 / (fan_in + fan_out))
            return jax.random.uniform(key, shape, jnp.float32, -a, a)
        logits = jnp.einsum('bsd,ed->bse', tgt, router_w) + router_b
        rw = jax.nn.softmax(logits, axis=-1)
        rw = jnp.zeros_like(rw).at[..., 0].set(1.0)
        h = jax.nn.relu(jnp.einsum('bsd,edf->besf', tgt, w1) + b1[None, :, None, :])
        eo = jnp.einsum('besf,efd->besd', h, w2) + b2[None, :, None, :]
        tgt2 = jnp.einsum('besd,bse->bsd', eo, rw)
        x = tgt + tgt2
        mean = jnp.mean(x, axis=-1, keepdims=True)
        var = jnp.mean(jnp.square(x - mean), axis=-1, keepdims=True)
        return (x - mean) * jax.lax.rsqrt(var + LN_EPS) * gamma + beta

    def _L1_xattn_ref(modality1, modality2, ln1_g, ln1_b, ln2_g, ln2_b, Wq, bq, Wk, bk, Wv, bv, Wo, bo):
        import jax, jax.numpy as jnp
        import numpy as np
        EPS = 1e-05

        def layernorm(x, g, b):
            mu = jnp.mean(x, axis=-1, keepdims=True)
            var = jnp.mean(jnp.square(x - mu), axis=-1, keepdims=True)
            return (x - mu) * jax.lax.rsqrt(var + EPS) * g + b
        E = Wq.shape[1]
        scaling = E ** (-0.5)
        x1 = layernorm(modality1, ln1_g, ln1_b)
        x2 = layernorm(modality2, ln2_g, ln2_b)
        q = x1 @ Wq + bq
        k = x2 @ Wk + bk
        v = x2 @ Wv + bv
        scores = jnp.einsum('bqe,bke->bqk', q, k) * scaling
        attn = jax.nn.softmax(scores, axis=-1)
        ctx = jnp.einsum('bqk,bke->bqe', attn, v)
        return ctx @ Wo + bo

    def _L1_ffn_ref(x, tile_sigs, W, b):
        import math
        import jax, jax.numpy as jnp
        import numpy as np
        D_CONTENT = 256
        D_POSITION = 32
        NUM_TILES = 8
        BATCH = 8
        SEQ = 512

        def make_pe(seq_len, d_pos):
            pos = jnp.arange(seq_len, dtype=jnp.float32)[:, None]
            div = jnp.exp(jnp.arange(0, d_pos, 2, dtype=jnp.float32) * (-math.log(10000.0) / d_pos))
            ang = pos * div
            pe = jnp.zeros((seq_len, d_pos), dtype=jnp.float32)
            pe = pe.at[:, 0::2].set(jnp.sin(ang))
            pe = pe.at[:, 1::2].set(jnp.cos(ang))
            return pe
        B, S, D = x.shape
        P = tile_sigs.shape[1]
        pe = make_pe(S, P)
        scores = jnp.einsum('sp,tp->st', pe, jnp.sign(tile_sigs))
        idx = jnp.argmax(scores, axis=-1)
        y_all = jnp.einsum('bsd,tod->bsto', x, W) + b
        idx4 = jnp.broadcast_to(idx[None, :, None, None], (B, S, 1, D))
        out = jnp.take_along_axis(y_all, idx4, axis=2)[:, :, 0]
        return out
    x = x + _L0_xattn_ref(_layernorm(x, axis=-1), ctx_768, L0_xattn_w_q, L0_xattn_b_q, L0_xattn_w_k, L0_xattn_b_k, L0_xattn_w_v, L0_xattn_b_v, L0_xattn_w_o, L0_xattn_b_o)
    x = x + _L0_ffn_ref(_layernorm(x, axis=-1), L0_ffn_router_w, L0_ffn_router_b, L0_ffn_w1, L0_ffn_b1, L0_ffn_w2, L0_ffn_b2, L0_ffn_gamma, L0_ffn_beta)
    x = x + _L1_xattn_ref(_layernorm(x, axis=-1), ctx_768, L1_xattn_ln1_g, L1_xattn_ln1_b, L1_xattn_ln2_g, L1_xattn_ln2_b, L1_xattn_Wq, L1_xattn_bq, L1_xattn_Wk, L1_xattn_bk, L1_xattn_Wv, L1_xattn_bv, L1_xattn_Wo, L1_xattn_bo)
    x = x + _L1_ffn_ref(_layernorm(x, axis=-1), L1_ffn_tile_sigs, L1_ffn_W, L1_ffn_b)
    return x

_drawn_inputs = setup_inputs


def setup_inputs(seed=0):
    import zlib

    import numpy as np

    out = dict(_drawn_inputs(seed))
    spreads = {'L0_ffn_router_b': (0.0, 0.1),
     'L0_ffn_b1': (0.0, 0.1),
     'L0_ffn_b2': (0.0, 0.1),
     'L0_ffn_gamma': (1.0, 0.2),
     'L0_ffn_beta': (0.0, 0.1),
     'L1_xattn_ln1_g': (1.0, 0.6),
     'L1_xattn_ln1_b': (0.0, 0.738),
     'L1_xattn_ln2_g': (1.0, 0.2),
     'L1_xattn_ln2_b': (0.0, 0.1)}
    factors = {'L0_xattn_b_q': 31.726,
     'L0_xattn_b_k': 64.0,
     'L0_xattn_b_v': 7.606,
     'L0_xattn_b_o': 7.08,
     'L1_xattn_bq': 61.846,
     'L1_xattn_bk': 64.0,
     'L1_xattn_bv': 8.0,
     'L1_xattn_bo': 8.0,
     'L1_ffn_b': 3.905}
    for name, (base, spread) in spreads.items():
        noise = np.random.default_rng([zlib.crc32(name.encode()), seed]).standard_normal(out[name].shape)
        drawn = base * np.exp(spread * noise) if base else spread * noise
        out[name] = jnp.asarray(drawn.astype(out[name].dtype))
    for name, factor in factors.items():
        out[name] = (out[name] * factor).astype(out[name].dtype)
    return out
```

```python
from contextlib import ExitStack

import numpy as np
import concourse.bass as bass
from concourse import mybir

F32 = mybir.dt.float32
F32R = mybir.dt.float32r
ALU = mybir.AluOpType
ACT = mybir.ActivationFunctionType
AX = mybir.AxisListType.X

NX = 3
NXT = 4
NG = 8
NK = 77
EPS = 1e-5
CW = 124
CM = [124, 124, 124, 124, 120]
PERIOD = 30.0
AT = dict(a1=0, a2=4, s0=8, t0=12, s1=13, t1=17, pv=21, wo=25, b1=27, w1=32, w2=38, b3=44,
          c1=48, c2=52, c3=57, d1=60, d2=65)


BUSY = "busy"


class Slots:

    def __init__(self, n):
        self.open = [(k, None) for k in range(n)]

    def take(self):
        assert self.open, "too few buffers"
        return self.open.pop(0)

    def give(self, k, token):
        self.open.append((k, token))


class Queue:

    def __init__(self, sem):
        self.sem, self.count, self.code, self.seen = sem, 0, [], {}

    def wait(self, *tokens):
        for t in tokens:
            if t is None:
                continue
            if isinstance(t, list):
                self.wait(*t)
                continue
            assert t is not BUSY, "a buffer that is still in use"
            sem, value = t
            if self.seen.get(id(sem), 0) < value:
                self.seen[id(sem)] = value
                self.code.append(lambda e, s=sem, v=value: e.wait_ge(s, v))

    def go(self, fn, *tokens):
        self.wait(*tokens)
        self.code.append(fn)

    def do(self, fn, *tokens):
        self.wait(*tokens)
        self.count += 1
        self.code.append(lambda e: fn(e).then_inc(self.sem, 1))
        return (self.sem, self.count)

    def run(self, eng):
        for fn in self.code:
            fn(eng)


def f(ap):
    return ap.bitcast(F32)


def program(nc, A, out, period=PERIOD, at=AT):
    with ExitStack() as ctx:
        def sb(name, shape, dt=F32):
            return ctx.enter_context(nc.sbuf_tensor(name, shape, dt))

        def sem(name):
            return ctx.enter_context(nc.semaphore(name))

        S4 = ctx.enter_context(nc.psum_tensor("S4", [128, 4, 512], F32))
        PT = ctx.enter_context(nc.psum_tensor("PT", [128, 2, 256], F32))
        PA = ctx.enter_context(nc.psum_tensor("PA", [128, 2, 256], F32))
        PB = [ctx.enter_context(nc.psum_tensor(f"PB{i}", [128, 512], F32)) for i in range(2)]

        pe, dve, act, pool = (Queue(sem(n)) for n in ("s_pe", "s_dve", "s_act", "s_pool"))
        sp = Queue(None)

        def load(dst, src):
            s = sem(f"s_ld{len(sp.code)}")
            sp.go(lambda e: e.dma_start(dst, src).then_inc(s, 16))
            return (s, 16)

        ident = sb("ident", [128, 128])
        mask8 = sb("mask8", [128, 8])
        mask5 = sb("mask5", [CW, 5, 8])
        nhalf = sb("nhalf", [128, 2])
        t0 = dve.do(lambda e: e.memset(ident[:, :], 0.0))
        t1 = dve.do(lambda e: e.memset(mask8[:, :], 1.0))
        t2 = dve.do(lambda e: e.memset(mask5[:, :, :], 1.0))
        t_nh = dve.do(lambda e: e.memset(nhalf[:, :], -0.5))
        t_id = pool.do(lambda e: e.affine_select(out=ident[:, :], in_=ident[:, :], compare_op=ALU.not_equal,
                                                 fill=1.0, base=0, pattern=[[-1, 128]], channel_multiplier=1), t0)
        t = pool.do(lambda e: e.affine_select(out=mask8[:, :], in_=mask8[:, :], compare_op=ALU.is_ge, fill=0.0,
                                              base=0, pattern=[[-16, 8]], channel_multiplier=1), t1)
        t_m8 = pool.do(lambda e: e.affine_select(out=mask8[:, :], in_=mask8[:, :], compare_op=ALU.is_ge, fill=0.0,
                                                 base=15, pattern=[[16, 8]], channel_multiplier=-1), t)
        t = pool.do(lambda e: e.affine_select(out=mask5[:, :, :], in_=mask5[:, :, :], compare_op=ALU.is_ge,
                                              fill=0.0, base=0, pattern=[[CW, 5], [-NK, 8]],
                                              channel_multiplier=1), t2)
        t_m5 = pool.do(lambda e: e.affine_select(out=mask5[:, :, :], in_=mask5[:, :, :], compare_op=ALU.is_ge,
                                                 fill=0.0, base=NK - 1, pattern=[[-CW, 5], [NK, 8]],
                                                 channel_multiplier=-1), t)

        X = sb("X", [128, NX, 2, 256])
        x_v = A["x"].rearrange("(g i p) n -> g p i n", i=2, p=128)
        t_x = {0: load(X[:, 0, :, :], x_v[0])}
        ctxT = sb("ctxT", [96, 2, 2 * NK])
        t_ctxT = load(ctxT[:, :, :], A["ctxT"].rearrange("(c p) n -> p c n", p=96))
        RAW = sb("RAW", [128, 2, 1024])
        cols = sb("cols", [128, 24])
        COLS = dict(b_q=0, b_k=2, bk1=4, bq1=6, bv1=8, g1=10, be1=12, b1=14)
        t_cols = load(cols[:, 0:22], A["cols"])
        WKV = sb("WKV", [96, 2, 512])
        t_wkv = load(WKV[:, :, 0:256], A["w_k"].rearrange("(c p) n -> p c n", p=96))
        t_wvv = load(WKV[:, :, 256:512], A["w_v"].rearrange("(c p) n -> p c n", p=96))
        bc = sb("bc", [128, 6, 256])
        BO, B2, BETA, GAMMA, BO1, BV = range(6)
        t_bc = load(bc[:, :, :], A["rows"].rearrange("(a r) n -> a r n", a=1).to_broadcast([128, 6, 256]))

        ring = Slots(2)

        def stage(src, parts, n):
            k, tf = ring.take()
            sp.wait(tf)
            dst = RAW[0:parts, k, 0:n]
            return k, dst, load(dst if len(src.shape) == 2 else dst.rearrange("p (a b) -> p a b", a=src.shape[1]), src)

        def split(H, L, k, raw, t):
            th = act.do(lambda e: e.activation(H, raw, ACT.Copy), t)
            tl = pool.do(lambda e: e.tensor_tensor(L, raw, f(H), ALU.subtract), th, t)
            ring.give(k, tl)
            return tl

        def flat2(T):
            return T.rearrange("p a b -> p (a b)")

        WqH, WqL, WoH, WoL = (sb(n, [128, 2, 256], F32R) for n in ("WqH", "WqL", "WoH", "WoL"))
        W1H, W1L = (sb(n, [128, 2, 1024], F32R) for n in ("W1H", "W1L"))
        W2H, W2L = (sb(n, [128, 8, 256], F32R) for n in ("W2H", "W2L"))
        WDH, WDL = (sb(n, [128, 2, 2048], F32R) for n in ("WDH", "WDL"))
        t_w = {}

        XN = sb("XN", [128, 4, 2, 256])
        XTH = sb("XTH", [128, NXT, 2, 256], F32R)
        XTL = sb("XTL", [128, NXT, 2, 256], F32R)
        E = sb("E", [128, 2, 16, NK])
        ETH = sb("ETH", [CW, 2, 5, 256], F32R)
        ETL = sb("ETL", [CW, 2, 5, 256], F32R)
        RR = sb("RR", [128, 16, 16])
        RT = sb("RT", [128, 2, 256])
        KF = sb("KF", [128, 2, NK])
        KTH = sb("KTH", [128, 2, NK])
        KTL = sb("KTL", [128, 2, NK])
        KBH = sb("KBH", [128, 16, NK], F32R)
        KBL = sb("KBL", [128, 16, NK], F32R)
        VBH = sb("VBH", [CW, 5, 2, 128], F32R)
        VBL = sb("VBL", [CW, 5, 2, 128], F32R)
        CR = RT[0:96, :, 0:2 * CW].rearrange("p a (b t) -> p a b t", b=2)
        HF = sb("HF", [128, 2, 2, 256])
        HH = sb("HH", [128, 8, 256], F32R)
        HL = sb("HL", [128, 8, 256], F32R)
        SM = sb("SM", [128, 10, 2, 10])
        SX = sb("SX", [128, 2, 3, 16])
        ST = sb("ST", [NK, 256])
        PP = sb("PP", [128, 2, NK])
        PS = sb("PS", [128, 4, 2])
        PTT = sb("PTT", [96, 256])
        M1H = sb("M1H", [128, 2, 2, NK], F32R)
        M1L = sb("M1L", [128, 2, 2, NK], F32R)
        M2 = sb("M2", [96, 2, 256])
        cT = sb("cT", [NK, 2])
        OHT = sb("OHT", [8, 256])
        OHM = sb("OHM", [128, 8, 8])

        free = {n: None for n in ("PT", "PA", 0, 1, "S4", "ET", "RR", "RT", "HH", "KF", "OHT",
                                  "ST", "PP", "PTT", "KB", "VB", "CR0", "CR1", "HF0", "HF1", "E0", "E1")}
        xfree = {}
        bank = [0]

        def next_bank():
            bank[0] ^= 1
            return bank[0]

        class G:
            pass

        gs = [G() for _ in range(NG)]
        for g, s in enumerate(gs):
            s.x = X[:, g % NX, :, :]
            s.b = g // 4
        xns, xts = Slots(4), Slots(NXT)
        sm_slot = [0]

        def col(name, m):
            c = COLS[name] + m
            return cols[:, c:c + 1]


        def rows(r):
            return bc[:, r, :].unsqueeze(1).to_broadcast([128, 2, 256])

        def norm(src, t_src, scale1=1.0, add=EPS):
            k, tf = xns.take()
            m = sm_slot[0] % 10
            sm_slot[0] += 1
            dst = XN[:, k, :, :]
            for i in range(2):
                st = SM[:, m, i, 0:6]
                mv = SM[:, m, i, 6:8]
                t = dve.do(lambda e, i=i, st=st: e.bn_stats(st, src[:, i, :]), t_src)
                t = dve.do(lambda e, st=st, mv=mv: e.bn_aggr(mv, st), t)
            t = dve.do(lambda e: e.tensor_scalar(SM[:, m, :, 8], SM[:, m, :, 7], scale1, add, ALU.mult, ALU.add), t)
            t = pool.do(lambda e: e.tensor_tensor(SM[:, m, :, 9], SM[:, m, :, 8], nhalf[:, :], ALU.pow), t, t_nh)
            for i in range(2):
                t2 = dve.do(lambda e, i=i: e.tensor_scalar(dst[:, i, :], src[:, i, :], SM[:, m, i, 6:7],
                                                           SM[:, m, i, 9:10], ALU.subtract, ALU.mult),
                            t, tf)
            return dst, t2, k

        def turn(xn, t_xn):
            k, tf = xts.take()
            for i in range(2):
                for c in range(2):
                    fn = (lambda e, i=i, c=c: e.transpose(PT[:, c, i * 128:(i + 1) * 128],
                                                          xn[:, i, c * 128:(c + 1) * 128], ident[:, :]))
                    if i + c < 2:
                        pe.go(fn, t_xn, t_id, free["PT"])
                    else:
                        t = pe.do(fn)
            H, L = XTH[:, k, :, :], XTL[:, k, :, :]
            th = act.do(lambda e: e.activation(H, PT[:, :, :], ACT.Copy), t, tf)
            tl = dve.do(lambda e: e.tensor_tensor(L, PT[:, :, :], f(H), ALU.subtract), t, th)
            free["PT"] = tl
            return H, L, tl, k, t

        def three(dst, pairs, waits=()):
            n = len(pairs) * 3
            j = 0
            pe.wait(*waits)
            for (sh, sl), (mh, ml) in pairs:
                for a, b in ((sh, mh), (sh, ml), (sl, mh)):
                    fn = lambda e, a=a, b=b, j=j: e.matmul(dst, a, b, start=(j == 0), stop=(j == n - 1))
                    j += 1
                    if j < n:
                        pe.go(fn)
                    else:
                        t = pe.do(fn)
            return t

        def full(dst, pairs, waits=()):
            pe.wait(*waits)
            for j, (a, b) in enumerate(pairs):
                fn = lambda e, a=a, b=b, j=j: e.matmul(dst, a, b, start=(j == 0), stop=(j == len(pairs) - 1))
                if j < len(pairs) - 1:
                    pe.go(fn)
                else:
                    t = pe.do(fn)
            return t


        def keys0(b):
            n = next_bank()
            for m in range(2):
                t = full(PB[n][:, m * NK:(m + 1) * NK],
                         [(WKV[:, c, m * 128:(m + 1) * 128], ctxT[:, c, b * NK:(b + 1) * NK]) for c in range(2)],
                         (t_ctxT, t_wkv, free[n]))
            for m in range(2):
                t = dve.do(lambda e, m=m: e.tensor_scalar(KF[:, m, :], PB[n][:, m * NK:(m + 1) * NK], col("b_k", m),
                                                          0.25, ALU.add, ALU.mult), t, t_cols)
            free[n] = t
            KHr = KBH[:, 0:2, :]
            th = dve.do(lambda e: e.tensor_copy(KHr, KF[:, :, :]), t, free["KB"])
            t1 = dve.do(lambda e: e.tensor_tensor(KTL[:, :, :], KF[:, :, :], f(KHr), ALU.subtract), th)
            t2 = dve.do(lambda e: e.tensor_copy(KTH[:, :, :], f(KHr)), t1)
            for m in range(2):
                for B, T in ((KBH, KTH), (KBL, KTL)):
                    t = dve.do(lambda e, m=m, B=B, T=T: e.tensor_tensor(
                        B[:, 8 * m:8 * m + 8, :], T[:, m, :].unsqueeze(1).to_broadcast([128, 8, NK]),
                        mask8[:, :].unsqueeze(2).to_broadcast([128, 8, NK]), ALU.mult), t2, t_m8)
            return t

        def values0(b):
            tv = free["VB"]
            free["CR0"] = free["CR1"] = free["RT"]
            kx, tx = xts.take()
            for c in range(5):
                M = CM[c]
                k = c % 2
                r = CW * c
                end = r + M
                while r < end:
                    key = r % NK
                    n = min(end - r, NK - key)
                    o = r - CW * c
                    t = act.do(lambda e, o=o, n=n, key=key, k=k: e.activation(
                        CR[:, k, :, o:o + n], ctxT[:, :, b * NK + key:b * NK + key + n], ACT.Copy),
                        t_ctxT, free[f"CR{k}"])
                    r += n
                p = next_bank()
                t = full(PB[p][0:M, 0:256], [(CR[:, k, j, 0:M], WKV[:, j, 256:512]) for j in range(2)],
                         (t, t_wvv, free[p]))
                free[f"CR{k}"] = t
                VF = HF[0:M, k, 0, :]
                VH = XTH[0:M, kx, k, :]
                VL = HF[0:M, k, 1, :]
                t = dve.do(lambda e, p=p, M=M, VF=VF: e.tensor_tensor(VF, PB[p][0:M, 0:256], bc[0:M, BV, :], ALU.add),
                           t, t_bc, free[f"HF{k}"])
                free[p] = t
                th = dve.do(lambda e, VF=VF, VH=VH: e.tensor_copy(VH, VF), t, tx)
                tl = dve.do(lambda e, VF=VF, VH=VH, VL=VL: e.tensor_tensor(VL, VF, f(VH), ALU.subtract), th)
                for B, T in ((VBH, f(VH)), (VBL, VL)):
                    t = dve.do(lambda e, c=c, M=M, B=B, T=T: e.tensor_tensor(
                        B[0:M, c, :, :].rearrange("p a (h d) -> p a h d", h=8),
                        T.rearrange("p (a h d) -> p a h d", a=2, h=8),
                        mask5[0:M, c, :].unsqueeze(1).unsqueeze(3).to_broadcast([M, 2, 8, 16]), ALU.mult),
                        tl, t_m5, tv)
                free[f"HF{k}"] = t
            xts.give(kx, t)
            free["RT"] = [free["CR0"], free["CR1"]]
            return t


        def load_x(g):
            if g > 0:
                sp.wait(xfree.get(("x", g % NX)))
                t_x[g] = load(X[:, g % NX, :, :], x_v[g])
                xfree["x", g % NX] = BUSY

        def a1(g):
            s = gs[g]
            t_x2 = t_x[g]
            xn, t, k = norm(s.x, t_x2)
            s.t_xr = pool.do(lambda e: e.tensor_tensor(s.x, s.x, rows(BO), ALU.add), t, t_bc)
            s.H, s.L, s.t, s.k, tp = turn(xn, t)
            xns.give(k, tp)

        def a2(g):
            s = gs[g]
            for m in range(2):
                ms = slice(m * 128, (m + 1) * 128)
                t = three(PA[:, m, :], [((WqH[:, c, ms], WqL[:, c, ms]), (s.H[:, c, :], s.L[:, c, :]))
                                        for c in range(2)], (s.t, t_w["q"], free["PA"]))
            xts.give(s.k, t)
            s.kq, tf = xts.take()
            QH, QL = XTH[:, s.kq, :, :], XTL[:, s.kq, :, :]
            s.q = QH, QL
            for m in range(2):
                th = act.do(lambda e, m=m: e.activation(QH[:, m, :], PA[:, m, :], ACT.Identity, bias=col("b_q", m)),
                            t, t_cols, tf)
            for m in range(2):
                tl = dve.do(lambda e, m=m: e.scalar_tensor_tensor(out=QL[:, m, :], in0=PA[:, m, :],
                                                                  scalar=col("b_q", m), in1=f(QH[:, m, :]),
                                                                  op0=ALU.add, op1=ALU.subtract), th)
            free["PA"] = tl
            s.t_q = tl

        def heads4(T):
            return T.rearrange("p (a h) k -> p a h k", a=4)

        def score(g, i):
            s = gs[g]
            ts = slice(i * 128, (i + 1) * 128)
            QH, QL = s.q
            for a in range(4):
                m = a // 2
                kh = KBH[:, 4 * a:4 * a + 4, :].rearrange("p h k -> p (h k)")
                kl = KBL[:, 4 * a:4 * a + 4, :].rearrange("p h k -> p (h k)")
                t = three(S4[:, a, 0:4 * NK], [((QH[:, m, ts], QL[:, m, ts]), (kh, kl))],
                          (s.t_q, t_w["kb", s.b], free["S4"]))
            if i == 1:
                xts.give(s.kq, t)
                if g % 4 == 3:
                    free["KB"] = t
            sx = SX[:, i, :, :]
            sv = S4[:, :, 0:4 * NK].rearrange("p a (h k) -> p a h k", k=NK)
            t = dve.do(lambda e: e.tensor_reduce(sx[:, 0, :].rearrange("p (a h) -> p a h", a=4), sv, AX, ALU.max), t)
            Ei = E[:, i, :, :]
            t = dve.do(lambda e: e.tensor_tensor(heads4(Ei), sv, sx[:, 0, :].rearrange("p (a h) -> p a h", a=4)
                                                 .unsqueeze(3).to_broadcast([128, 4, 4, NK]), ALU.subtract),
                       t, free[f"E{i}"])
            free[f"E{i}"] = BUSY
            free["S4"] = t
            t = act.do(lambda e: e.activation(Ei, Ei, ACT.Exp), t)
            s.t_e = t

        def weigh(g, i):
            s = gs[g]
            Ei = E[:, i, :, :]
            sx = SX[:, i, :, :]
            t = dve.do(lambda e: e.tensor_reduce(sx[:, 1, :], Ei, AX, ALU.add), s.t_e)
            t = dve.do(lambda e: e.reciprocal(sx[:, 2, :], sx[:, 1, :]), t)
            t_r = act.do(lambda e: e.activation(RR[:, :, :], sx[:, 2, :].unsqueeze(2).to_broadcast([128, 16, 16]),
                                                ACT.Copy), t, free["RR"])
            ef = Ei.rearrange("p h k -> p (h k)")
            pe.wait(s.t_e, free["S4"])
            for c in range(5):
                for a in range(2):
                    M = CM[c]
                    o = a * 616 + CW * c
                    dst = S4[0:M, a, c * 128:(c + 1) * 128] if c < 4 else S4[0:M, 2, a * 128:(a + 1) * 128]
                    t = pe.do(lambda e, dst=dst, o=o, M=M: e.transpose(dst, ef[:, o:o + M], ident[:, :]))
            te = t
            rf = RR[:, :, :].rearrange("p a b -> p (a b)")
            for a in range(2):
                t = pe.do(lambda e, a=a: e.transpose(S4[:, 3, a * 128:(a + 1) * 128], rf[:, a * 128:(a + 1) * 128],
                                                     ident[:, :]), t_r)
            free["RR"] = t
            free[f"E{i}"] = t
            ts = slice(i * 128, (i + 1) * 128)
            srcs = [(S4[0:CW, 0:2, :].rearrange("p a (c t) -> p a c t", c=4), 4, CW, slice(0, 4)),
                    (S4[0:120, 2, 0:256].rearrange("p (a t) -> p a t", a=2), 1, 120, 4)]
            for src, nc_, M, cs in srcs:
                th = act.do(lambda e, src=src, M=M, cs=cs: e.activation(ETH[0:M, :, cs, ts], src, ACT.Copy),
                            te, free["ET"])
            tr = act.do(lambda e: e.activation(RT[:, :, ts], S4[:, 3, 0:256].rearrange("p (a t) -> p a t", a=2),
                                               ACT.Copy), t, free["RT"])
            for src, nc_, M, cs in srcs:
                tl = dve.do(lambda e, src=src, M=M, cs=cs: e.tensor_tensor(ETL[0:M, :, cs, ts], src,
                                                                           f(ETH[0:M, :, cs, ts]), ALU.subtract),
                            th, free["ET"])
            free["S4"] = [tl, tr]
            s.t_et, s.t_rt = tl, tr
            if i == 1:
                free["ET"] = free["RT"] = BUSY

        def pv(g):
            s = gs[g]
            for a in range(2):
                pairs = [((VBH[0:CM[c], c, a, :], VBL[0:CM[c], c, a, :]),
                          (ETH[0:CM[c], a, c, :], ETL[0:CM[c], a, c, :])) for c in range(5)]
                t = three(PA[:, a, :], pairs, (s.t_et, t_w["vb", s.b], free["PA"]))
            free["ET"] = t
            if g % 4 == 3:
                free["VB"] = t
            t = dve.do(lambda e: e.tensor_tensor(RT[:, :, :], PA[:, :, :], RT[:, :, :], ALU.mult), t, s.t_rt)
            free["PA"] = t
            s.ko, tf = xts.take()
            OH, OL = XTH[:, s.ko, :, :], XTL[:, s.ko, :, :]
            s.o = OH, OL
            th = act.do(lambda e: e.activation(OH, RT[:, :, :], ACT.Copy), t, tf)
            tl = dve.do(lambda e: e.tensor_tensor(OL, RT[:, :, :], f(OH), ALU.subtract), th)
            free["RT"] = tl
            s.t_o = tl

        def wo(g):
            s = gs[g]
            OH, OL = s.o
            for i in range(2):
                ts = slice(i * 128, (i + 1) * 128)
                t = three(PA[:, i, :], [((OH[:, a, ts], OL[:, a, ts]), (WoH[:, a, :], WoL[:, a, :]))
                                        for a in range(2)], (s.t_o, t_w["o"], free["PA"]))
            xts.give(s.ko, t)
            t = dve.do(lambda e: e.tensor_tensor(s.x, PA[:, :, :], s.x, ALU.add), t, s.t_xr)
            free["PA"] = t
            s.t_x = t

        def b1(g):
            s = gs[g]
            xn, t, k = norm(s.x, s.t_x)
            s.t_x1b = pool.do(lambda e: e.tensor_tensor(s.x, s.x, rows(BETA), ALU.add), t)
            s.H, s.L, s.t, s.k, tp = turn(xn, t)
            s.t_xrb = pool.do(lambda e: e.tensor_tensor(xn, xn, rows(B2), ALU.add), tp)
            s.y, s.ky = xn, k

        def w1(g, j):
            s = gs[g]
            n = next_bank()
            for q in range(2):
                fs = slice((2 * j + q) * 128, (2 * j + q + 1) * 128)
                t = three(PB[n][:, q * 256:(q + 1) * 256],
                          [((W1H[:, c, fs], W1L[:, c, fs]), (s.H[:, c, :], s.L[:, c, :])) for c in range(2)],
                          (s.t, t_w["w1"], free[n]))
            if j == 3:
                xts.give(s.k, t)
            k = j % 2
            for q in range(2):
                t2 = act.do(lambda e, q=q: e.activation(HF[:, k, q, :], PB[n][:, q * 256:(q + 1) * 256], ACT.Relu,
                                                        bias=col("b1", 2 * j + q)), t, free[f"HF{k}"])
            free[n] = t2
            hs = slice(2 * j, 2 * j + 2)
            th = dve.do(lambda e: e.tensor_copy(HH[:, hs, :], HF[:, k, :, :]), t2, free["HH"])
            tl = pool.do(lambda e: e.tensor_tensor(HL[:, hs, :], HF[:, k, :, :], f(HH[:, hs, :]), ALU.subtract), th,
                         free["HH"])
            free[f"HF{k}"] = tl
            s.t_h = tl
            if j == 3:
                free["HH"] = BUSY

        def w2(g):
            s = gs[g]
            n = next_bank()
            for i in range(2):
                ts = slice(i * 128, (i + 1) * 128)
                t = three(PB[n][:, i * 256:(i + 1) * 256],
                          [((HH[:, j, ts], HL[:, j, ts]), (W2H[:, j, :], W2L[:, j, :])) for j in range(8)],
                          (s.t_h, t_w["w2"], free[n]))
            free["HH"] = t
            t = dve.do(lambda e: e.tensor_tensor(s.y, PB[n][:, :].rearrange("p (i n) -> p i n", i=2), s.y,
                                                 ALU.add), t, s.t_xrb)
            free[n] = t
            s.t_y = t

        def b3(g):
            s = gs[g]
            yn, t, k = norm(s.y, s.t_y)
            xns.give(s.ky, t)
            t = pool.do(lambda e: e.tensor_tensor(yn, yn, rows(GAMMA), ALU.mult), t)
            t = pool.do(lambda e: e.tensor_tensor(s.x, yn, s.x, ALU.add), t, s.t_x1b)
            xns.give(k, t)
            s.t_x = t

        def c1(g):
            s = gs[g]
            xn, t, k = norm(s.x, s.t_x, 1.0 + EPS, EPS * EPS)
            s.t_xr = pool.do(lambda e: e.tensor_tensor(s.x, s.x, rows(BO1), ALU.add), t)
            s.H, s.L, s.t, s.k, tp = turn(xn, t)
            xns.give(k, tp)

        def c2(g):
            s = gs[g]
            b = s.b
            n = next_bank()
            t = three(PB[n][0:NK, 0:256], [((M1H[:, c, b, :], M1L[:, c, b, :]), (s.H[:, c, :], s.L[:, c, :]))
                                           for c in range(2)], (s.t, t_w["m1"], free[n]))
            xts.give(s.k, t)
            t = act.do(lambda e: e.activation(ST[:, :], PB[n][0:NK, 0:256], ACT.Identity, bias=cT[:, b:b + 1]), t,
                       t_w["m1"], free["ST"])
            for i in range(2):
                t = pe.do(lambda e, i=i: e.transpose(PB[n][:, i * NK:(i + 1) * NK], ST[:, i * 128:(i + 1) * 128],
                                                     ident[0:NK, 0:NK]), t)
            free["ST"] = t
            sv = PB[n][:, 0:2 * NK].rearrange("p (i k) -> p i k", i=2)
            t = dve.do(lambda e: e.tensor_reduce(PS[:, 0, :], sv, AX, ALU.max), t)
            t = dve.do(lambda e: e.tensor_tensor(PP[:, :, :], sv, PS[:, 0, :].unsqueeze(2)
                                                 .to_broadcast([128, 2, NK]), ALU.subtract), t, free["PP"])
            free[n] = t
            t = act.do(lambda e: e.activation(PP[:, :, :], PP[:, :, :], ACT.Exp), t)
            t = dve.do(lambda e: e.tensor_reduce(PS[:, 1, :], PP[:, :, :], AX, ALU.add), t)
            t = dve.do(lambda e: e.reciprocal(PS[:, 2, :], PS[:, 1, :]), t)
            s.t_p = dve.do(lambda e: e.tensor_tensor(PP[:, :, :], PP[:, :, :], PS[:, 2, :].unsqueeze(2)
                                                     .to_broadcast([128, 2, NK]), ALU.mult), t)
            free["PP"] = BUSY

        def c3(g):
            s = gs[g]
            b = s.b
            n = next_bank()
            for i in range(2):
                t = pe.do(lambda e, i=i: e.transpose(PB[n][0:NK, i * 128:(i + 1) * 128], PP[:, i, :], ident[:, :]),
                          s.t_p, free[n])
            free["PP"] = t
            t = act.do(lambda e: e.activation(PTT[0:NK, :], PB[n][0:NK, 0:256], ACT.Copy), t, t_w["pz"],
                       free["PTT"])
            free[n] = t
            n = next_bank()
            for i in range(2):
                t = full(PB[n][:, i * 256:(i + 1) * 256], [(PTT[:, i * 128:(i + 1) * 128], M2[:, b, :])],
                         (t, t_w["m2"], free[n]))
            free["PTT"] = t
            t = dve.do(lambda e: e.tensor_tensor(s.x, PB[n][:, :].rearrange("p (i n) -> p i n", i=2), s.x, ALU.add),
                       t, s.t_xr)
            free[n] = t
            s.t_x = t

        def d1(g):
            s = gs[g]
            xn, t, k = norm(s.x, s.t_x)
            s.H, s.L, s.t, s.k, tp = turn(xn, t)
            xns.give(k, tp)
            pb = (g % 4) * 2
            n = next_bank()
            for i in range(2):
                t = pe.do(lambda e, i=i, n=n: e.transpose(PB[n][0:8, i * 128:(i + 1) * 128], OHM[:, pb + i, :],
                                                          ident[:, :]), t_w["oh"], t_id, free[n])
            th = act.do(lambda e, n=n: e.activation(OHT[:, :], PB[n][0:8, 0:256], ACT.Copy), t, free["OHT"])
            free[n] = th
            n = next_bank()
            for i in range(2):
                t = full(PB[n][:, i * 256:(i + 1) * 256],
                         [(OHT[:, i * 128:(i + 1) * 128], BD[:, :])], (th, t_w["bd"], free[n]))
            free["OHT"] = t
            t = dve.do(lambda e: e.tensor_tensor(s.x, PB[n][:, :].rearrange("p (i n) -> p i n", i=2), s.x, ALU.add), t)
            free[n] = t

        def d2(g, i):
            s = gs[g]
            ts = slice(i * 128, (i + 1) * 128)
            pb = (g % 4) * 2 + i
            for q in range(4):
                n = next_bank()
                es = slice(q * 512, (q + 1) * 512)
                t = three(PB[n][:, :], [((s.H[:, c, ts], s.L[:, c, ts]), (WDH[:, c, es], WDL[:, c, es]))
                                        for c in range(2)], (s.t, t_w["wd"], free[n]))
                for r in range(2):
                    td = dve.do(lambda e, q=q, r=r, n=n: e.scalar_tensor_tensor(
                        out=s.x[:, i, :], in0=PB[n][:, r * 256:(r + 1) * 256],
                        scalar=OHM[:, pb, 2 * q + r:2 * q + r + 1], in1=s.x[:, i, :], op0=ALU.mult, op1=ALU.add),
                        t, (dve.sem, dve.count))
                free[n] = td
            if i == 1:
                xts.give(s.k, t)
            o_v = out.rearrange("(k p) n -> k p n", p=128)
            sp.wait(td)
            stores.append(load(o_v[2 * g + i], s.x[:, i, :]))
            if i == 1:
                xfree["x", g % NX] = stores[-2:]
            else:
                xfree["x", g % NX] = BUSY

        stores = []

        ctx_v = A["ctx"].rearrange("b k n -> k b n")

        def fold():
            CK = HF[0:NK, 0, :, 0:192]
            CN = HF[0:NK, 1, :, 0:192]
            sp.wait(free["HF0"])
            t_ck = load(CK, ctx_v)
            kg, tf = ring.take()
            sp.wait(tf)
            GB = RAW[0:NK, kg, 0:384].rearrange("p (r n) -> p r n", r=2)
            t_gb = load(GB, A["rows2"].rearrange("(a r) n -> a r n", a=1).to_broadcast([NK, 2, 192]))
            for i in range(2):
                t = dve.do(lambda e, i=i: e.bn_stats(SM[0:NK, 9, i, 0:6], CK[:, i, :]), t_ck, free["HF1"])
                t = dve.do(lambda e, i=i: e.bn_aggr(SM[0:NK, 9, i, 6:8], SM[0:NK, 9, i, 0:6]), t)
            t = dve.do(lambda e: e.tensor_scalar(SM[0:NK, 9, :, 8], SM[0:NK, 9, :, 7], EPS, None, ALU.add), t)
            t = pool.do(lambda e: e.tensor_tensor(SM[0:NK, 9, :, 9], SM[0:NK, 9, :, 8], nhalf[0:NK, :], ALU.pow), t,
                        t_nh)
            for i in range(2):
                t1 = dve.do(lambda e, i=i: e.tensor_scalar(CN[:, i, :], CK[:, i, :], SM[0:NK, 9, i, 6:7],
                                                           SM[0:NK, 9, i, 9:10], ALU.subtract, ALU.mult), t)
            t = dve.do(lambda e: e.tensor_tensor(CN, CN, GB[:, 0, :].unsqueeze(1).to_broadcast([NK, 2, 192]),
                                                 ALU.mult), t1, t_gb)
            t = dve.do(lambda e: e.tensor_tensor(CN, CN, GB[:, 1, :].unsqueeze(1).to_broadcast([NK, 2, 192]),
                                                 ALU.add), t)
            ring.give(kg, t)
            n = next_bank()
            for c in range(2):
                for i in range(2):
                    o = (c * 2 + i) * NK
                    tt = pe.do(lambda e, c=c, i=i, o=o: e.transpose(PB[n][0:96, o:o + NK],
                                                                    CN[:, i, c * 96:(c + 1) * 96],
                                                                    ident[0:NK, 0:NK]), t, t_id, free[n])
            CT = E[0:96, 0, 12:16, :].rearrange("p h k -> p (h k)").rearrange("p (c k) -> p c k", c=2)
            t_ct = act.do(lambda e: e.activation(CT, PB[n][0:96, 0:4 * NK].rearrange("p (c k) -> p c k", c=2),
                                                 ACT.Copy), tt, free["E0"])
            free[n] = t_ct
            free["HF0"] = free["HF1"] = t_ct
            k, wk1, t_wk1 = stage(A["Wk"].rearrange("(c p) n -> p c n", p=96), 96, 512)
            k2, wv1, t_wv1 = stage(A["Wv"].rearrange("(c p) n -> p c n", p=96), 96, 512)
            K1S = E[:, 0, 0:4, :].rearrange("p h k -> p (h k)").rearrange("p (m k) -> p m k", m=2)
            V1S = E[:, 0, 4:8, :].rearrange("p h k -> p (h k)").rearrange("p (m k) -> p m k", m=2)
            for kk, w, tw, dst, bias in ((k, wk1, t_wk1, K1S, "bk1"), (k2, wv1, t_wv1, V1S, "bv1")):
                wv = w.rearrange("p (c n) -> p c n", c=2)
                n = next_bank()
                for m in range(2):
                    tp = full(PB[n][:, m * 154:(m + 1) * 154],
                              [(wv[:, c, m * 128:(m + 1) * 128], CT[:, c, :]) for c in range(2)],
                              (t_ct, tw, free[n]))
                ring.give(kk, tp)
                for m in range(2):
                    td = dve.do(lambda e, m=m, n=n, dst=dst, bias=bias: e.tensor_scalar(
                        dst[:, m, :], PB[n][:, m * 154:(m + 1) * 154], col(bias, m), None, ALU.add), tp, t_cols,
                        free["E0"])
                free[n] = td
                if bias == "bk1":
                    t_k1 = td
                else:
                    t_v1 = td
            k, wqT, t_wqT = stage(A["WqT"].rearrange("(c p) n -> p c n", p=128), 128, 512)
            k2, wqn, t_wqn = stage(A["Wq"].rearrange("(c p) n -> p c n", p=128), 128, 512)
            wqT, wqn = (w.rearrange("p (c n) -> p c n", c=2) for w in (wqT, wqn))
            n = next_bank()
            for m in range(2):
                t = full(PB[n][:, m * 154:(m + 1) * 154],
                         [(wqT[:, c, m * 128:(m + 1) * 128], K1S[:, c, :]) for c in range(2)],
                         (t_k1, t_wqT, free[n]))
            ring.give(k, t)
            M1S = E[:, 0, 8:12, :].rearrange("p h k -> p (h k)").rearrange("p (m b k) -> p m b k", m=2, b=2)
            for m in range(2):
                t1 = dve.do(lambda e, m=m, n=n: e.tensor_scalar(
                    M1S[:, m, :, :], PB[n][:, m * 154:(m + 1) * 154].rearrange("p (b k) -> p b k", b=2),
                    col("g1", m), 0.0625, ALU.mult, ALU.mult), t)
            free[n] = t1
            th = dve.do(lambda e: e.tensor_copy(M1H[:, :, :, :], M1S), t1)
            tl = dve.do(lambda e: e.tensor_tensor(M1L[:, :, :, :], M1S, f(M1H[:, :, :, :]), ALU.subtract), th)
            n = next_bank()
            for m in range(2):
                t = full(PB[n][:, m:m + 1], [(wqn[:, c, m * 128:(m + 1) * 128], col("be1", c)) for c in range(2)],
                         (t_wqn, t_cols, free[n]))
            ring.give(k2, t)
            tq = dve.do(lambda e, n=n: e.tensor_tensor(PS[:, 3, :], PB[n][:, 0:2], cols[:, COLS["bq1"]:COLS["bq1"] + 2],
                                                       ALU.add), t)
            free[n] = tq
            n = next_bank()
            for b in range(2):
                t = full(PB[n][0:NK, b:b + 1], [(K1S[:, c, b * NK:(b + 1) * NK], PS[:, 3, c:c + 1])
                                                for c in range(2)], (tq, free[n]))
            tc = dve.do(lambda e, n=n: e.tensor_scalar(cT[:, :], PB[n][0:NK, 0:2], 0.0625, None, ALU.mult), t)
            free[n] = tc
            t_w["m1"] = tc
            tz = dve.do(lambda e: e.memset(M2[64:96, :, :], 0.0))
            t_w["pz"] = dve.do(lambda e: e.memset(PTT[64:96, :], 0.0))
            k3, wo1, t_wo1 = stage(A["Wo"].rearrange("(c p) n -> p c n", p=128), 128, 512)
            wo1 = wo1.rearrange("p (c n) -> p c n", c=2)
            n = next_bank()
            for b in range(2):
                t = full(PB[n][0:NK, b * 256:(b + 1) * 256],
                         [(V1S[:, c, b * NK:(b + 1) * NK], wo1[:, c, :]) for c in range(2)],
                         (t_v1, t_wo1, free[n]))
            ring.give(k3, t)
            free["E0"] = t
            t = dve.do(lambda e, n=n: e.tensor_copy(M2[0:NK, :, :], PB[n][0:NK, :].rearrange("p (b n) -> p b n", b=2)),
                       t, tz)
            free[n] = t
            t_w["m2"] = t

        BD = sb("BD", [8, 256])

        def route():
            sg = sb("sg", [32, 3, 8])
            kp, tf = ring.take()
            sp.wait(tf)
            peT = RAW[0:32, kp, :]
            t_sg = load(sg[:, 0, :], A["sigT"])
            t_pe = load(peT, A["peT"])
            tb = load(BD[:, :], A["bD"])
            t = dve.do(lambda e: e.tensor_scalar(sg[:, 1, :], sg[:, 0, :], 0.0, None, ALU.is_gt), t_sg)
            t = dve.do(lambda e: e.tensor_scalar(sg[:, 2, :], sg[:, 0, :], 0.0, None, ALU.is_lt), t)
            t = dve.do(lambda e: e.tensor_tensor(sg[:, 1, :], sg[:, 1, :], sg[:, 2, :], ALU.subtract), t)
            n = next_bank()
            for j in range(8):
                tp = pe.do(lambda e, j=j: e.matmul(PB[n][:, j * 8:(j + 1) * 8], peT[:, j * 128:(j + 1) * 128],
                                                   sg[:, 1, :], start=True, stop=True), t, t_pe, free[n])
            ring.give(kp, tp)
            sc = PB[n][:, 0:64].rearrange("p (j t) -> p j t", t=8)
            rk = sb("rk", [128, 8])
            mx = sb("mx", [128, 2, 8])
            eq = sb("eq", [128, 8, 8])
            rep = lambda a: a.unsqueeze(2).to_broadcast([128, 8, 8])
            rev = rk[:, :].unsqueeze(1).to_broadcast([128, 8, 8])
            ti = pool.do(lambda e: e.iota(rk[:, :], [[-1, 8]], base=8, channel_multiplier=0,
                                          allow_small_or_imprecise_dtypes=True))
            t = dve.do(lambda e: e.tensor_reduce(mx[:, 0, :], sc, AX, ALU.max), tp)
            t = dve.do(lambda e: e.tensor_tensor(eq[:, :, :], sc, rep(mx[:, 0, :]), ALU.is_equal), t)
            free[n] = t
            t = dve.do(lambda e: e.tensor_tensor(eq[:, :, :], eq[:, :, :], rev, ALU.mult), t, ti)
            t = dve.do(lambda e: e.tensor_reduce(mx[:, 1, :], eq[:, :, :], AX, ALU.max), t)
            t = dve.do(lambda e: e.tensor_tensor(OHM[:, :, :], rep(mx[:, 1, :]), rev, ALU.is_equal), t)
            t_w["oh"] = t
            t_w["bd"] = tb

        k, raw, t = stage(A["w_q"].rearrange("(c p) n -> p c n", p=128), 128, 512)
        t_w["q"] = split(flat2(WqH[:, :, :]), flat2(WqL[:, :, :]), k, raw, t)
        t_w["kb", 0] = keys0(0)
        t_w["vb", 0] = values0(0)

        def w_o():
            k, raw, t = stage(A["w_o"].rearrange("(c p) n -> p c n", p=128), 128, 512)
            t_w["o"] = split(flat2(WoH[:, :, :]), flat2(WoL[:, :, :]), k, raw, t)

        def w_1(c):
            k, raw, t = stage(A["w1"][c * 128:(c + 1) * 128, :], 128, 1024)
            t_w["w1"] = split(W1H[:, c, :], W1L[:, c, :], k, raw, t)

        def w_2(c):
            k, raw, t = stage(A["w2"][c * 512:(c + 1) * 512, :].rearrange("(j p) n -> p j n", p=128), 128, 1024)
            t_w["w2"] = split(flat2(W2H[:, 4 * c:4 * c + 4, :]), flat2(W2L[:, 4 * c:4 * c + 4, :]), k, raw, t)

        def w_d(c, h):
            k, raw, t = stage(A["WD"][c * 128:(c + 1) * 128, h * 1024:(h + 1) * 1024], 128, 1024)
            t_w["wd"] = split(WDH[:, c, h * 1024:(h + 1) * 1024], WDL[:, c, h * 1024:(h + 1) * 1024], k, raw, t)

        steps = []

        def step(when, fn, *args):
            steps.append((when, len(steps), fn, args))

        step(1, w_o)
        step(2, w_1, 0)
        step(3, w_1, 1)
        step(6, w_2, 0)
        step(9, w_2, 1)
        step(14.5, fold)
        step(22, route)
        step(23, w_d, 0, 0)
        step(24, w_d, 0, 1)
        step(25, w_d, 1, 0)
        step(26, w_d, 1, 1)

        def batch1():
            t_w["kb", 1] = keys0(1)
            t_w["vb", 1] = values0(1)

        for g in range(NG):
            o = g * period
            if g == 4:
                step(max(o + at["a2"] + 0.5, 3 * period + at["pv"] + 0.1), batch1)
                shift = max(0, 3 * period + at["pv"] + 0.2 - o - at["s0"])
            step(o - 6, load_x, g)
            step(o + at["a1"], a1, g)
            step(o + at["a2"], a2, g)
            step(o + at["s0"], score, g, 0)
            step(o + at["t0"], weigh, g, 0)
            step(o + at["s1"], score, g, 1)
            step(o + at["t1"], weigh, g, 1)
            step(o + at["pv"], pv, g)
            step(o + at["wo"], wo, g)
            step(o + at["b1"], b1, g)
            for j in range(4):
                step(o + at["w1"] + 1.3 * j, w1, g, j)
            step(o + at["w2"], w2, g)
            step(o + at["b3"], b3, g)
            step(o + at["c1"], c1, g)
            step(o + at["c2"], c2, g)
            step(o + at["c3"], c3, g)
            step(o + at["d1"], d1, g)
            step(o + at["d2"], d2, g, 0)
            step(o + at["d2"] + 5, d2, g, 1)
        for when, _, fn, args in sorted(steps, key=lambda s: s[:2]):
            fn(*args)
        sp.wait(*stores)

        block = ctx.enter_context(nc.Block())
        block.sync(sp.run)
        block.tensor(pe.run)
        block.vector(dve.run)
        block.scalar(act.run)
        block.gpsimd(pool.run)


def table():
    pos = np.arange(1024, dtype=np.float32)[:, None]
    div = np.exp(np.arange(0, 32, 2, dtype=np.float32) * np.float32(-np.log(10000.0) / 32))
    ang = (pos * div.astype(np.float32)).astype(np.float32)
    pe = np.zeros((1024, 32), np.float32)
    pe[:, 0::2] = np.sin(ang)
    pe[:, 1::2] = np.cos(ang)
    return np.ascontiguousarray(pe.T)


def laid_out(i):
    p = "L0_xattn_"
    q = "L1_xattn_"
    a = {
        "x": i["x"].reshape(2048, 256),
        "ctx": i["ctx_768"],
        "ctxT": i["ctx_768"].transpose(2, 0, 1).reshape(192, 154),
        "w_q": i[p + "w_q"], "w_k": i[p + "w_k"], "w_v": i[p + "w_v"], "w_o": i[p + "w_o"],
        "w1": i["L0_ffn_w1"][0], "w2": i["L0_ffn_w2"][0],
        "Wk": i[q + "Wk"], "Wv": i[q + "Wv"], "Wq": i[q + "Wq"], "WqT": i[q + "Wq"].T, "Wo": i[q + "Wo"],
        "WD": i["L1_ffn_W"].transpose(2, 0, 1).reshape(256, 2048),
        "bD": i["L1_ffn_b"],
        "sigT": i["L1_ffn_tile_sigs"].T,
        "peT": table(),
        "cols": np.concatenate([i[p + "b_q"], i[p + "b_k"], i[q + "bk"], i[q + "bq"], i[q + "bv"],
                                i[q + "ln1_g"], i[q + "ln1_b"], i["L0_ffn_b1"][0]]).reshape(22, 128).T,
        "rows": np.stack([i[p + "b_o"], i["L0_ffn_b2"][0], i["L0_ffn_beta"], i["L0_ffn_gamma"],
                          i[q + "bo"], i[p + "b_v"]]),
        "rows2": np.stack([i[q + "ln2_g"], i[q + "ln2_b"]]),
    }
    return {k: np.ascontiguousarray(v) for k, v in a.items()}


def kernel(**inputs):
    import concourse.bacc as bacc
    from concourse.bass_utils import run_bass_kernel_spmd

    nc = bacc.Bacc("TRN2", target_bir_lowering=False, num_devices=1)
    arrays = laid_out({k: np.asarray(v) for k, v in inputs.items()})
    A = {k: nc.dram_tensor(f"in_{k}", a.shape, mybir.dt.from_np(a.dtype), kind="ExternalInput").ap()
         for k, a in arrays.items()}
    out = nc.dram_tensor("out_x", (2048, 256), F32, kind="ExternalOutput").ap()
    program(nc, A, out)
    r = run_bass_kernel_spmd(nc, [{f"in_{k}": a for k, a in arrays.items()}], core_ids=[0])
    return r.results[0]["out_x"].reshape(2, 1024, 256)
```

```python
from contextlib import ExitStack

import numpy as np
import concourse.bass as bass
from concourse import mybir

F32 = mybir.dt.float32
F32R = mybir.dt.float32r
I32 = mybir.dt.int32
ALU = mybir.AluOpType
ACT = mybir.ActivationFunctionType
AX = mybir.AxisListType.X

NX = 3
NXT = 4
NG = 8
NK = 77
EPS = 1e-5
CW = 124
CM = [124, 124, 124, 124, 120]
NB = 15
LAG = 0.1
BIAS_ON_POOL = (0, 4)
HAND = dict(ex=0.0)
CF = 0.00105
CA = 0.00085
CP = 0.0023


BUSY = "busy"


class Slots:

    def peek(self):
        return self.open[0][1] if self.open else BUSY

    def __init__(self, n):
        self.open = [(k, None) for k in range(n)]

    def take(self):
        assert self.open, "too few buffers"
        return self.open.pop(0)

    def give(self, k, token):
        self.open.append((k, token))


class Queue:

    def __init__(self, sem):
        self.sem, self.count, self.code, self.seen, self.now = sem, 0, [], {}, 0.0

    def wait(self, *tokens):
        for t in tokens:
            if t is None:
                continue
            if isinstance(t, list):
                self.wait(*t)
                continue
            assert t is not BUSY, "a buffer that is still in use"
            sem, value, when = t
            self.now = max(self.now, when + LATENCY)
            if sem is self.sem and self.pe:
                continue
            if self.seen.get(id(sem), 0) < value:
                self.seen[id(sem)] = value
                self.code.append(lambda e, s=sem, v=value: e.wait_ge(s, v))

    pe = False

    def go(self, fn, *tokens, c=0.11):
        self.wait(*tokens)
        self.now += c
        self.code.append(fn)

    def do(self, fn, *tokens, c=0.11):
        self.wait(*tokens)
        self.now += c
        self.count += 1
        self.code.append(lambda e: fn(e).then_inc(self.sem, 1))
        return (self.sem, self.count, self.now)

    def run(self, eng):
        for fn in self.code:
            fn(eng)


LATENCY = 0.1


def ready(tokens):
    if tokens is BUSY:
        return None
    if tokens is None:
        return 0.0
    if isinstance(tokens, list):
        w = [ready(t) for t in tokens]
        return None if None in w else max(w, default=0.0)
    return tokens[2] + LATENCY


def schedule(work):
    live = []

    def advance(item):
        try:
            item[2] = next(item[1])
            live.append(item)
        except StopIteration:
            pass

    for handicap, gen in work:
        advance([handicap, gen, None])
    while live:
        best = None
        for n, (handicap, _, (queue, needs)) in enumerate(live):
            when = ready(needs())
            if when is not None:
                key = max(when, queue.now) + handicap
                if best is None or key < best[0]:
                    best = (key, n)
        assert best is not None, "no piece of work can go on"
        advance(live.pop(best[1]))


def f(ap):
    return ap.bitcast(F32)


def program(nc, A, out, lag=LAG, hand={}):
    with ExitStack() as ctx:
        def sb(name, shape, dt=F32):
            return ctx.enter_context(nc.sbuf_tensor(name, shape, dt))

        def sem(name):
            return ctx.enter_context(nc.semaphore(name))

        hand = {**HAND, **hand}
        S4 = ctx.enter_context(nc.psum_tensor("S4", [128, 4, 512], F32))
        PB = [ctx.enter_context(nc.psum_tensor(f"PB{i}", [128, 512], F32)) for i in range(4)]

        pe, dve, act, pool = (Queue(sem(n)) for n in ("s_pe", "s_dve", "s_act", "s_pool"))
        sp = Queue(None)
        pe.pe = True

        def load(dst, src):
            s = sem(f"s_ld{len(sp.code)}")
            sp.go(lambda e: e.dma_start(dst, src).then_inc(s, 16))
            sp.now += 0.1
            return (s, 16, sp.now + 2.2)

        ident = sb("ident", [128, 128])
        mask8 = sb("mask8", [128, 8])
        mask5 = sb("mask5", [CW, 5, 8])
        nhalf = sb("nhalf", [128, 2])
        t0 = dve.do(lambda e: e.memset(ident[:, :], 0.0))
        t1 = dve.do(lambda e: e.memset(mask8[:, :], 1.0))
        t2 = dve.do(lambda e: e.memset(mask5[:, :, :], 1.0))
        t_nh = dve.do(lambda e: e.memset(nhalf[:, :], -0.5))
        t_id = pool.do(lambda e: e.affine_select(out=ident[:, :], in_=ident[:, :], compare_op=ALU.not_equal,
                                                 fill=1.0, base=0, pattern=[[-1, 128]], channel_multiplier=1), t0)
        t = pool.do(lambda e: e.affine_select(out=mask8[:, :], in_=mask8[:, :], compare_op=ALU.is_ge, fill=0.0,
                                              base=0, pattern=[[-16, 8]], channel_multiplier=1), t1)
        t_m8 = pool.do(lambda e: e.affine_select(out=mask8[:, :], in_=mask8[:, :], compare_op=ALU.is_ge, fill=0.0,
                                                 base=15, pattern=[[16, 8]], channel_multiplier=-1), t)
        t = pool.do(lambda e: e.affine_select(out=mask5[:, :, :], in_=mask5[:, :, :], compare_op=ALU.is_ge,
                                              fill=0.0, base=0, pattern=[[CW, 5], [-NK, 8]],
                                              channel_multiplier=1), t2)
        t_m5 = pool.do(lambda e: e.affine_select(out=mask5[:, :, :], in_=mask5[:, :, :], compare_op=ALU.is_ge,
                                                 fill=0.0, base=NK - 1, pattern=[[-CW, 5], [NK, 8]],
                                                 channel_multiplier=-1), t)

        X = sb("X", [128, NX, 2, 256])
        x_v = A["x"].rearrange("(g i p) n -> g p i n", i=2, p=128)
        slots = Slots(NX)
        x_k = {0: slots.take()[0]}
        t_x0 = load(X[:, x_k[0], :, :], x_v[0])
        ctxT = sb("ctxT", [96, 2, 2 * NK])
        t_ctxT = load(ctxT[:, :, :], A["ctxT"].rearrange("(c p) n -> p c n", p=96))
        RAW = sb("RAW", [128, 2, 1024])
        cols = sb("cols", [128, 24])
        COLS = dict(b_q=0, b_k=2, bk1=4, bq1=6, bv1=8, g1=10, be1=12, b1=14)
        t_cols = load(cols[:, 0:22], A["cols"])
        WKV = sb("WKV", [96, 2, 512])
        t_wkv = load(WKV[:, :, 0:256], A["w_k"].rearrange("(c p) n -> p c n", p=96))
        t_wvv = load(WKV[:, :, 256:512], A["w_v"].rearrange("(c p) n -> p c n", p=96))
        bc = sb("bc", [128, 6, 256])
        BO, B2, BETA, GAMMA, BO1, BV = range(6)
        t_bc = load(bc[:, :, :], A["rows"].rearrange("(a r) n -> a r n", a=1).to_broadcast([128, 6, 256]))

        ring = Slots(2)

        def flat2(T):
            return T.rearrange("p a b -> p (a b)")

        def two(ap):
            return ap.rearrange("p (a b) -> p a b", a=2)

        WqH, WqL, WoH, WoL = (sb(n, [128, 2, 256], F32R) for n in ("WqH", "WqL", "WoH", "WoL"))
        W1H, W1L = (sb(n, [128, 2, 1024], F32R) for n in ("W1H", "W1L"))
        W2H, W2L = (sb(n, [128, 8, 256], F32R) for n in ("W2H", "W2L"))
        WDH, WDL = (sb(n, [128, 2, 2048], F32R) for n in ("WDH", "WDL"))

        XN = sb("XN", [128, 4, 2, 256])
        XTH = sb("XTH", [128, NXT, 2, 256], F32R)
        XTL = sb("XTL", [128, NXT, 2, 256], F32R)
        E = sb("E", [128, 2, 16, NK])
        ETH = sb("ETH", [CW, 2, 5, 256], F32R)
        ETL = sb("ETL", [CW, 2, 5, 256], F32R)
        RR = sb("RR", [128, 16, 16])
        RT = sb("RT", [128, 2, 256])
        KF = sb("KF", [128, 2, NK])
        KTH = sb("KTH", [128, 2, NK])
        KTL = sb("KTL", [128, 2, NK])
        KBH = sb("KBH", [128, 16, NK], F32R)
        KBL = sb("KBL", [128, 16, NK], F32R)
        VBH = sb("VBH", [CW, 5, 2, 128], F32R)
        VBL = sb("VBL", [CW, 5, 2, 128], F32R)
        CR = RT[0:96, :, 0:2 * CW].rearrange("p a (b t) -> p a b t", b=2)
        HF = sb("HF", [128, 2, 2, 256])
        HH = sb("HH", [128, 8, 256], F32R)
        HL = sb("HL", [128, 8, 256], F32R)
        SM = sb("SM", [128, 12, 2, 11])
        SX = sb("SX", [128, 2, 3, 16])
        ST = sb("ST", [NK, 256])
        PP = sb("PP", [128, 2, NK])
        PS = sb("PS", [128, 4, 2])
        PTT = sb("PTT", [96, 256])
        M1H = sb("M1H", [128, 2, 2, NK], F32R)
        M1L = sb("M1L", [128, 2, 2, NK], F32R)
        M2 = sb("M2", [96, 2, 256])
        cT = sb("cT", [NK, 2])
        SI = sb("SI", [128, 2, 16], I32)
        GI = sb("GI", [128, 2, 16], I32)
        EV = sb("EV", [1, 2, 16], I32)
        quarter = RAW[:, :, :].rearrange("p a (b i n) -> p (a b) i n", b=2, i=2)
        XS = [X[:, k, :, :] for k in range(NX)] + [quarter[:, k, :, :] for k in range(2)]
        BB = quarter[:, 2:4, :, :]

        scratch = [nc.dram_tensor(f"x3_{b}", (1024, 256), F32, kind="Internal").ap() for b in range(2)]
        tab = nc.dram_tensor("slot_table", (2048, 1), I32, kind="Internal").ap()

        banks, s4, xns, xts, sms = Slots(4), Slots(1), Slots(4), Slots(NXT), Slots(12)
        es, ets, rrs, hhs, hfs, pps, sts, ptts, bbs = (Slots(n) for n in (2, 1, 1, 1, 2, 1, 1, 1, 1))

        class State(dict):
            def __missing__(self, k):
                return BUSY

        t_w = State()
        gs = [State(b=g // 4) for g in range(NG)]
        kv_done = State()

        def col(name, m):
            c = COLS[name] + m
            return cols[:, c:c + 1]

        def rows(r, n=2):
            return bc[:, r, :].unsqueeze(1).to_broadcast([128, n, 256])


        def stage(src, parts, n, k, tf):
            sp.wait(tf)
            dst = RAW[0:parts, k, 0:n]
            return dst, load(dst if len(src.shape) == 2 else dst.rearrange("p (a b) -> p a b", a=src.shape[1]), src)

        def halves(H, L, src, parts, n, name):
            yield sp, ring.peek
            k, tf = ring.take()
            raw, t = stage(src, parts, n, k, tf)
            yield act, lambda: t
            th = act.do(lambda e: e.activation(H, raw, ACT.Copy), t, c=n * CA)
            yield pool, lambda: th
            tl = pool.do(lambda e: e.tensor_tensor(L, raw, f(H), ALU.subtract), th, t, c=n * CP)
            ring.give(k, tl)
            t_w[name] = tl

        def norm(src, need, scale1=1.0, add=EPS, n=2):
            yield dve, lambda: [need(), xns.peek(), sms.peek()]
            t_src = need()
            k, tf = xns.take()
            m, tm = sms.take()
            dst = XN[:, k, :, :]
            dve.wait(tm)
            for i in range(n):
                st = SM[:, m, i, 0:6]
                t = dve.do(lambda e, i=i, st=st: e.bn_stats(st, src[:, i, :]), t_src, c=0.33)
            for i in range(n):
                st = SM[:, m, i, 0:6]
                mv = SM[:, m, i, 6:8]
                t = dve.do(lambda e, st=st, mv=mv: e.bn_aggr(mv, st), t, c=0.08)
            t = dve.do(lambda e: e.tensor_scalar(SM[:, m, 0:n, 8], SM[:, m, 0:n, 7], scale1, add, ALU.mult, ALU.add),
                       t, c=0.08)
            yield pool, lambda: t
            t = pool.do(lambda e: e.tensor_tensor(SM[:, m, 0:n, 9], SM[:, m, 0:n, 8], nhalf[:, 0:n], ALU.pow), t,
                        t_nh, c=0.6)
            yield dve, lambda: t
            ts = []
            if n == 2:
                tm = dve.do(lambda e: e.scalar_tensor_tensor(out=SM[:, m, 1, 10:11], in0=SM[:, m, 1, 6:7],
                                                             scalar=-1.0, in1=SM[:, m, 1, 9:10], op0=ALU.mult,
                                                             op1=ALU.mult), t, c=0.08)
            ts.append(dve.do(lambda e: e.tensor_scalar(dst[:, 0, :], src[:, 0, :], SM[:, m, 0, 6:7],
                                                       SM[:, m, 0, 9:10], ALU.subtract, ALU.mult), t, tf, c=0.33))
            if n == 2:
                yield act, lambda: tm
                ts.append(act.do(lambda e: e.activation(dst[:, 1, :], src[:, 1, :], ACT.Identity,
                                                        bias=SM[:, m, 1, 10:11], scale=SM[:, m, 1, 9:10]),
                                 tm, t, tf, c=0.49))
            sms.give(m, ts)
            return dst, ts, k

        def turn(xn, t_xn, n=2):
            yield pe, lambda: [t_xn, banks.peek(), xts.peek()]
            p, tb = banks.take()
            k, tf = xts.take()
            w = n * 128
            pe.wait(t_xn, t_id, tb)
            for i in range(n):
                for c in range(2):
                    fn = (lambda e, i=i, c=c: e.transpose(PB[p][:, c * w + i * 128:c * w + (i + 1) * 128],
                                                          xn[:, i, c * 128:(c + 1) * 128], ident[:, :]))
                    if i + c < n:
                        pe.go(fn)
                    else:
                        t = pe.do(fn)
            H, L = XTH[:, k, :, 0:w], XTL[:, k, :, 0:w]
            src = PB[p][:, 0:2 * w].rearrange("p (c t) -> p c t", c=2)
            yield act, lambda: t
            th = act.do(lambda e: e.activation(H, src, ACT.Copy), t, tf, c=2 * w * CA)
            yield dve, lambda: th
            tl = dve.do(lambda e: e.tensor_tensor(L, src, f(H), ALU.subtract), th, t, c=2 * w * CF)
            banks.give(p, tl)
            return H, L, tl, k, t

        def three(dst, pairs, waits=(), c=0.109, first=True, last=True):
            n = len(pairs) * 3
            j = 0
            pe.wait(*waits)
            for (sh, sl), (mh, ml) in pairs:
                for a, b in ((sh, mh), (sh, ml), (sl, mh)):
                    fn = lambda e, a=a, b=b, j=j: e.matmul(dst, a, b, start=first and (j == 0),
                                                                stop=last and (j == n - 1))
                    j += 1
                    if j < n:
                        pe.go(fn, c=c)
                    else:
                        t = pe.do(fn, c=c)
            return t

        def full(dst, pairs, waits=(), c=0.43):
            pe.wait(*waits)
            for j, (a, b) in enumerate(pairs):
                fn = lambda e, a=a, b=b, j=j: e.matmul(dst, a, b, start=(j == 0), stop=(j == len(pairs) - 1))
                if j < len(pairs) - 1:
                    pe.go(fn, c=c)
                else:
                    t = pe.do(fn, c=c)
            return t


        def keys0(b):
            yield pe, lambda: [banks.peek(), t_ctxT, t_wkv]
            n, tb = banks.take()
            for m in range(2):
                t = full(PB[n][:, m * NK:(m + 1) * NK],
                         [(WKV[:, c, m * 128:(m + 1) * 128], ctxT[:, c, b * NK:(b + 1) * NK]) for c in range(2)],
                         (t_ctxT, t_wkv, tb))
            yield dve, lambda: [t, t_cols, kv_done["kb", b]]
            for m in range(2):
                t = dve.do(lambda e, m=m: e.tensor_scalar(KF[:, m, :], PB[n][:, m * NK:(m + 1) * NK], col("b_k", m),
                                                          0.25, ALU.add, ALU.mult), t, t_cols, c=0.15)
            banks.give(n, t)
            KHr = KBH[:, 0:2, :]
            th = dve.do(lambda e: e.tensor_copy(KHr, KF[:, :, :]), t, kv_done["kb", b], c=0.2)
            t1 = dve.do(lambda e: e.tensor_tensor(KTL[:, :, :], KF[:, :, :], f(KHr), ALU.subtract), th, c=0.2)
            t2 = dve.do(lambda e: e.tensor_copy(KTH[:, :, :], f(KHr)), t1, c=0.2)
            for m in range(2):
                for B, T in ((KBH, KTH), (KBL, KTL)):
                    t = dve.do(lambda e, m=m, B=B, T=T: e.tensor_tensor(
                        B[:, 8 * m:8 * m + 8, :], T[:, m, :].unsqueeze(1).to_broadcast([128, 8, NK]),
                        mask8[:, :].unsqueeze(2).to_broadcast([128, 8, NK]), ALU.mult), t2, t_m8, c=0.7)
            t_w["kb", b] = t

        def values0(b):
            tv = kv_done["vb", b]
            yield act, lambda: [t_ctxT, ets.peek(), kv_done["vb", b]]
            tv = kv_done["vb", b]
            kr, tr = ets.take()
            crs = [[tr], [tr]]
            for c in range(5):
                M = CM[c]
                k = c % 2
                yield act, lambda: crs[k]
                r = CW * c
                end = r + M
                while r < end:
                    key = r % NK
                    n = min(end - r, NK - key)
                    o = r - CW * c
                    t = act.do(lambda e, o=o, n=n, key=key, k=k: e.activation(
                        CR[:, k, :, o:o + n], ctxT[:, :, b * NK + key:b * NK + key + n], ACT.Copy),
                        t_ctxT, crs[k], c=0.2)
                    r += n
                yield pe, lambda: [t, banks.peek()]
                p, tb = banks.take()
                t = full(PB[p][0:M, 0:256], [(CR[:, k, j, 0:M], WKV[:, j, 256:512]) for j in range(2)],
                         (t, t_wvv, tb))
                crs[k] = [t]
                yield dve, lambda: [t, t_bc, xts.peek(), hfs.peek()]
                kx, tx = xts.take()
                kf, tf = hfs.take()
                VF = HF[0:M, kf, 0, :]
                VH = XTH[0:M, kx, 0, :]
                VL = HF[0:M, kf, 1, :]
                t = dve.do(lambda e, p=p, M=M, VF=VF: e.tensor_tensor(VF, PB[p][0:M, 0:256], bc[0:M, BV, :], ALU.add),
                           t, t_bc, tf, c=0.33)
                banks.give(p, t)
                th = dve.do(lambda e, VF=VF, VH=VH: e.tensor_copy(VH, VF), t, tx, c=0.33)
                tl = dve.do(lambda e, VF=VF, VH=VH, VL=VL: e.tensor_tensor(VL, VF, f(VH), ALU.subtract), th, c=0.33)
                for B, T in ((VBH, f(VH)), (VBL, VL)):
                    t = dve.do(lambda e, c=c, M=M, B=B, T=T: e.tensor_tensor(
                        B[0:M, c, :, :].rearrange("p a (h d) -> p a h d", h=8),
                        T.rearrange("p (a h d) -> p a h d", a=2, h=8),
                        mask5[0:M, c, :].unsqueeze(1).unsqueeze(3).to_broadcast([M, 2, 8, 16]), ALU.mult),
                        tl, t_m5, tv, c=0.33)
                hfs.give(kf, t)
                xts.give(kx, t)
            ets.give(kr, [crs[0], crs[1]])
            t_w["vb", b] = t


        def load_x(g):
            s = gs[g]
            if g == 0:
                s["kx"], s["x0"] = x_k[0], t_x0
            else:
                yield sp, lambda: [slots.peek(), gs[g - 1]["x0"], gs[g - 1]["begun"] if g > 1 else None]
                s["kx"], tf = slots.take()
                sp.wait(tf)
                s["x0"] = load(XS[s["kx"]], x_v[g])
            s["x"] = XS[s["kx"]]

        def a1(g):
            s = gs[g]
            yield dve, lambda: s["x0"]
            xn, t, k = yield from norm(s["x"], lambda: s["x0"])
            s["begun"] = t
            s["t_xr"] = pool.do(lambda e: e.tensor_tensor(s["x"], s["x"], rows(BO), ALU.add), t, t_bc, c=1.2)
            s["H"], s["L"], t_xt, s["k"], tp = yield from turn(xn, t)
            s["xt"] = t_xt
            xns.give(k, tp)

        def a2(g):
            s = gs[g]
            yield pe, lambda: [s["xt"], t_w["q"], banks.peek(), xts.peek()]
            H, L = s["H"], s["L"]
            p, tb = banks.take()
            s["kq"], tf = xts.take()
            for m in range(2):
                ms = slice(m * 128, (m + 1) * 128)
                t = three(PB[p][:, m * 256:(m + 1) * 256],
                          [((WqH[:, c, ms], WqL[:, c, ms]), (H[:, c, :], L[:, c, :])) for c in range(2)],
                          (s["xt"], t_w["q"], tb))
            xts.give(s["k"], t)
            QH, QL = XTH[:, s["kq"], :, :], XTL[:, s["kq"], :, :]
            s["q"] = QH, QL
            yield act, lambda: t
            for m in range(2):
                th = act.do(lambda e, m=m: e.activation(QH[:, m, :], PB[p][:, m * 256:(m + 1) * 256], ACT.Identity,
                                                        bias=col("b_q", m)), t, t_cols, tf, c=0.36)
            yield dve, lambda: th
            for m in range(2):
                tl = dve.do(lambda e, m=m: e.scalar_tensor_tensor(
                    out=QL[:, m, :], in0=PB[p][:, m * 256:(m + 1) * 256], scalar=col("b_q", m), in1=f(QH[:, m, :]),
                    op0=ALU.add, op1=ALU.subtract), th, t, c=0.35)
            banks.give(p, tl)
            s["t_q"] = tl

        def heads4(T):
            return T.rearrange("p (a h) k -> p a h k", a=4)

        def score(g, i):
            s = gs[g]
            b = s["b"]
            yield pe, lambda: [s["t_q"], t_w["kb", b], s4.peek(), es.peek(), s["scored", 0] if i else None]
            QH, QL = s["q"]
            _, t4 = s4.take()
            ke, te = es.take()
            s["ke", i] = ke
            ts = slice(i * 128, (i + 1) * 128)
            for a in range(4):
                m = a // 2
                kh = KBH[:, 4 * a:4 * a + 4, :].rearrange("p h k -> p (h k)")
                kl = KBL[:, 4 * a:4 * a + 4, :].rearrange("p h k -> p (h k)")
                t = three(S4[:, a, 0:4 * NK], [((QH[:, m, ts], QL[:, m, ts]), (kh, kl))],
                          (s["t_q"], t_w["kb", b], t4), c=0.131)
            s["scored", i] = t
            if i == 1:
                xts.give(s["kq"], t)
                if g == 3:
                    kv_done["kb", 1] = t
            sx = SX[:, ke, :, :]
            sv = S4[:, :, 0:4 * NK].rearrange("p a (h k) -> p a h k", k=NK)
            Ei = E[:, ke, :, :]
            mx = sx[:, 0, :].rearrange("p (a h) -> p a h", a=4)
            yield dve, lambda: [t, te]
            t = dve.do(lambda e: e.tensor_reduce(mx, sv, AX, ALU.max), t, te, c=1.35)
            t = dve.do(lambda e: e.tensor_tensor(heads4(Ei), sv, mx.unsqueeze(3).to_broadcast([128, 4, 4, NK]),
                                                 ALU.subtract), t, c=1.35)
            s4.give(0, t)
            yield act, lambda: t
            t = act.do(lambda e: e.activation(Ei, Ei, ACT.Exp), t, c=1.13)
            s["t_e", i] = t
            yield dve, lambda: t
            t = dve.do(lambda e: e.tensor_reduce(sx[:, 1, :], Ei, AX, ALU.add), t, c=1.35)
            s["t_r", i] = dve.do(lambda e: e.reciprocal(sx[:, 2, :], sx[:, 1, :]), t, c=0.17)

        def weigh(g, i):
            s = gs[g]
            yield act, lambda: [s["t_r", i], rrs.peek()]
            _, trr = rrs.take()
            ke = s["ke", i]
            t_r = act.do(lambda e: e.activation(RR[:, :, :], SX[:, ke, 2, :].unsqueeze(2)
                                                .to_broadcast([128, 16, 16]), ACT.Copy), s["t_r", i], trr, c=0.28)
            yield pe, lambda: [t_r, s["t_e", i], s4.peek(), ets.peek() if i == 0 else s["et"]]
            if i == 0:
                s["ket"], s["et"] = ets.take()
            tet = s["et"]
            _, t4 = s4.take()
            ef = E[:, ke, :, :].rearrange("p h k -> p (h k)")
            pe.wait(s["t_e", i], t4)
            for c in range(5):
                for a in range(2):
                    M = CM[c]
                    o = a * 616 + CW * c
                    dst = S4[0:M, a, c * 128:(c + 1) * 128] if c < 4 else S4[0:M, 2, a * 128:(a + 1) * 128]
                    t = pe.do(lambda e, dst=dst, o=o, M=M: e.transpose(dst, ef[:, o:o + M], ident[:, :]))
            te = t
            rf = RR[:, :, :].rearrange("p a b -> p (a b)")
            for a in range(2):
                t = pe.do(lambda e, a=a: e.transpose(S4[:, 3, a * 128:(a + 1) * 128], rf[:, a * 128:(a + 1) * 128],
                                                     ident[:, :]), t_r)
            rrs.give(0, t)
            es.give(ke, t)
            ts = slice(i * 128, (i + 1) * 128)
            srcs = [(S4[0:CW, 0:2, :].rearrange("p a (c t) -> p a c t", c=4), CW, slice(0, 4), 1024),
                    (S4[0:120, 2, 0:256].rearrange("p (a t) -> p a t", a=2), 120, 4, 256)]
            yield act, lambda: [te, tet]
            ths = []
            for src, M, cs, n in srcs:
                ths.append(act.do(lambda e, src=src, M=M, cs=cs: e.activation(ETH[0:M, :, cs, ts], src, ACT.Copy),
                                  te, tet, c=0.06 + n * CA))
            tr = act.do(lambda e: e.activation(RT[:, :, ts], S4[:, 3, 0:256].rearrange("p (a t) -> p a t", a=2),
                                               ACT.Copy), t, tet, c=0.28)
            yield dve, lambda: ths[0]
            for (src, M, cs, n), th in zip(srcs, ths):
                tl = dve.do(lambda e, src=src, M=M, cs=cs: e.tensor_tensor(ETL[0:M, :, cs, ts], src,
                                                                           f(ETH[0:M, :, cs, ts]), ALU.subtract),
                            th, tet, te, c=0.06 + n * CF)
            s4.give(0, [tl, tr])
            s["t_et", i], s["t_rt", i] = tl, tr

        def pv(g):
            s = gs[g]
            b = s["b"]
            need = lambda: [s["t_et", 0], s["t_et", 1], s["t_rt", 0], s["t_rt", 1], t_w["vb", b], banks.peek(),
                            xts.peek()]
            yield pe, need
            w = need()
            p, tb = banks.take()
            s["ko"], tf = xts.take()
            for a in range(2):
                pairs = [((VBH[0:CM[c], c, a, :], VBL[0:CM[c], c, a, :]),
                          (ETH[0:CM[c], a, c, :], ETL[0:CM[c], a, c, :])) for c in range(5)]
                if a:
                    yield pe, lambda: t
                t = three(PB[p][:, a * 256:(a + 1) * 256], pairs, w[:6])
            tpv = t
            if g == 3:
                kv_done["vb", 1] = t
            yield dve, lambda: t
            t = dve.do(lambda e: e.tensor_tensor(RT[:, :, :], two(PB[p][:, :]), RT[:, :, :], ALU.mult), t,
                       s["t_rt", 0], s["t_rt", 1], c=0.6)
            banks.give(p, t)
            OH, OL = XTH[:, s["ko"], :, :], XTL[:, s["ko"], :, :]
            s["o"] = OH, OL
            yield act, lambda: t
            th = act.do(lambda e: e.activation(OH, RT[:, :, :], ACT.Copy), t, tf, c=0.49)
            yield dve, lambda: th
            tl = dve.do(lambda e: e.tensor_tensor(OL, RT[:, :, :], f(OH), ALU.subtract), th, c=0.6)
            ets.give(s["ket"], [tl, tpv])
            s["t_o"] = tl

        def wo(g):
            s = gs[g]
            yield pe, lambda: [s["t_o"], t_w["o"], banks.peek()]
            OH, OL = s["o"]
            p, tb = banks.take()
            for i in range(2):
                ts = slice(i * 128, (i + 1) * 128)
                t = three(PB[p][:, i * 256:(i + 1) * 256],
                          [((OH[:, a, ts], OL[:, a, ts]), (WoH[:, a, :], WoL[:, a, :])) for a in range(2)],
                          (s["t_o"], t_w["o"], tb))
            xts.give(s["ko"], t)
            yield dve, lambda: t
            t = dve.do(lambda e: e.tensor_tensor(s["x"], two(PB[p][:, :]), s["x"], ALU.add), t, s["t_xr"], c=0.6)
            banks.give(p, t)
            s["x1"] = t

        def b1(g):
            s = gs[g]
            yield dve, lambda: s["x1"]
            xn, t, k = yield from norm(s["x"], lambda: s["x1"])
            s["t_x1b"] = pool.do(lambda e: e.tensor_tensor(s["x"], s["x"], rows(BETA), ALU.add), t, c=1.2)
            s["H"], s["L"], t_xt, s["k"], tp = yield from turn(xn, t)
            s["t_xrb"] = pool.do(lambda e: e.tensor_tensor(xn, xn, rows(B2), ALU.add), tp, t, c=1.2)
            s["y"], s["ky"] = xn, k
            s["hused"] = []
            s["xt1"] = t_xt

        def w1(g, j):
            s = gs[g]
            yield pe, lambda: [s["xt1"], t_w["w1", 0], t_w["w1", 1], banks.peek(), hfs.peek(),
                               hhs.peek() if j == 0 else s["hh"]]
            if j == 0:
                s["khh"], s["hh"] = hhs.take()
            tf = s["hh"]
            H, L = s["H"], s["L"]
            p, tb = banks.take()
            k, tk = hfs.take()
            for q in range(2):
                fs = slice((2 * j + q) * 128, (2 * j + q + 1) * 128)
                t = three(PB[p][:, q * 256:(q + 1) * 256],
                          [((W1H[:, c, fs], W1L[:, c, fs]), (H[:, c, :], L[:, c, :])) for c in range(2)],
                          (s["xt1"], t_w["w1", 0], t_w["w1", 1], tb))
            s["hused"].append(t)
            if len(s["hused"]) == 4:
                xts.give(s["k"], s["hused"])
            yield act, lambda: t
            for q in range(2):
                t2 = act.do(lambda e, q=q: e.activation(HF[:, k, q, :], PB[p][:, q * 256:(q + 1) * 256], ACT.Relu,
                                                        bias=col("b1", 2 * j + q)), t, t_cols, tk, c=0.36)
            banks.give(p, t2)
            hs = slice(2 * j, 2 * j + 2)
            if j % 2:
                th = act.do(lambda e: e.activation(HH[:, hs, :], HF[:, k, :, :], ACT.Copy), t2, tf, c=0.5)
            else:
                yield dve, lambda: t2
                th = dve.do(lambda e: e.tensor_copy(HH[:, hs, :], HF[:, k, :, :]), t2, tf, c=0.33)
            yield pool, lambda: th
            tl = pool.do(lambda e: e.tensor_tensor(HL[:, hs, :], HF[:, k, :, :], f(HH[:, hs, :]), ALU.subtract), th,
                         t2, tf, c=1.2)
            hfs.give(k, tl)
            s["t_h", j] = tl

        def w2(g):
            s = gs[g]
            hs = lambda: [s["t_h", j] for j in range(4)]
            yield pe, lambda: [hs(), t_w["w2", 0], t_w["w2", 1], banks.peek()]
            p, tb = banks.take()
            for i in range(2):
                ts = slice(i * 128, (i + 1) * 128)
                pairs = [((HH[:, j, ts], HL[:, j, ts]), (W2H[:, j, :], W2L[:, j, :])) for j in range(8)]
                for a in range(0, 8, 4):
                    if i + a:
                        yield pe, lambda: t
                    t = three(PB[p][:, i * 256:(i + 1) * 256], pairs[a:a + 4],
                              (hs(), t_w["w2", 0], t_w["w2", 1], tb), first=a == 0, last=a == 4)
            hhs.give(s["khh"], t)
            yield dve, lambda: [t, s["t_xrb"]]
            y = s["y"]
            t = dve.do(lambda e: e.tensor_tensor(y, two(PB[p][:, :]), y, ALU.add), t, s["t_xrb"], c=0.6)
            banks.give(p, t)
            s["t_y"] = t

        def b3(g):
            s = gs[g]
            yield dve, lambda: s["t_y"]
            yn, t, k = yield from norm(s["y"], lambda: s["t_y"])
            xns.give(s["ky"], t)
            yield pool, lambda: t
            t = pool.do(lambda e: e.tensor_tensor(yn, yn, rows(GAMMA), ALU.mult), t, c=1.2)
            t = pool.do(lambda e: e.tensor_tensor(s["x"], yn, s["x"], ALU.add), t, s["t_x1b"], c=1.2)
            xns.give(k, t)
            s["x2"] = t

        def c1(g):
            s = gs[g]
            yield dve, lambda: s["x2"]
            xn, t, k = yield from norm(s["x"], lambda: s["x2"], 1.0 + EPS, EPS * EPS)
            s["t_xrc"] = pool.do(lambda e: e.tensor_tensor(s["x"], s["x"], rows(BO1), ALU.add), t, c=1.2)
            s["H"], s["L"], t_xt, s["k"], tp = yield from turn(xn, t)
            s["xt2"] = t_xt
            xns.give(k, tp)

        def c2(g):
            s = gs[g]
            b = s["b"]
            yield pe, lambda: [s["xt2"], t_w["m1"], banks.peek(), pps.peek(), sts.peek()]
            n1, tb = banks.take()
            _, tpp = pps.take()
            _, tst = sts.take()
            H, L = s["H"], s["L"]
            t = three(PB[n1][0:NK, 0:256], [((M1H[:, c, b, :], M1L[:, c, b, :]), (H[:, c, :], L[:, c, :]))
                                           for c in range(2)], (s["xt2"], t_w["m1"], tb))
            xts.give(s["k"], t)
            yield act, lambda: t
            t = act.do(lambda e: e.activation(ST[:, :], PB[n1][0:NK, 0:256], ACT.Identity, bias=cT[:, b:b + 1]), t,
                       t_w["m1"], tst, c=0.36)
            yield pe, lambda: t
            for i in range(2):
                t = pe.do(lambda e, i=i: e.transpose(PB[n1][:, i * NK:(i + 1) * NK], ST[:, i * 128:(i + 1) * 128],
                                                     ident[0:NK, 0:NK]), t)
            sts.give(0, t)
            sv = PB[n1][:, 0:2 * NK].rearrange("p (i k) -> p i k", i=2)
            yield dve, lambda: t
            t = dve.do(lambda e: e.tensor_reduce(PS[:, 0, :], sv, AX, ALU.max), t, tpp, c=0.23)
            t = dve.do(lambda e: e.tensor_tensor(PP[:, :, :], sv, PS[:, 0, :].unsqueeze(2)
                                                 .to_broadcast([128, 2, NK]), ALU.subtract), t, tpp, c=0.23)
            banks.give(n1, t)
            yield act, lambda: t
            t = act.do(lambda e: e.activation(PP[:, :, :], PP[:, :, :], ACT.Exp), t, c=0.2)
            yield dve, lambda: t
            t = dve.do(lambda e: e.tensor_reduce(PS[:, 1, :], PP[:, :, :], AX, ALU.add), t, c=0.2)
            t = dve.do(lambda e: e.reciprocal(PS[:, 2, :], PS[:, 1, :]), t, c=0.08)
            t = dve.do(lambda e: e.tensor_tensor(PP[:, :, :], PP[:, :, :], PS[:, 2, :].unsqueeze(2)
                                                 .to_broadcast([128, 2, NK]), ALU.mult), t, c=0.2)
            yield pe, lambda: [t, banks.peek(), ptts.peek()]
            n, tb = banks.take()
            _, tpt = ptts.take()
            for i in range(2):
                t = pe.do(lambda e, i=i, n=n: e.transpose(PB[n][0:NK, i * 128:(i + 1) * 128], PP[:, i, :],
                                                          ident[:, :]), t, tb)
            pps.give(0, t)
            yield act, lambda: [t, t_w["pz"]]
            t = act.do(lambda e, n=n: e.activation(PTT[0:NK, :], PB[n][0:NK, 0:256], ACT.Copy), t, t_w["pz"], tpt,
                       c=0.28)
            yield pe, lambda: [t, t_w["m2"]]
            for i in range(2):
                tm = full(PB[n][:, i * 256:(i + 1) * 256], [(PTT[:, i * 128:(i + 1) * 128], M2[:, b, :])],
                          (t, t_w["m2"]))
            t = tm
            ptts.give(0, t)
            yield dve, lambda: [t, s["t_xrc"]]
            t = dve.do(lambda e, n=n: e.tensor_tensor(s["x"], two(PB[n][:, :]), s["x"], ALU.add), t, s["t_xrc"],
                       c=0.6)
            banks.give(n, t)
            yield sp, lambda: t
            sp.wait(t)
            r = (g % 4) * 256
            t = load(scratch[b][r:r + 256, :].rearrange("(i p) n -> p i n", i=2), s["x"])
            slots.give(s["kx"], t)
            s["x3"] = t


        s_ga = [sem(f"s_ga{k}") for k in range(NX + 2)]
        s_sc = [sem(f"s_sc{k}") for k in range(NX + 2)]
        n_ga, n_sc = [0] * (NX + 2), [0] * (NX + 2)
        s_bb = [sem(f"s_bb{k}") for k in range(2)]
        n_bb = [0, 0]
        bb_k, bb_at = {}, State()
        pairs_done = []

        def bias(b, r):
            yield sp, lambda: [bbs.peek(), t_w["route"], ("order", 0, 0.0) if (b, r) == (0, 0) else bb_at[8 * b + r - 1]]
            k, tb = bbs.take()
            sp.wait(tb, t_w["route"])
            blocks = [q for q in (2 * r, 2 * r + 1) if q < NB]
            for i, q in enumerate(blocks):
                def fetch(e, i=i, q=q):
                    v = e.value_load(EV[0:1, 0, q:q + 1], min_val=0, max_val=7)
                    e.dma_start(BB[:, k, i, :], A["bD"][bass.ds(v, 1), :].to_broadcast([128, 256])).then_inc(
                        s_bb[k], 16)
                sp.go(fetch, c=0.3)
            n_bb[k] += 16 * len(blocks)
            bb_k[8 * b + r] = k
            bb_at[8 * b + r] = (s_bb[k], n_bb[k], sp.now + 2.2)

        def expert(b, r):
            blocks = [q for q in (2 * r, 2 * r + 1) if q < NB]
            n = len(blocks)
            need = lambda: [t_w["route"], [gs[g]["x3"] for g in range(4 * b, 4 * b + 4)], slots.peek()]
            yield pool, need
            w = need()
            k, tf = slots.take()
            x = XS[k]
            pool.wait(w[0], w[1], tf)
            for i, q in enumerate(blocks):
                pool.go(lambda e, i=i, q=q, k=k: e.indirect_dma_start(
                    x[:, i, :], None, scratch[b][:, :],
                    bass.IndirectOffsetOnAxis(ap=GI[:, 0, q:q + 1], axis=0)).then_inc(s_ga[k], 16), c=1.0)
            n_ga[k] += 16 * n
            tg = (s_ga[k], n_ga[k], pool.now + 3.0)
            xn, t, kn = yield from norm(x, lambda: tg, n=n)
            e_ = 8 * b + r
            q_, c_ = (pool, CP) if (e_ % 8) in BIAS_ON_POOL else (dve, CF)
            yield q_, lambda: [t, bb_at[e_]]
            kb = bb_k[e_]
            tx = q_.do(lambda e: e.tensor_tensor(x[:, 0:n, :], x[:, 0:n, :], BB[:, kb, 0:n, :], ALU.add), t, tg,
                       bb_at[e_], c=256 * n * c_)
            bbs.give(kb, tx)
            H, L, txt, kt, tp = yield from turn(xn, t, n)
            xns.give(kn, tp)
            yield pe, lambda: [txt, t_w["wd"], banks.peek()]
            p, tb = banks.take()
            pe.wait(txt, t_w["wd"], tb, t_w["route"])
            for i, q in enumerate(blocks):
                dst = PB[p][:, i * 256:(i + 1) * 256]
                ts = slice(i * 128, (i + 1) * 128)
                box = {}

                def first(e, dst=dst, ts=ts, q=q, box=box):
                    box["v"] = e.value_load(EV[0:1, 1, q:q + 1], min_val=0, max_val=7 * 256)
                pe.go(first, c=0.1)
                terms = [(A_, W_, c) for c in range(2) for A_, W_ in ((H, WDH), (H, WDL), (L, WDH))]
                for j, (A_, W_, c) in enumerate(terms):
                    fn = (lambda e, j=j, A_=A_, W_=W_, c=c, dst=dst, ts=ts, box=box: e.matmul(
                        dst, A_[:, c, ts], W_[:, c, bass.ds(box["v"], 256)], start=(j == 0), stop=(j == 5)))
                    if j < 5:
                        pe.go(fn)
                    else:
                        t = pe.do(fn)
            xts.give(kt, t)
            yield dve, lambda: [t, tx]
            t = dve.do(lambda e: e.tensor_tensor(x[:, 0:n, :], PB[p][:, 0:n * 256].rearrange("p (i n) -> p i n", i=n),
                                                 x[:, 0:n, :], ALU.add), t, tx, c=0.3 * n)
            banks.give(p, t)
            yield pool, lambda: t
            pool.wait(t)
            for i, q in enumerate(blocks):
                pool.go(lambda e, i=i, q=q, k=k: e.indirect_dma_start(
                    out[:, :], bass.IndirectOffsetOnAxis(ap=SI[:, b, q:q + 1], axis=0), x[:, i, :], None,
                    bounds_check=2047, oob_is_err=False).then_inc(s_sc[k], 16), c=1.0)
            n_sc[k] += 16 * n
            t = (s_sc[k], n_sc[k], pool.now + 3.0)
            slots.give(k, t)
            pairs_done.append(t)


        def fold():
            yield sp, lambda: [hfs.peek() if len(hfs.open) > 1 else BUSY, ring.peek(), es.peek()]
            ka, ta = hfs.take()
            kb, tb_ = hfs.take()
            ke, te = es.take()
            CK = HF[0:NK, ka, :, 0:192]
            CN = HF[0:NK, kb, :, 0:192]
            sp.wait(ta)
            t_ck = load(CK, A["ctx"].rearrange("b k n -> k b n"))
            kg, tf = ring.take()
            sp.wait(tf)
            GB = RAW[0:NK, kg, 0:384].rearrange("p (r n) -> p r n", r=2)
            t_gb = load(GB, A["rows2"].rearrange("(a r) n -> a r n", a=1).to_broadcast([NK, 2, 192]))
            m = 11
            yield dve, lambda: t_ck
            for i in range(2):
                t = dve.do(lambda e, i=i: e.bn_stats(SM[0:NK, m, i, 0:6], CK[:, i, :]), t_ck, tb_, t_sm, c=0.25)
                t = dve.do(lambda e, i=i: e.bn_aggr(SM[0:NK, m, i, 6:8], SM[0:NK, m, i, 0:6]), t, c=0.08)
            t = dve.do(lambda e: e.tensor_scalar(SM[0:NK, m, :, 8], SM[0:NK, m, :, 7], EPS, None, ALU.add), t, c=0.08)
            yield pool, lambda: t
            t = pool.do(lambda e: e.tensor_tensor(SM[0:NK, m, :, 9], SM[0:NK, m, :, 8], nhalf[0:NK, :], ALU.pow), t,
                        t_nh, c=0.6)
            yield dve, lambda: [t, t_gb]
            for i in range(2):
                t1 = dve.do(lambda e, i=i: e.tensor_scalar(CN[:, i, :], CK[:, i, :], SM[0:NK, m, i, 6:7],
                                                           SM[0:NK, m, i, 9:10], ALU.subtract, ALU.mult), t, c=0.26)
            t = dve.do(lambda e: e.tensor_tensor(CN, CN, GB[:, 0, :].unsqueeze(1).to_broadcast([NK, 2, 192]),
                                                 ALU.mult), t1, t_gb, c=0.46)
            t = dve.do(lambda e: e.tensor_tensor(CN, CN, GB[:, 1, :].unsqueeze(1).to_broadcast([NK, 2, 192]),
                                                 ALU.add), t, c=0.46)
            ring.give(kg, t)
            yield pe, lambda: [t, banks.peek()]
            n, tb = banks.take()
            for c in range(2):
                for i in range(2):
                    o = (c * 2 + i) * NK
                    tt = pe.do(lambda e, c=c, i=i, o=o, n=n: e.transpose(PB[n][0:96, o:o + NK],
                                                                         CN[:, i, c * 96:(c + 1) * 96],
                                                                         ident[0:NK, 0:NK]), t, t_id, tb)
            yield act, lambda: tt
            EE = E[:, ke, :, :]
            CT = EE[0:96, 12:16, :].rearrange("p h k -> p (h k)").rearrange("p (c k) -> p c k", c=2)
            t_ct = act.do(lambda e, n=n: e.activation(CT, PB[n][0:96, 0:4 * NK].rearrange("p (c k) -> p c k", c=2),
                                                      ACT.Copy), tt, te, c=0.3)
            banks.give(n, t_ct)
            hfs.give(ka, t_ct)
            hfs.give(kb, t_ct)
            K1S = EE[:, 0:4, :].rearrange("p h k -> p (h k)").rearrange("p (m k) -> p m k", m=2)
            V1S = EE[:, 4:8, :].rearrange("p h k -> p (h k)").rearrange("p (m k) -> p m k", m=2)
            M1S = EE[:, 8:12, :].rearrange("p h k -> p (h k)").rearrange("p (m b k) -> p m b k", m=2, b=2)
            done = {}
            for name, dst, bias in (("Wk", K1S, "bk1"), ("Wv", V1S, "bv1")):
                yield sp, ring.peek
                kk, tf = ring.take()
                w, tw = stage(A[name].rearrange("(c p) n -> p c n", p=96), 96, 512, kk, tf)
                wv = two(w)
                yield pe, lambda: [t_ct, tw, banks.peek()]
                n, tb = banks.take()
                for m_ in range(2):
                    tp = full(PB[n][:, m_ * 154:(m_ + 1) * 154],
                              [(wv[:, c, m_ * 128:(m_ + 1) * 128], CT[:, c, :]) for c in range(2)],
                              (t_ct, tw, tb))
                ring.give(kk, tp)
                yield dve, lambda: [tp, t_cols]
                for m_ in range(2):
                    td = dve.do(lambda e, m=m_, n=n, dst=dst, bias=bias: e.tensor_scalar(
                        dst[:, m, :], PB[n][:, m * 154:(m + 1) * 154], col(bias, m), None, ALU.add), tp, t_cols,
                        te, c=0.22)
                banks.give(n, td)
                done[bias] = td
            t_k1, t_v1 = done["bk1"], done["bv1"]
            yield sp, ring.peek
            k, tf = ring.take()
            wqT, t_wqT = stage(A["WqT"].rearrange("(c p) n -> p c n", p=128), 128, 512, k, tf)
            wqT = two(wqT)
            yield pe, lambda: [t_k1, t_wqT, banks.peek()]
            n, tb = banks.take()
            for m_ in range(2):
                t = full(PB[n][:, m_ * 154:(m_ + 1) * 154],
                         [(wqT[:, c, m_ * 128:(m_ + 1) * 128], K1S[:, c, :]) for c in range(2)],
                         (t_k1, t_wqT, tb))
            ring.give(k, t)
            yield dve, lambda: t
            for m_ in range(2):
                t1 = dve.do(lambda e, m=m_, n=n: e.tensor_scalar(
                    M1S[:, m, :, :], PB[n][:, m * 154:(m + 1) * 154].rearrange("p (b k) -> p b k", b=2),
                    col("g1", m), 0.0625, ALU.mult, ALU.mult), t, c=0.22)
            banks.give(n, t1)
            th = dve.do(lambda e: e.tensor_copy(M1H[:, :, :, :], M1S), t1, c=0.22)
            tl = dve.do(lambda e: e.tensor_tensor(M1L[:, :, :, :], M1S, f(M1H[:, :, :, :]), ALU.subtract), th, c=0.36)
            yield sp, ring.peek
            k, tf = ring.take()
            wqn, t_wqn = stage(A["Wq"].rearrange("(c p) n -> p c n", p=128), 128, 512, k, tf)
            wqn = two(wqn)
            yield pe, lambda: [t_wqn, banks.peek()]
            n, tb = banks.take()
            for m_ in range(2):
                t = full(PB[n][:, m_:m_ + 1], [(wqn[:, c, m_ * 128:(m_ + 1) * 128], col("be1", c)) for c in range(2)],
                         (t_wqn, t_cols, tb))
            ring.give(k, t)
            yield dve, lambda: t
            tq = dve.do(lambda e, n=n: e.tensor_tensor(PS[:, 3, :], PB[n][:, 0:2],
                                                       cols[:, COLS["bq1"]:COLS["bq1"] + 2], ALU.add), t, c=0.1)
            yield pe, lambda: tq
            for b in range(2):
                t = full(PB[n][0:NK, 4 + b:5 + b], [(K1S[:, c, b * NK:(b + 1) * NK], PS[:, 3, c:c + 1])
                                                    for c in range(2)], (tq,))
            yield dve, lambda: t
            tc = dve.do(lambda e, n=n: e.tensor_scalar(cT[:, :], PB[n][0:NK, 4:6], 0.0625, None, ALU.mult), t, c=0.1)
            banks.give(n, tc)
            t_w["m1"] = tc
            yield sp, ring.peek
            k, tf = ring.take()
            wo1, t_wo1 = stage(A["Wo"].rearrange("(c p) n -> p c n", p=128), 128, 512, k, tf)
            wo1 = two(wo1)
            yield pe, lambda: [t_v1, t_wo1, banks.peek()]
            n, tb = banks.take()
            for b in range(2):
                t = full(PB[n][0:NK, b * 256:(b + 1) * 256],
                         [(V1S[:, c, b * NK:(b + 1) * NK], wo1[:, c, :]) for c in range(2)],
                         (t_v1, t_wo1, tb))
            ring.give(k, t)
            es.give(ke, [t, tl])
            yield dve, lambda: t
            tz = dve.do(lambda e: e.memset(M2[64:96, :, :], 0.0), c=0.3)
            t_w["pz"] = dve.do(lambda e: e.memset(PTT[64:96, :], 0.0), c=0.2)
            t = dve.do(lambda e, n=n: e.tensor_copy(M2[0:NK, :, :], PB[n][0:NK, :].rearrange("p (b n) -> p b n", b=2)),
                       t, tz, c=0.6)
            banks.give(n, t)
            t_w["m2"] = t


        def route():
            sg = sb("sg", [32, 3, 8])
            RK = sb("RK", [128, 16])
            OHM = sb("OHM", [128, 8, 8])
            mx = sb("mx", [128, 4, 8])
            big = sb("big", [128, 16, 8])
            cum = sb("cum", [128, 9, 8])
            sbt = sb("sbt", [128, 4, 9])
            own = sb("own", [128, 8], I32)
            sl = sb("sl", [128, 8], I32)
            void = sb("void", [128, 16], I32)
            ef = sb("ef", [1, 2, 16])
            sf = sb("sf", [128, 2, 16])
            yield sp, lambda: [ring.peek() if len(ring.open) > 1 else BUSY]
            t_sg = load(sg[:, 0, :], A["sigT"])
            kp, tf = ring.take()
            kq, tfq = ring.take()
            sp.wait(tf)
            peT = RAW[0:32, kp, :]
            LT = RAW[:, kq, 0:128]
            ON = RAW[:, kq, 128:256]
            t_pe = load(peT, A["peT"])
            yield dve, lambda: t_sg
            t = dve.do(lambda e: e.tensor_scalar(sg[:, 1, :], sg[:, 0, :], 0.0, None, ALU.is_gt), t_sg)
            t = dve.do(lambda e: e.tensor_scalar(sg[:, 2, :], sg[:, 0, :], 0.0, None, ALU.is_lt), t)
            t = dve.do(lambda e: e.tensor_tensor(sg[:, 1, :], sg[:, 1, :], sg[:, 2, :], ALU.subtract), t)
            to = dve.do(lambda e: e.memset(RAW[:, kq, 0:256], 1.0), tfq)
            tc0 = dve.do(lambda e: e.memset(cum[:, 0, :], 0.0))
            tc1 = dve.do(lambda e: e.memset(sbt[:, 1, 0:1], 0.0))
            tv = dve.do(lambda e: e.memset(void[:, :], 9999))
            yield pool, lambda: to
            tlt = pool.do(lambda e: e.affine_select(out=LT, in_=LT, compare_op=ALU.is_ge, fill=0.0, base=-1,
                                                    pattern=[[1, 128]], channel_multiplier=-1), to)
            ti = pool.do(lambda e: e.iota(RK[:, :], [[1, 16]], base=0, channel_multiplier=0,
                                          allow_small_or_imprecise_dtypes=True))
            tw = pool.do(lambda e: e.iota(own[:, :], [[128, 8]], base=0, channel_multiplier=1))
            yield sp, lambda: tv
            sp.wait(tv)
            t_void = load(tab.rearrange("(p q) a -> p (q a)", p=128), void[:, :])
            yield pe, lambda: [t, t_pe, banks.peek()]
            n1, tb = banks.take()
            for j in range(8):
                tp = pe.do(lambda e, j=j: e.matmul(PB[n1][:, j * 8:(j + 1) * 8], peT[:, j * 128:(j + 1) * 128],
                                                   sg[:, 1, :], start=True, stop=True), t, t_pe, tb)
            sc = PB[n1][:, 0:64].rearrange("p (j t) -> p j t", t=8)
            rep = lambda a, w=8: a.unsqueeze(2).to_broadcast([128, a.shape[1], w])
            yield dve, lambda: [tp, ti]
            tr = dve.do(lambda e: e.tensor_scalar(mx[:, 2, :], RK[:, 0:8], -1.0, 8.0, ALU.mult, ALU.add), ti)
            rev = mx[:, 2, :].unsqueeze(1).to_broadcast([128, 8, 8])
            eq = big[:, 0:8, :]
            t = dve.do(lambda e: e.tensor_reduce(mx[:, 0, :], sc, AX, ALU.max), tp)
            t = dve.do(lambda e: e.tensor_tensor(eq, sc, rep(mx[:, 0, :]), ALU.is_equal), t)
            banks.give(n1, t)
            t = dve.do(lambda e: e.tensor_tensor(eq, eq, rev, ALU.mult), t, tr)
            t = dve.do(lambda e: e.tensor_reduce(mx[:, 1, :], eq, AX, ALU.max), t)
            t = dve.do(lambda e: e.tensor_tensor(OHM[:, :, :], rep(mx[:, 1, :]), rev, ALU.is_equal), t)
            yield pe, lambda: [t, tlt, banks.peek()]
            n, tb = banks.take()
            om = OHM[:, :, :].rearrange("p j t -> p (j t)")
            tp = pe.do(lambda e: e.matmul(PB[n][:, 0:64], LT, om, start=True, stop=True), t, tlt, tb, c=0.4)
            tp = pe.do(lambda e: e.matmul(PB[n][:, 64:128], ON, om, start=True, stop=True), to, c=0.4)
            ring.give(kp, tp)
            ring.give(kq, tp)
            rank = PB[n][:, 0:64].rearrange("p (j t) -> p j t", t=8)
            tot = PB[n][:, 64:128].rearrange("p (j t) -> p j t", t=8)
            yield dve, lambda: tp
            t = tc0
            for j in range(8):
                t = dve.do(lambda e, j=j: e.tensor_tensor(cum[:, j + 1, :], cum[:, j, :], tot[:, j, :], ALU.add), t,
                           tp)
            kk = mx[:, 3, :]
            t2 = dve.do(lambda e: e.tensor_scalar(kk, RK[:, 0:8], 128.0, None, ALU.mult), t)
            t = dve.do(lambda e: e.tensor_tensor(eq, rep(cum[:, 8, :]), kk.unsqueeze(1).to_broadcast([128, 8, 8]),
                                                 ALU.is_gt), t2)
            t = dve.do(lambda e: e.tensor_reduce(sbt[:, 0, 0:8], eq, AX, ALU.add), t)
            for k in range(8):
                t = dve.do(lambda e, k=k: e.tensor_tensor(sbt[:, 1, k + 1:k + 2], sbt[:, 1, k:k + 1],
                                                          sbt[:, 0, k:k + 1], ALU.add), t, tc1)
            t = dve.do(lambda e: e.tensor_scalar(sbt[:, 2, 0:8], sbt[:, 1, 0:8], 128.0, None, ALU.mult), t)
            t = dve.do(lambda e: e.tensor_tensor(eq, rank, cum[:, 0:8, :], ALU.add), t)
            banks.give(n, t)
            t = dve.do(lambda e: e.tensor_tensor(eq, eq, sbt[:, 2, 0:8].unsqueeze(1).to_broadcast([128, 8, 8]),
                                                 ALU.add), t)
            t = dve.do(lambda e: e.tensor_tensor(eq, eq, OHM[:, :, :], ALU.mult), t)
            t = dve.do(lambda e: e.tensor_reduce(mx[:, 0, :], eq, AX, ALU.add), t)
            t_sl = dve.do(lambda e: e.tensor_copy(sl[:, :], mx[:, 0, :]), t)
            t = dve.do(lambda e: e.tensor_tensor(big[0:1, :, :], RK[0:1, :].unsqueeze(2).to_broadcast([1, 16, 8]),
                                                 sbt[0:1, 1, 1:9].unsqueeze(1).to_broadcast([1, 16, 8]), ALU.is_ge),
                       t_sl)
            t = dve.do(lambda e: e.tensor_reduce(ef[:, 0, :], big[0:1, :, :], AX, ALU.add), t)
            t = dve.do(lambda e: e.tensor_scalar(ef[:, 0, :], ef[:, 0, :], 7.0, None, ALU.min), t)
            t = dve.do(lambda e: e.tensor_scalar(ef[:, 1, :], ef[:, 0, :], 256.0, None, ALU.mult), t)
            t_ev = dve.do(lambda e: e.tensor_copy(EV[:, :, :], ef[:, :, :]), t)
            yield pool, lambda: [t_sl, t_void, tw]
            s_tab = sem("s_tab")
            pool.wait(t_sl, t_void, tw)
            for j in range(8):
                pool.go(lambda e, j=j: e.indirect_dma_start(
                    tab, bass.IndirectOffsetOnAxis(ap=sl[:, j:j + 1], axis=0), own[:, j:j + 1],
                    None).then_inc(s_tab, 16), c=1.0)
            t_tab = (s_tab, 128, pool.now + 3)
            yield sp, lambda: t_tab
            sp.wait(t_tab)
            s_si = sem("s_si")

            def back(e):
                with nc.allow_non_contiguous_dma(reason="a table of 8 KB"):
                    e.dma_start(SI[:, 0, :], tab.rearrange("(q p) a -> p (q a)", p=128)).then_inc(s_si, 16)
            sp.go(back)
            t_si = (s_si, 16, sp.now + 8)
            yield dve, lambda: t_si
            t = dve.do(lambda e: e.tensor_copy(sf[:, 0, :], SI[:, 0, :]), t_si)
            t = dve.do(lambda e: e.tensor_scalar(sf[:, 1, :], sf[:, 0, :], 1024.0, None, ALU.add), t)
            t2 = dve.do(lambda e: e.tensor_copy(SI[:, 1, :], sf[:, 1, :]), t)
            t = dve.do(lambda e: e.tensor_scalar(sf[:, 1, :], sf[:, 0, :], 1024.0, None, ALU.is_lt), t2)
            t = dve.do(lambda e: e.tensor_tensor(sf[:, 1, :], sf[:, 1, :], sf[:, 0, :], ALU.mult), t)
            t = dve.do(lambda e: e.tensor_copy(GI[:, 0, :], sf[:, 1, :]), t)
            t_w["route"] = [t, t2, t_ev]

        t_sm = None
        sms.open.pop()
        kv_done["kb", 0] = kv_done["vb", 0] = None

        def wds():
            for c in range(2):
                for h in range(2):
                    yield from halves(WDH[:, c, h * 1024:(h + 1) * 1024], WDL[:, c, h * 1024:(h + 1) * 1024],
                                      A["WD"][c * 128:(c + 1) * 128, h * 1024:(h + 1) * 1024], 128, 1024, ("wdp", c, h))
            t_w["wd"] = [t_w["wdp", c, h] for c in range(2) for h in range(2)]
            yield act, lambda: [t_w["wd"], ring.peek() if len(ring.open) > 1 else BUSY]
            t = [ring.take()[1], ring.take()[1]]
            for k in range(2):
                bbs.give(k, t)
                slots.give(NX + k, t)

        def early():
            yield from halves(flat2(WoH[:, :, :]), flat2(WoL[:, :, :]),
                              A["w_o"].rearrange("(c p) n -> p c n", p=128), 128, 512, "o")
            for c in range(2):
                yield from halves(W1H[:, c, :], W1L[:, c, :], A["w1"][c * 128:(c + 1) * 128, :], 128, 1024, ("w1", c))
            for c in range(2):
                yield from halves(flat2(W2H[:, 4 * c:4 * c + 4, :]), flat2(W2L[:, 4 * c:4 * c + 4, :]),
                                  A["w2"][c * 512:(c + 1) * 512, :].rearrange("(j p) n -> p j n", p=128), 128, 1024,
                                  ("w2", c))
            yield from fold()
            yield from route()
            yield from wds()

        bbs.open.clear()
        work = [(0, halves(flat2(WqH[:, :, :]), flat2(WqL[:, :, :]),
                           A["w_q"].rearrange("(c p) n -> p c n", p=128), 128, 512, "q")),
                (0, keys0(0)), (0, values0(0)), (lag, early())]
        for g in range(NG):
            def add(fn, *a, name):
                work.append((g * lag + hand.get(name, 0.0), fn(g, *a)))
            add(load_x, name="ld")
            if g == 4:
                work += [(g * lag, keys0(1)), (g * lag, values0(1))]
            add(a1, name="a1")
            add(a2, name="a2")
            for i in range(2):
                add(score, i, name="sc")
                add(weigh, i, name="we")
            add(pv, name="pv")
            add(wo, name="wo")
            add(b1, name="b1")
            for j in range(4):
                add(w1, j, name="w1")
            add(w2, name="w2")
            add(b3, name="b3")
            add(c1, name="c1")
            add(c2, name="c2")
        for b in range(2):
            for r in range(8):
                o = (4 * b + 4) * lag + 0.1 * r + hand["ex"]
                work.append((o, expert(b, r)))
                work.append((o, bias(b, r)))
        schedule(work)
        sp.wait(*pairs_done)

        block = ctx.enter_context(nc.Block())
        block.sync(sp.run)
        block.tensor(pe.run)
        block.vector(dve.run)
        block.scalar(act.run)
        block.gpsimd(pool.run)


def table():
    pos = np.arange(1024, dtype=np.float32)[:, None]
    div = np.exp(np.arange(0, 32, 2, dtype=np.float32) * np.float32(-np.log(10000.0) / 32))
    ang = (pos * div.astype(np.float32)).astype(np.float32)
    pe = np.zeros((1024, 32), np.float32)
    pe[:, 0::2] = np.sin(ang)
    pe[:, 1::2] = np.cos(ang)
    return np.ascontiguousarray(pe.T)


def laid_out(i):
    p = "L0_xattn_"
    q = "L1_xattn_"
    a = {
        "x": i["x"].reshape(2048, 256),
        "ctx": i["ctx_768"],
        "ctxT": i["ctx_768"].transpose(2, 0, 1).reshape(192, 154),
        "w_q": i[p + "w_q"], "w_k": i[p + "w_k"], "w_v": i[p + "w_v"], "w_o": i[p + "w_o"],
        "w1": i["L0_ffn_w1"][0], "w2": i["L0_ffn_w2"][0],
        "Wk": i[q + "Wk"], "Wv": i[q + "Wv"], "Wq": i[q + "Wq"], "WqT": i[q + "Wq"].T, "Wo": i[q + "Wo"],
        "WD": i["L1_ffn_W"].transpose(2, 0, 1).reshape(256, 2048),
        "bD": i["L1_ffn_b"],
        "sigT": i["L1_ffn_tile_sigs"].T,
        "peT": table(),
        "cols": np.concatenate([i[p + "b_q"], i[p + "b_k"], i[q + "bk"], i[q + "bq"], i[q + "bv"],
                                i[q + "ln1_g"], i[q + "ln1_b"], i["L0_ffn_b1"][0]]).reshape(22, 128).T,
        "rows": np.stack([i[p + "b_o"], i["L0_ffn_b2"][0], i["L0_ffn_beta"], i["L0_ffn_gamma"],
                          i[q + "bo"], i[p + "b_v"]]),
        "rows2": np.stack([i[q + "ln2_g"], i[q + "ln2_b"]]),
    }
    return {k: np.ascontiguousarray(v) for k, v in a.items()}


def kernel(**inputs):
    import concourse.bacc as bacc
    from concourse.bass_utils import run_bass_kernel_spmd

    nc = bacc.Bacc("TRN2", target_bir_lowering=False, num_devices=1)
    arrays = laid_out({k: np.asarray(v) for k, v in inputs.items()})
    A = {k: nc.dram_tensor(f"in_{k}", a.shape, mybir.dt.from_np(a.dtype), kind="ExternalInput").ap()
         for k, a in arrays.items()}
    out = nc.dram_tensor("out_x", (2048, 256), F32, kind="ExternalOutput").ap()
    program(nc, A, out)
    r = run_bass_kernel_spmd(nc, [{f"in_{k}": a for k, a in arrays.items()}], core_ids=[0])
    return r.results[0]["out_x"].reshape(2, 1024, 256)
```

```python
from contextlib import ExitStack

import numpy as np
import concourse.bass as bass
from concourse import mybir

F32 = mybir.dt.float32
F32R = mybir.dt.float32r
I32 = mybir.dt.int32
BF16 = mybir.dt.bfloat16
ALU = mybir.AluOpType
ACT = mybir.ActivationFunctionType
AX = mybir.AxisListType.X

NX = 5
NXT = 4
NHF = 4
NXN = 4
NET = 2
NG = 8
NK = 77
EPS = 1e-5
CW = 124
NP = 15
BY_HEAD = ((0, 0), (1, 0))
ON_ACT = (1,)
LATE = (0, 6, 7)
LAG = 0.186
HAND = dict(ex=2.5, c2=0.4, w2=0.6, d1=1.1, k0=-1, r2=3, pv=0.1, qw=1, put=-1.0, ld=2.3, sx=-3, v1=0.3)
CF = 0.00105
CA = 0.00085
CP = 0.0023
CD = 1.4e-5


BUSY = "busy"


class Slots:

    def peek(self, spare=0):
        return self.open[0][1] if len(self.open) > spare else BUSY

    def __init__(self, n):
        self.open = [(k, None) for k in range(n)]

    def take(self):
        assert self.open, "too few buffers"
        return self.open.pop(0)

    def give(self, k, token):
        self.open.append((k, token))


class Queue:

    def __init__(self, sem):
        self.sem, self.count, self.code, self.seen, self.now = sem, 0, [], {}, 0.0

    def wait(self, *tokens):
        for t in tokens:
            if t is None:
                continue
            if isinstance(t, list):
                self.wait(*t)
                continue
            assert t is not BUSY, "a buffer that is still in use"
            sem, value, when = t
            self.now = max(self.now, when + LATENCY)
            if sem is self.sem and self.pe:
                continue
            if self.seen.get(id(sem), 0) < value:
                self.seen[id(sem)] = value
                self.code.append(lambda e, s=sem, v=value: e.wait_ge(s, v))

    pe = False

    def go(self, fn, *tokens, c=0.11):
        self.wait(*tokens)
        self.now += c
        self.code.append(fn)

    def do(self, fn, *tokens, c=0.11):
        self.wait(*tokens)
        self.now += c
        self.count += 1
        self.code.append(lambda e: fn(e).then_inc(self.sem, 1))
        return (self.sem, self.count, self.now)

    def run(self, eng):
        for fn in self.code:
            fn(eng)


LATENCY = 0.17


def ready(tokens):
    if tokens is BUSY:
        return None
    if tokens is None:
        return 0.0
    if isinstance(tokens, list):
        w = [ready(t) for t in tokens]
        return None if None in w else max(w, default=0.0)
    return tokens[2] + LATENCY


def schedule(work):
    live = []

    def advance(item):
        try:
            item[2] = next(item[1])
            live.append(item)
        except StopIteration:
            pass

    for handicap, gen in work:
        advance([handicap, gen, None])
    while live:
        best = None
        for n, (handicap, _, (queue, needs)) in enumerate(live):
            when = ready(needs())
            if when is not None:
                key = max(when, queue.now) + handicap
                if best is None or key < best[0]:
                    best = (key, n)
        assert best is not None, "no piece of work can go on"
        advance(live.pop(best[1]))


def f(ap):
    return ap.bitcast(F32)


def program(nc, A, out, lag=LAG, hand={}):
    with ExitStack() as ctx:
        def sb(name, shape, dt=F32):
            return ctx.enter_context(nc.sbuf_tensor(name, shape, dt))

        def sem(name):
            return ctx.enter_context(nc.semaphore(name))

        hand = {**HAND, **hand}
        S4 = ctx.enter_context(nc.psum_tensor("S4", [128, 2, 1024], F32))
        PB = [ctx.enter_context(nc.psum_tensor(f"PB{i}", [128, 512], F32)) for i in range(4)]

        pe, dve, act, pool = (Queue(sem(n)) for n in ("s_pe", "s_dve", "s_act", "s_pool"))
        sp = Queue(None)
        pe.pe = True

        dma = [0.0]

        def load(dst, src):
            s = sem(f"s_ld{len(sp.code)}")
            sp.go(lambda e: e.dma_start(dst, src).then_inc(s, 16))
            sp.now += 0.1
            n = 1
            for d in dst.shape:
                n *= d
            dma[0] = max(dma[0], sp.now) + n * CD
            return (s, 16, dma[0] + 1.8)

        def flat2(T):
            return T.rearrange("p a b -> p (a b)")

        ident = sb("ident", [128, 128])
        mask8 = sb("mask8", [128, 8])
        mask4 = sb("mask4", [128, 4])
        mask5 = sb("mask5", [CW, 5, 8])
        nhalf = sb("nhalf", [128, 2])
        t0 = dve.do(lambda e: e.memset(ident[:, :], 0.0))
        t1 = dve.do(lambda e: e.memset(mask8[:, :], 1.0))
        t2 = dve.do(lambda e: e.memset(mask5[:, :, :], 1.0))
        t_nh = dve.do(lambda e: e.memset(nhalf[:, :], -0.5))
        t_id = pool.do(lambda e: e.affine_select(out=ident[:, :], in_=ident[:, :], compare_op=ALU.not_equal,
                                                 fill=1.0, base=0, pattern=[[-1, 128]], channel_multiplier=1), t0)
        t = pool.do(lambda e: e.affine_select(out=mask8[:, :], in_=mask8[:, :], compare_op=ALU.is_ge, fill=0.0,
                                              base=0, pattern=[[-16, 8]], channel_multiplier=1), t1)
        t_m8 = pool.do(lambda e: e.affine_select(out=mask8[:, :], in_=mask8[:, :], compare_op=ALU.is_ge, fill=0.0,
                                                 base=15, pattern=[[16, 8]], channel_multiplier=-1), t)
        t = pool.do(lambda e: e.affine_select(out=mask5[:, :, :], in_=mask5[:, :, :], compare_op=ALU.is_ge,
                                              fill=0.0, base=0, pattern=[[CW, 5], [-NK, 8]],
                                              channel_multiplier=1), t2)
        t_m5 = pool.do(lambda e: e.affine_select(out=mask5[:, :, :], in_=mask5[:, :, :], compare_op=ALU.is_ge,
                                                 fill=0.0, base=NK - 1, pattern=[[-CW, 5], [NK, 8]],
                                                 channel_multiplier=-1), t)

        t_m4 = dve.do(lambda e: e.tensor_tensor(mask4[:, :], mask8[:, 0:4], mask8[:, 4:8], ALU.add), t_m8)

        X = sb("X", [128, NG, 2, 256])
        slots = Slots(NX)
        x_v = A["x"].rearrange("(g i p) n -> g p i n", i=2, p=128)
        t_x0 = load(X[:, 0, :, :], x_v[0])
        XN = sb("XN", [128, NXN, 2, 256])
        xns = Slots(NXN)
        WD = sb("WD", [128, 2, 2048])
        peT = WD[0:32, 1, 0:1024]
        ctxT = sb("ctxT", [96, 2, 2 * NK])
        t_ctxT = load(ctxT[:, :, :], A["ctxT"].rearrange("(c p) n -> p c n", p=96))
        RAW = sb("RAW", [128, 2, 1024])
        cols = sb("cols", [128, 22])
        COLS = dict(b_q=0, b_k=2, bk1=4, bq1=6, bv1=8, g1=10, be1=12, b1=14)
        t_cols = load(cols[:, :], A["cols"])
        WKV = sb("WKV", [96, 2, 512])
        t_wkv = load(WKV[:, :, 0:256], A["w_k"].rearrange("(c p) n -> p c n", p=96))
        t_wvv = load(WKV[:, :, 256:512], A["w_v"].rearrange("(c p) n -> p c n", p=96))
        bc = sb("bc", [128, 6, 256])
        BO, B2, BETA, GAMMA, BO1, BV = range(6)
        ring = Slots(2)
        kwq = ring.take()[0]
        wq = A["w_q"].rearrange("(c p) n -> p c n", p=128)
        t_wq = load(RAW[:, kwq, 0:512].rearrange("p (c n) -> p c n", c=2), wq)
        sg = sb("sg", [32, 3, 8])
        t_sg = load(sg[:, 0, :], A["sigT"])
        t_pe = load(peT, A["peT"])
        t_bc = load(bc[:, :, :], A["rows"].rearrange("(a r) n -> a r n", a=1).to_broadcast([128, 6, 256]))

        def two(ap):
            return ap.rearrange("p (a b) -> p a b", a=2)

        WqH, WqL = (sb(n, [128, 2, 256], F32R) for n in ("WqH", "WqL"))
        Wo = sb("Wo", [128, 2, 256])
        t_w_o = load(Wo[:, :, :], A["w_o"].rearrange("(c p) n -> p c n", p=128))
        W1H, W1L = (sb(n, [128, 2, 1024], F32R) for n in ("W1H", "W1L"))
        W2H, W2L = (sb(n, [128, 8, 256], F32R) for n in ("W2H", "W2L"))

        XTE = sb("XTE", [128, 2, 1024])
        XTH = sb("XTH", [128, NXT, 2, 256], F32R)
        XTL = sb("XTL", [128, NXT, 2, 256], F32R)
        E = sb("E", [128, 2, 2, 5 * CW])
        t_pad = dve.do(lambda e: e.memset(E[:, :, :, 8 * NK:5 * CW], 0.0))
        ET = sb("ET", [CW, NET, 2, 5, 256])
        RR = sb("RR", [128, 2, 128])
        RT = sb("RT", [128, NET, 2, 256])
        KBH = sb("KBH", [128, 16, NK], F32R)
        KBL = sb("KBL", [128, 16, NK], F32R)
        VB = sb("VB", [CW, 5, 2, 128])
        HF = sb("HF", [128, NHF, 2, 256])
        HH = sb("HH", [128, 8, 256], F32R)
        HL = sb("HL", [128, 8, 256], F32R)
        SM = sb("SM", [128, 12, 2, 11])
        SX = sb("SX", [128, 2, 3, 16])
        ST = sb("ST", [NK, 256])
        PP = sb("PP", [128, 2, NK])
        PS = sb("PS", [128, 4, 2])
        PTT = sb("PTT", [96, 256])
        M1 = sb("M1", [128, 2, 2, NK])
        M2 = sb("M2", [96, 2, 256])
        cT = sb("cT", [NK, 2])
        SI = sb("SI", [128, 16], I32)
        EI = sb("EI", [128, 8], I32)
        EV = sb("EV", [1, 3, 16], I32)
        MK = sb("MK", [128, 16])
        BS = RAW[:, :, :].rearrange("p a (b n) -> p (a b) n", n=256)

        x3 = nc.dram_tensor("x3", (1024, 256), F32, kind="Internal").ap()

        banks, s4, xts, sms = Slots(4), Slots(2), Slots(NXT), Slots(12)
        es, ets, rrs, hhs, hfs, pps, sts, ptts = (Slots(n) for n in (2, NET, 2, 1, NHF, 1, 1, 1))

        class State(dict):
            def __missing__(self, k):
                return BUSY

        t_w = State()
        gs = [State(b=g // 4) for g in range(NG)]
        kv_done = State()

        def col(name, m):
            c = COLS[name] + m
            return cols[:, c:c + 1]

        def rows(r, n=2):
            return bc[:, r, :].unsqueeze(1).to_broadcast([128, n, 256])


        def stage(src, parts, n, k, tf):
            sp.wait(tf)
            dst = RAW[0:parts, k, 0:n]
            return dst, load(dst if len(src.shape) == 2 else dst.rearrange("p (a b) -> p a b", a=src.shape[1]), src)

        def halves(H, L, src, parts, n, name, loaded=None):
            if loaded:
                k, t = loaded
                raw = RAW[0:parts, k, 0:n]
            else:
                yield sp, ring.peek
                k, tf = ring.take()
                raw, t = stage(src, parts, n, k, tf)
            yield act, lambda: t
            th = act.do(lambda e: e.activation(H, raw, ACT.Copy), t, c=n * CA)
            yield pool, lambda: th
            tl = pool.do(lambda e: e.tensor_tensor(L, raw, f(H), ALU.subtract), th, t, c=n * CP)
            ring.give(k, tl)
            t_w[name] = tl

        def norm(src, need, scale1=1.0, add=EPS, n=2, spare=0):
            yield dve, lambda: [need(), xns.peek(spare), sms.peek()]
            t_src = need()
            k, tf = xns.take()
            m, tm = sms.take()
            dst = XN[:, k, :, :]
            dve.wait(tm)
            for i in range(n):
                st = SM[:, m, i, 0:6]
                t = dve.do(lambda e, i=i, st=st: e.bn_stats(st, src[:, i, :]), t_src, c=0.33)
            for i in range(n):
                st = SM[:, m, i, 0:6]
                mv = SM[:, m, i, 6:8]
                t = dve.do(lambda e, st=st, mv=mv: e.bn_aggr(mv, st), t, c=0.08)
            t = dve.do(lambda e: e.tensor_scalar(SM[:, m, 0:n, 8], SM[:, m, 0:n, 7], scale1, add, ALU.mult, ALU.add),
                       t, c=0.08)
            yield pool, lambda: t
            t = pool.do(lambda e: e.tensor_tensor(SM[:, m, 0:n, 9], SM[:, m, 0:n, 8], nhalf[:, 0:n], ALU.pow), t,
                        t_nh, c=0.6)
            yield dve, lambda: t
            tm = dve.do(lambda e: e.scalar_tensor_tensor(out=SM[:, m, :, 10], in0=SM[:, m, :, 6], scalar=-1.0,
                                                         in1=SM[:, m, :, 9], op0=ALU.mult, op1=ALU.mult), t, c=0.08)
            ts = [dve.do(lambda e: e.tensor_scalar(dst[:, 0, :], src[:, 0, :], SM[:, m, 0, 6:7],
                                                   SM[:, m, 0, 9:10], ALU.subtract, ALU.mult), t, tf, c=0.33)]
            yield act, lambda: tm
            ts.append(act.do(lambda e: e.activation(dst[:, 1, :], src[:, 1, :], ACT.Identity,
                                                    bias=SM[:, m, 1, 10:11], scale=SM[:, m, 1, 9:10]),
                             tm, t, tf, c=0.46))
            sms.give(m, ts)
            return dst, ts, k

        def turn(xn, t_xn, n=2, spare=0, split=True):
            pool_ = xts if split else xns
            yield pe, lambda: [t_xn, banks.peek(), pool_.peek(spare)]
            p, tb = banks.take()
            k, tf = pool_.take()
            w = n * 128
            pe.wait(t_xn, t_id, tb)
            for i in range(n):
                for c in range(2):
                    fn = (lambda e, i=i, c=c: e.transpose(PB[p][:, c * w + i * 128:c * w + (i + 1) * 128],
                                                          xn[:, i, c * 128:(c + 1) * 128], ident[:, :]))
                    if i + c < n:
                        pe.go(fn)
                    else:
                        t = pe.do(fn)
            H, L = XTH[:, k, :, 0:w], XTL[:, k, :, 0:w]
            src = PB[p][:, 0:2 * w].rearrange("p (c t) -> p c t", c=2)
            yield act, lambda: t
            if not split:
                XT = XN[:, k, :, :]
                t1 = act.do(lambda e: e.activation(XT, src, ACT.Copy), t, tf, c=2 * w * CA)
                banks.give(p, t1)
                return XT, t1, k, t
            th = act.do(lambda e: e.activation(H, src, ACT.Copy), t, tf, c=2 * w * CA)
            yield dve, lambda: th
            tl = dve.do(lambda e: e.tensor_tensor(L, src, f(H), ALU.subtract), th, t, c=2 * w * CF)
            banks.give(p, tl)
            return H, L, tl, k, t

        def three(dst, pairs, waits=(), c=0.109, first=True, last=True):
            n = len(pairs) * 3
            j = 0
            pe.wait(*waits)
            for (sh, sl), (mh, ml) in pairs:
                for a, b in ((sh, mh), (sh, ml), (sl, mh)):
                    fn = lambda e, a=a, b=b, j=j: e.matmul(dst, a, b, start=first and (j == 0),
                                                                stop=last and (j == n - 1))
                    j += 1
                    if j < n:
                        pe.go(fn, c=c)
                    else:
                        t = pe.do(fn, c=c)
            return t

        def full(dst, pairs, waits=(), c=0.43):
            pe.wait(*waits)
            for j, (a, b) in enumerate(pairs):
                fn = lambda e, a=a, b=b, j=j: e.matmul(dst, a, b, start=(j == 0), stop=(j == len(pairs) - 1))
                if j < len(pairs) - 1:
                    pe.go(fn, c=c)
                else:
                    t = pe.do(fn, c=c)
            return t


        def keys0(b):
            yield pe, lambda: [banks.peek(), xns.peek(), hfs.peek(), t_ctxT, t_wkv]
            n, tb = banks.take()
            kx, tx = xns.take()
            kh, th_ = hfs.take()
            KF, KT = (flat2(T)[:, 0:4 * NK].rearrange("p (m k) -> p m k", m=4)
                      for T in (XN[:, kx, :, :], HF[:, kh, :, :]))
            for m in range(2):
                t = full(PB[n][:, m * NK:(m + 1) * NK],
                         [(WKV[:, c, m * 128:(m + 1) * 128], ctxT[:, c, b * NK:(b + 1) * NK]) for c in range(2)],
                         (t_ctxT, t_wkv, tb))
            yield dve, lambda: [t, t_cols, kv_done["kb", b]]
            for m in range(4):
                own = slice(64 * (m % 2), 64 * (m % 2) + 64)
                for to in (slice(0, 64), slice(64, 128)):
                    tk = dve.do(lambda e, m=m, own=own, to=to: e.tensor_scalar(
                        KF[to, m, :], PB[n][own, m // 2 * NK:(m // 2 + 1) * NK], col("b_k", m // 2)[own, :], 0.25,
                        ALU.add, ALU.mult), t, t_cols, tx, c=0.15)
            t = tk
            banks.give(n, t)
            KHr = KBH[:, 0:4, :]
            th = dve.do(lambda e: e.tensor_copy(KHr, KF), t, kv_done["kb", b], c=0.2)
            t1 = dve.do(lambda e: e.tensor_tensor(KF, KF, f(KHr), ALU.subtract), th, c=0.35)
            t2 = dve.do(lambda e: e.tensor_copy(KT, f(KHr)), t1, th_, c=0.2)
            for m in range(4):
                t = dve.do(lambda e, m=m: e.tensor_tensor(
                    KBL[:, 4 * m:4 * m + 4, :], KF[:, m, :].unsqueeze(1).to_broadcast([128, 4, NK]),
                    mask4[:, :].unsqueeze(2).to_broadcast([128, 4, NK]), ALU.mult), t2, t_m4, c=0.38)
            yield act, lambda: t2
            for h in range(4):
                tb = act.do(lambda e, h=h: e.activation(
                    KBH[:, :, :].rearrange("p (m h) k -> p m h k", h=4)[:, :, h, :], KT, ACT.Copy,
                    scale=mask4[:, h:h + 1]), t2, t_m4, c=0.41)
            t = [t, tb]
            xns.give(kx, t)
            hfs.give(kh, t)
            t_w["kb", b] = t

        def values0(b):
            tv = kv_done["vb", b]
            yield act, lambda: [t_ctxT, ets.peek(), kv_done["vb", b]]
            tv = kv_done["vb", b]
            kr, tr = ets.take()
            CR = RT[0:96, kr, :, 0:2 * CW].rearrange("p a (b t) -> p a b t", b=2)
            crs = [[tr], [tr]]
            for c in range(5):
                k = c % 2
                yield act, lambda: crs[k]
                r = CW * c
                end = min(r + CW, 8 * NK)
                while r < end:
                    key = r % NK
                    n = min(end - r, NK - key)
                    o = r - CW * c
                    t = act.do(lambda e, o=o, n=n, key=key, k=k: e.activation(
                        CR[:, k, :, o:o + n], ctxT[:, :, b * NK + key:b * NK + key + n], ACT.Copy),
                        t_ctxT, crs[k], c=0.2)
                    r += n
                yield pe, lambda: [t, banks.peek()]
                p, tb = banks.take()
                t = full(PB[p][0:CW, 0:256], [(CR[:, k, j, 0:CW], WKV[:, j, 256:512]) for j in range(2)],
                         (t, t_wvv, tb))
                crs[k] = [t]
                yield dve, lambda: [t, t_bc, hfs.peek()]
                kf, tf = hfs.take()
                VF = HF[0:CW, kf, 0, :]
                t = dve.do(lambda e, p=p, VF=VF: e.tensor_tensor(VF, PB[p][0:CW, 0:256], bc[0:CW, BV, :], ALU.add),
                           t, t_bc, tf, c=0.33)
                banks.give(p, t)
                t = dve.do(lambda e, c=c, VF=VF: e.tensor_tensor(
                    VB[:, c, :, :].rearrange("p a (h d) -> p a h d", h=8),
                    VF.rearrange("p (a h d) -> p a h d", a=2, h=8),
                    mask5[0:CW, c, :].unsqueeze(1).unsqueeze(3).to_broadcast([CW, 2, 8, 16]), ALU.mult),
                    t, t_m5, tv, c=0.33)
                hfs.give(kf, t)
            ets.give(kr, [crs[0], crs[1]])
            t_w["vb", b] = t


        def load_x(g):
            s = gs[g]
            s["x"] = X[:, g, :, :]
            if g == 0:
                s["kx"], _ = slots.take()
                s["x0"] = t_x0
                return
            if g < 4:
                yield sp, lambda: [slots.peek(), gs[g - 1]["x0"]]
                s["kx"], tf = slots.take()
                s["x0"] = load(s["x"], x_v[g])
                return
            yield pool, lambda: [slots.peek(), t_w["route"], gs[g - 1]["x0"], gs[g - 1]["begun"]]
            s["kx"], tf = slots.take()
            sx0 = sem(f"s_x{g}")
            pool.wait(tf, t_w["route"])
            for i in range(2):
                q = 2 * g + i
                pool.go(lambda e, i=i, q=q: e.indirect_dma_start(
                    X[:, g, i, :], None, A["x"][:, :],
                    bass.IndirectOffsetOnAxis(ap=SI[:, q:q + 1], axis=0)).then_inc(sx0, 16), c=1.0)
            s["x0"] = (sx0, 32, pool.now + 2.0)

        def a1(g):
            s = gs[g]
            yield dve, lambda: s["x0"]
            xn, t, k = yield from norm(s["x"], lambda: s["x0"])
            s["begun"] = t
            s["t_xr"] = pool.do(lambda e: e.tensor_tensor(s["x"], s["x"], rows(BO), ALU.add), t, t_bc, c=1.2)
            s["H"], s["L"], t_xt, s["k"], tp = yield from turn(xn, t, spare=1)
            s["xt"] = t_xt
            xns.give(k, tp)

        def a2(g):
            s = gs[g]
            yield pe, lambda: [s["xt"], t_w["q"], banks.peek(), xts.peek()]
            H, L = s["H"], s["L"]
            p, tb = banks.take()
            s["kq"], tf = xts.take()
            for m in range(2):
                ms = slice(m * 128, (m + 1) * 128)
                t = three(PB[p][:, m * 256:(m + 1) * 256],
                          [((WqH[:, c, ms], WqL[:, c, ms]), (H[:, c, :], L[:, c, :])) for c in range(2)],
                          (s["xt"], t_w["q"], tb))
            xts.give(s["k"], t)
            Q = [[T[:, s["kq"], m, :] for T in (XTH, XTL)] for m in range(2)]
            s["q"] = Q
            mu = [(m, u, slice(64 * u, 64 * u + 64), slice(64 - 64 * u, 128 - 64 * u))
                  for m in range(2) for u in range(2)]
            yield act, lambda: t
            for m, u, own, other in mu:
                th = act.do(lambda e, m=m, u=u, own=own: e.activation(
                    Q[m][u][own, :], PB[p][own, m * 256:(m + 1) * 256], ACT.Identity, bias=col("b_q", m)[own, :]),
                    t, t_cols, tf, c=0.36)
            yield dve, lambda: th
            for m, u, own, other in mu:
                tl = dve.do(lambda e, m=m, u=u, own=own, other=other: e.scalar_tensor_tensor(
                    out=Q[m][u][other, :], in0=PB[p][own, m * 256:(m + 1) * 256], scalar=col("b_q", m)[own, :],
                    in1=f(Q[m][u][own, :]), op0=ALU.add, op1=ALU.subtract), th, t, tf, c=0.35)
            banks.give(p, tl)
            s["t_q"] = tl

        def score(g, i, a):
            s = gs[g]
            b = s["b"]
            before = lambda: s["scored", i, a - 1] if a else s["scored", i - 1, 1] if i else None
            yield pe, lambda: [s["t_q"], t_w["kb", b], s4.peek(), es.peek() if a == 0 else s["te", i], before()]
            k4, t4 = s4.take()
            if a == 0:
                s["ke", i], s["te", i] = es.take()
            ke, te = s["ke", i], s["te", i]
            ts = slice(i * 128, (i + 1) * 128)
            for u in range(2):
                h = 8 * a + 4 * u
                kh = KBH[:, h:h + 4, :].rearrange("p h k -> p (h k)")
                kl = KBL[:, h:h + 4, :].rearrange("p h k -> p (h k)")
                t = full(S4[:, k4, u * 512:u * 512 + 4 * NK], [(s["q"][a][u][:, ts], kh), (s["q"][a][u][:, ts], kl)],
                         (s["t_q"], t_w["kb", b], t4), c=0.131)
            s["scored", i, a] = t
            if i + a == 2:
                xts.give(s["kq"], t)
                if g == 3:
                    kv_done["kb", 1] = t
            hs = slice(8 * a, 8 * a + 8)
            sx = SX[:, ke, :, :]
            sv = S4[:, k4, :].rearrange("p (u n) -> p u n", u=2)[:, :, 0:4 * NK].rearrange("p u (h k) -> p u h k", k=NK)
            Ei = E[:, ke, a, 0:8 * NK]
            mx = sx[:, 0, hs].rearrange("p (u h) -> p u h", u=2)
            yield dve, lambda: [t, te]
            t = dve.do(lambda e: e.tensor_reduce(mx, sv, AX, ALU.max), t, te, c=0.71)
            if (i, a) in BY_HEAD:
                t = dve.do(lambda e: e.tensor_scalar(sx[:, 2, hs], sx[:, 0, hs], -1.0, None, ALU.mult), t, c=0.07)
                yield act, lambda: t
                for h in range(8):
                    th = act.do(lambda e, h=h: e.activation(
                        Ei[:, h * NK:(h + 1) * NK], S4[:, k4, h // 4 * 512 + h % 4 * NK:h // 4 * 512 + (h % 4 + 1) * NK],
                        ACT.Exp, bias=sx[:, 2, 8 * a + h:8 * a + h + 1],
                        accum_out=sx[:, 1, 8 * a + h:8 * a + h + 1]), t, te, t_pad, c=0.3)
                s4.give(k4, th)
                s["t_e", i, a] = th
                yield dve, lambda: th
                s["t_r", i, a] = dve.do(lambda e: e.reciprocal(sx[:, 2, hs], sx[:, 1, hs]), th, c=0.11)
                return
            t = dve.do(lambda e: e.tensor_tensor(Ei.rearrange("p (u h k) -> p u h k", u=2, h=4), sv,
                                                 mx.unsqueeze(3).to_broadcast([128, 2, 4, NK]), ALU.subtract), t,
                       t_pad, c=0.71)
            s4.give(k4, t)
            yield act, lambda: t
            t = act.do(lambda e: e.activation(Ei, Ei, ACT.Exp), t, c=0.57)
            s["t_e", i, a] = t
            yield dve, lambda: t
            t = dve.do(lambda e: e.tensor_reduce(sx[:, 1, hs], Ei.rearrange("p (h k) -> p h k", h=8), AX, ALU.add), t,
                       c=0.71)
            s["t_r", i, a] = dve.do(lambda e: e.reciprocal(sx[:, 2, hs], sx[:, 1, hs]), t, c=0.11)

        def weigh(g, i, a):
            s = gs[g]
            yield act, lambda: [s["t_r", i, a], rrs.peek()]
            kr, trr = rrs.take()
            ke = s["ke", i]
            rf = RR[:, kr, :]
            t_r = act.do(lambda e: e.activation(rf.rearrange("p (h d) -> p h d", h=8), SX[:, ke, 2, 8 * a:8 * a + 8]
                                                .unsqueeze(2).to_broadcast([128, 8, 16]), ACT.Copy),
                         s["t_r", i, a], trr, c=0.17)
            first = i == 0 and a == 0
            yield pe, lambda: [t_r, s["t_e", i, a], s4.peek(), ets.peek() if first else s["et"]]
            if first:
                s["ket"], s["et"] = ets.take()
            tet = s["et"]
            k4, t4 = s4.take()
            pe.wait(s["t_e", i, a], t4)
            pe.go(lambda e: e.transpose(S4[:, k4, 640:768], rf, ident[:, :]), t_r)
            for c in range(5):
                t = pe.do(lambda e, c=c: e.transpose(S4[0:CW, k4, c * 128:(c + 1) * 128],
                                                      E[:, ke, a, c * CW:(c + 1) * CW], ident[:, :]))
            rrs.give(kr, t)
            s["turned", i, a] = t
            if ("turned", i, 1 - a) in s:
                es.give(ke, [s["turned", i, 0], s["turned", i, 1]])
            ts = slice(i * 128, (i + 1) * 128)
            src = S4[0:CW, k4, 0:640].rearrange("p (c t) -> p c t", c=5)
            yield act, lambda: [t, tet]
            ket = s["ket"]
            tr = act.do(lambda e: e.activation(RT[:, ket, a, ts], S4[:, k4, 640:768], ACT.Copy), t, tet, c=0.17)
            th = act.do(lambda e: e.activation(ET[:, ket, a, :, ts], src, ACT.Copy), t, tet, c=0.06 + 640 * CA)
            s4.give(k4, th)
            s["t_et", i, a], s["t_rt", i, a] = th, tr

        def pv(g):
            s = gs[g]
            b = s["b"]
            both = lambda name, a: [s[name, 0, a], s[name, 1, a]]
            need = lambda: [both("t_et", 0), t_w["vb", b], banks.peek()]
            yield pe, need
            w = need()
            p, _ = banks.take()
            ket = s["ket"]
            for a in range(2):
                if a:
                    yield pe, lambda: [t, both("t_et", 1)]
                    w = [both("t_et", 1)]
                t = full(PB[p][:, a * 256:(a + 1) * 256], [(VB[:, c, a, :], ET[:, ket, a, c, :]) for c in range(5)],
                         w[:3])
            if g == 3:
                kv_done["vb", 1] = t
            rt = [both("t_rt", 0), both("t_rt", 1)]
            yield dve, lambda: [t, rt]
            R = RT[:, ket, :, :]
            t = dve.do(lambda e: e.tensor_tensor(R, two(PB[p][:, :]), R, ALU.mult), t, rt, c=0.6)
            banks.give(p, t)
            s["o"], s["t_o"] = R, t

        def wo(g):
            s = gs[g]
            yield pe, lambda: [s["t_o"], banks.peek()]
            p, tb = banks.take()
            for i in range(2):
                ts = slice(i * 128, (i + 1) * 128)
                t = full(PB[p][:, i * 256:(i + 1) * 256], [(s["o"][:, a, ts], Wo[:, a, :]) for a in range(2)],
                         (s["t_o"], t_w_o, tb))
            ets.give(s["ket"], t)
            yield dve, lambda: [t, s["t_xr"]]
            t = dve.do(lambda e: e.tensor_tensor(s["x"], two(PB[p][:, :]), s["x"], ALU.add), t, s["t_xr"], c=0.6)
            banks.give(p, t)
            s["x1"] = t

        def b1(g):
            s = gs[g]
            yield dve, lambda: s["x1"]
            xn, t, k = yield from norm(s["x"], lambda: s["x1"], spare=1)
            s["t_x1b"] = pool.do(lambda e: e.tensor_tensor(s["x"], s["x"], rows(BETA), ALU.add), t, c=1.2)
            s["H"], s["L"], t_xt, s["k"], tp = yield from turn(xn, t)
            s["t_xrb"] = pool.do(lambda e: e.tensor_tensor(xn, xn, rows(B2), ALU.add), tp, t, c=1.2)
            s["y"], s["ky"] = xn, k
            s["hused"] = []
            s["xt1"] = t_xt

        def w1(g, j):
            s = gs[g]
            yield pe, lambda: [s["xt1"], t_w["w1", 0], t_w["w1", 1], banks.peek(), hfs.peek(),
                               hhs.peek() if j == 0 else s["hh"]]
            if j == 0:
                s["khh"], s["hh"] = hhs.take()
            tf = s["hh"]
            H, L = s["H"], s["L"]
            p, tb = banks.take()
            k, tk = hfs.take()
            for q in range(2):
                fs = slice((2 * j + q) * 128, (2 * j + q + 1) * 128)
                t = three(PB[p][:, q * 256:(q + 1) * 256],
                          [((W1H[:, c, fs], W1L[:, c, fs]), (H[:, c, :], L[:, c, :])) for c in range(2)],
                          (s["xt1"], t_w["w1", 0], t_w["w1", 1], tb))
            s["hused"].append(t)
            if len(s["hused"]) == 4:
                xts.give(s["k"], s["hused"])
            yield act, lambda: t
            for q in range(2):
                t2 = act.do(lambda e, q=q: e.activation(HF[:, k, q, :], PB[p][:, q * 256:(q + 1) * 256], ACT.Relu,
                                                        bias=col("b1", 2 * j + q)), t, t_cols, tk, c=0.36)
            banks.give(p, t2)
            hs = slice(2 * j, 2 * j + 2)
            if j in ON_ACT:
                th = act.do(lambda e: e.activation(HH[:, hs, :], HF[:, k, :, :], ACT.Copy), t2, tf, c=0.5)
            else:
                yield dve, lambda: t2
                th = dve.do(lambda e: e.tensor_copy(HH[:, hs, :], HF[:, k, :, :]), t2, tf, c=0.33)
            q_, c_ = (dve, 0.6) if g in LATE and j in (1, 3) else (pool, 1.2)
            yield q_, lambda: th
            tl = q_.do(lambda e: e.tensor_tensor(HL[:, hs, :], HF[:, k, :, :], f(HH[:, hs, :]), ALU.subtract), th,
                       t2, tf, c=c_)
            hfs.give(k, tl)
            s["t_h", j] = tl

        def w2(g):
            s = gs[g]
            hs = lambda: [s["t_h", j] for j in range(4)]
            yield pe, lambda: [hs(), t_w["w2", 0], t_w["w2", 1], banks.peek()]
            p, tb = banks.take()
            for i in range(2):
                ts = slice(i * 128, (i + 1) * 128)
                pairs = [((HH[:, j, ts], HL[:, j, ts]), (W2H[:, j, :], W2L[:, j, :])) for j in range(8)]
                for a in range(0, 8, 4):
                    if i + a:
                        yield pe, lambda: t
                    t = three(PB[p][:, i * 256:(i + 1) * 256], pairs[a:a + 4],
                              (hs(), t_w["w2", 0], t_w["w2", 1], tb), first=a == 0, last=a == 4)
            hhs.give(s["khh"], t)
            yield dve, lambda: [t, s["t_xrb"]]
            y = s["y"]
            t = dve.do(lambda e: e.tensor_tensor(y, two(PB[p][:, :]), y, ALU.add), t, s["t_xrb"], c=0.6)
            banks.give(p, t)
            s["t_y"] = t

        def b3(g):
            s = gs[g]
            q_, c_ = (dve, 0.6) if g in LATE else (pool, 1.2)
            yield dve, lambda: s["t_y"]
            yn, t, k = yield from norm(s["y"], lambda: s["t_y"])
            xns.give(s["ky"], t)
            yield q_, lambda: [t, s["t_x1b"]]
            t = q_.do(lambda e: e.tensor_tensor(yn, yn, rows(GAMMA), ALU.mult), t, t_bc, c=c_)
            t = q_.do(lambda e: e.tensor_tensor(s["x"], yn, s["x"], ALU.add), t, s["t_x1b"], c=c_)
            xns.give(k, t)
            s["x2"] = t

        def c1(g):
            s = gs[g]
            yield dve, lambda: s["x2"]
            xn, t, k = yield from norm(s["x"], lambda: s["x2"], 1.0 + EPS, EPS * EPS, spare=1)
            s["t_xrc"] = pool.do(lambda e: e.tensor_tensor(s["x"], s["x"], rows(BO1), ALU.add), t, c=1.2)
            s["XT"], t_xt, s["k"], tp = yield from turn(xn, t, split=False)
            s["xt2"] = t_xt
            xns.give(k, tp)

        def c2(g):
            s = gs[g]
            b = s["b"]
            yield pe, lambda: [s["xt2"], t_w["m1"], banks.peek(), pps.peek(), sts.peek()]
            n1, tb = banks.take()
            _, tpp = pps.take()
            _, tst = sts.take()
            XT = s["XT"]
            t = full(PB[n1][0:NK, 0:256], [(M1[:, c, b, :], XT[:, c, :]) for c in range(2)], (s["xt2"], t_w["m1"], tb))
            xns.give(s["k"], t)
            yield act, lambda: t
            t = act.do(lambda e: e.activation(ST[:, :], PB[n1][0:NK, 0:256], ACT.Identity, bias=cT[:, b:b + 1]), t,
                       t_w["m1"], tst, c=0.36)
            yield pe, lambda: t
            for i in range(2):
                t = pe.do(lambda e, i=i: e.transpose(PB[n1][:, i * NK:(i + 1) * NK], ST[:, i * 128:(i + 1) * 128],
                                                     ident[0:NK, 0:NK]), t)
            sts.give(0, t)
            sv = PB[n1][:, 0:2 * NK].rearrange("p (i k) -> p i k", i=2)
            yield dve, lambda: t
            t = dve.do(lambda e: e.tensor_reduce(PS[:, 0, :], sv, AX, ALU.max), t, tpp, c=0.23)
            t = dve.do(lambda e: e.tensor_tensor(PP[:, :, :], sv, PS[:, 0, :].unsqueeze(2)
                                                 .to_broadcast([128, 2, NK]), ALU.subtract), t, tpp, c=0.23)
            banks.give(n1, t)
            yield act, lambda: t
            t = act.do(lambda e: e.activation(PP[:, :, :], PP[:, :, :], ACT.Exp), t, c=0.2)
            yield dve, lambda: t
            t = dve.do(lambda e: e.tensor_reduce(PS[:, 1, :], PP[:, :, :], AX, ALU.add), t, c=0.2)
            t = dve.do(lambda e: e.reciprocal(PS[:, 2, :], PS[:, 1, :]), t, c=0.08)
            t = dve.do(lambda e: e.tensor_tensor(PP[:, :, :], PP[:, :, :], PS[:, 2, :].unsqueeze(2)
                                                 .to_broadcast([128, 2, NK]), ALU.mult), t, c=0.2)
            yield pe, lambda: [t, banks.peek(), ptts.peek()]
            n, tb = banks.take()
            _, tpt = ptts.take()
            for i in range(2):
                t = pe.do(lambda e, i=i, n=n: e.transpose(PB[n][0:NK, i * 128:(i + 1) * 128], PP[:, i, :],
                                                          ident[:, :]), t, tb)
            pps.give(0, t)
            yield act, lambda: [t, t_w["pz"]]
            t = act.do(lambda e, n=n: e.activation(PTT[0:NK, :], PB[n][0:NK, 0:256], ACT.Copy), t, t_w["pz"], tpt,
                       c=0.28)
            yield pe, lambda: [t, t_w["m2"]]
            for i in range(2):
                tm = full(PB[n][:, i * 256:(i + 1) * 256], [(PTT[:, i * 128:(i + 1) * 128], M2[:, b, :])],
                          (t, t_w["m2"]))
            t = tm
            ptts.give(0, t)
            yield dve, lambda: [t, s["t_xrc"]]
            t = dve.do(lambda e, n=n: e.tensor_tensor(s["x"], two(PB[n][:, :]), s["x"], ALU.add), t, s["t_xrc"],
                       c=0.6)
            banks.give(n, t)
            slots.give(s["kx"], t)
            if b == 0:
                yield sp, lambda: t
                sp.wait(t)
                s["kept"] = load(x3[g * 256:(g + 1) * 256, :].rearrange("(i p) n -> p i n", i=2), s["x"])
            else:
                s["x3"] = t

        def sort_x(g):
            s = gs[g]
            kept = lambda: [gs[j]["kept"] for j in range(4)]
            yield pool, lambda: [kept(), t_w["route"]]
            sx3 = sem(f"s_y{g}")
            pool.wait(kept(), t_w["route"])
            for i in range(2):
                q = 2 * g + i
                pool.go(lambda e, i=i, q=q: e.indirect_dma_start(
                    X[:, g, i, :], None, x3[:, :],
                    bass.IndirectOffsetOnAxis(ap=SI[:, q:q + 1], axis=0)).then_inc(sx3, 16), c=1.0)
            s["x3"] = (sx3, 32, pool.now + 2.0)


        def d1(g):
            s = gs[g]
            yield dve, lambda: s["x3"]
            xn, t, k = yield from norm(s["x"], lambda: s["x3"])
            yield pool, lambda: [t, t_w["bs"]]
            s["t_bs"] = pool.do(lambda e: e.tensor_tensor(s["x"], s["x"], BS[:, 2 * (g % 4):2 * (g % 4) + 2, :],
                                                          ALU.add), t, t_w["bs"], c=1.2)
            yield pe, lambda: [t, banks.peek()]
            p, tb = banks.take()
            pe.wait(t, t_id, tb)
            for c in range(2):
                for i in range(2):
                    tp = pe.do(lambda e, i=i, c=c: e.transpose(PB[p][:, c * 256 + i * 128:c * 256 + (i + 1) * 128],
                                                               xn[:, i, c * 128:(c + 1) * 128], ident[:, :]))
            xns.give(k, tp)
            free = (lambda: copied[0, g % 4 + 4]) if g >= 4 else (lambda: None)
            yield act, lambda: [tp, free()]
            o = (g % 4) * 256
            t = act.do(lambda e: e.activation(XTE[:, :, o:o + 256], two(PB[p][:, :]), ACT.Copy), tp, free(), c=0.49)
            banks.give(p, t)
            s["xte"] = t

        regs = {}
        copied, added = State(), State()

        def register(e, queue, row, n, most):
            if (id(queue), n) not in regs:
                regs[id(queue), n] = e.value_load(EV[0:1, row, n:n + 1], min_val=0, max_val=most)
            return regs[id(queue), n]

        def pairs(b, r):
            ns = [n for n in (2 * r, 2 * r + 1) if n < NP]
            last = 4 * b + min(r, 3)
            xte = lambda: [gs[g]["xte"] for g in range(4 * b, last + 1)]
            yield act, lambda: [xte(), hfs.peek(), t_w["route2"]]
            k, tf = hfs.take()
            act.wait(xte(), tf, t_w["route2"])
            for i, n in enumerate(ns):
                xp = HF[:, k, i, :].rearrange("p (c t) -> p c t", c=2)

                def copy(e, n=n, xp=xp):
                    v = register(e, act, 2, n, 7 * 128)
                    return e.activation(xp, XTE[:, :, bass.ds(v, 128)], ACT.Copy)
                t = act.do(copy, c=0.3 + (0 if b else 0.4))
            copied[b, r] = t
            yield pe, lambda: [t, t_w["wd"], banks.peek()]
            p, tb = banks.take()
            pe.wait(t, t_w["wd"], tb, t_w["route2"])
            for i, n in enumerate(ns):
                for c in range(2):
                    def product(e, i=i, n=n, c=c):
                        v = register(e, pe, 0, n, 7 * 256)
                        return e.matmul(PB[p][:, i * 256:(i + 1) * 256], HF[:, k, i, c * 128:(c + 1) * 128],
                                        WD[:, c, bass.ds(v, 256)], start=c == 0, stop=c == 1)
                    t = pe.do(product, c=0.43)
            hfs.give(k, t)
            need = lambda: [gs[last]["t_bs"], added[b, r - 1] if r else None]
            yield dve, lambda: [t, need()]
            dve.wait(t, [gs[g]["t_bs"] for g in range(4 * b, last + 1)], t_w["route2"])
            ta = need()
            for i, n in enumerate(ns):
                def add(e, i=i, n=n):
                    v = register(e, dve, 1, n, 7 * 256)
                    x = X[:, 4 * b:4 * b + 4, :, :].rearrange("p g i n -> p (g i n)")[:, bass.ds(v, 256)]
                    return e.scalar_tensor_tensor(out=x, in0=PB[p][:, i * 256:(i + 1) * 256], scalar=MK[:, n:n + 1],
                                                  in1=x, op0=ALU.mult, op1=ALU.add)
                ta = dve.do(add, ta, c=0.4 + (0 if b else 0.37))
            banks.give(p, ta)
            added[b, r] = ta

        def put(g):
            b = g // 4
            r = g % 4 + 4
            yield pool, lambda: added[b, r]
            pool.wait(added[b, r])
            s_o = sem(f"s_o{g}")
            for i in range(2):
                q = 2 * g + i
                pool.go(lambda e, i=i, q=q: e.indirect_dma_start(
                    out[:, :], bass.IndirectOffsetOnAxis(ap=SI[:, q:q + 1], axis=0), X[:, g, i, :],
                    None).then_inc(s_o, 16), c=1.0)
            stored.append((s_o, 32, pool.now + 2.0))

        stored = []


        def fold():
            yield sp, lambda: [ring.peek(), t_w["pe"]]
            CK, CN = (WD[0:NK, 1, o:o + 384].rearrange("p (b n) -> p b n", b=2) for o in (0, 384))
            sp.wait(t_w["pe"])
            t_ck = load(CK, A["ctx"].rearrange("b k n -> k b n"))
            kg, tf = ring.take()
            sp.wait(tf)
            GB = RAW[0:NK, kg, 0:384].rearrange("p (r n) -> p r n", r=2)
            t_gb = load(GB, A["rows2"].rearrange("(a r) n -> a r n", a=1).to_broadcast([NK, 2, 192]))
            m = 11
            yield dve, lambda: t_ck
            for i in range(2):
                t = dve.do(lambda e, i=i: e.bn_stats(SM[0:NK, m, i, 0:6], CK[:, i, :]), t_ck, t_w["pe"], c=0.25)
                t = dve.do(lambda e, i=i: e.bn_aggr(SM[0:NK, m, i, 6:8], SM[0:NK, m, i, 0:6]), t, c=0.08)
            t = dve.do(lambda e: e.tensor_scalar(SM[0:NK, m, :, 8], SM[0:NK, m, :, 7], EPS, None, ALU.add), t, c=0.08)
            yield pool, lambda: t
            t = pool.do(lambda e: e.tensor_tensor(SM[0:NK, m, :, 9], SM[0:NK, m, :, 8], nhalf[0:NK, :], ALU.pow), t,
                        t_nh, c=0.6)
            yield dve, lambda: [t, t_gb]
            for i in range(2):
                t1 = dve.do(lambda e, i=i: e.tensor_scalar(CN[:, i, :], CK[:, i, :], SM[0:NK, m, i, 6:7],
                                                           SM[0:NK, m, i, 9:10], ALU.subtract, ALU.mult), t, c=0.26)
            t = dve.do(lambda e: e.tensor_tensor(CN, CN, GB[:, 0, :].unsqueeze(1).to_broadcast([NK, 2, 192]),
                                                 ALU.mult), t1, t_gb, c=0.46)
            t = dve.do(lambda e: e.tensor_tensor(CN, CN, GB[:, 1, :].unsqueeze(1).to_broadcast([NK, 2, 192]),
                                                 ALU.add), t, c=0.46)
            ring.give(kg, t)
            yield pe, lambda: [t, banks.peek()]
            n, tb = banks.take()
            for c in range(2):
                for i in range(2):
                    o = (c * 2 + i) * NK
                    tt = pe.do(lambda e, c=c, i=i, o=o, n=n: e.transpose(PB[n][0:96, o:o + NK],
                                                                         CN[:, i, c * 96:(c + 1) * 96],
                                                                         ident[0:NK, 0:NK]), t, t_id, tb)
            yield act, lambda: tt
            K1S, V1S, CT = (WD[:, 0, 1024 + o:1024 + o + 4 * NK].rearrange("p (m k) -> p m k", m=2)
                            for o in (0, 4 * NK, 8 * NK))
            CT = CT[0:96, :, :]
            t_ct = act.do(lambda e, n=n: e.activation(CT, PB[n][0:96, 0:4 * NK].rearrange("p (c k) -> p c k", c=2),
                                                      ACT.Copy), tt, c=0.3)
            banks.give(n, t_ct)
            done = {}
            for name, dst, bias in (("Wk", K1S, "bk1"), ("Wv", V1S, "bv1")):
                yield sp, ring.peek
                kk, tf = ring.take()
                w, tw = stage(A[name].rearrange("(c p) n -> p c n", p=96), 96, 512, kk, tf)
                wv = two(w)
                yield pe, lambda: [t_ct, tw, banks.peek()]
                n, tb = banks.take()
                for m_ in range(2):
                    tp = full(PB[n][:, m_ * 154:(m_ + 1) * 154],
                              [(wv[:, c, m_ * 128:(m_ + 1) * 128], CT[:, c, :]) for c in range(2)],
                              (t_ct, tw, tb))
                ring.give(kk, tp)
                yield dve, lambda: [tp, t_cols]
                for m_ in range(2):
                    td = dve.do(lambda e, m=m_, n=n, dst=dst, bias=bias: e.tensor_scalar(
                        dst[:, m, :], PB[n][:, m * 154:(m + 1) * 154], col(bias, m), None, ALU.add), tp, t_cols,
                        c=0.22)
                banks.give(n, td)
                done[bias] = td
            t_k1, t_v1 = done["bk1"], done["bv1"]
            yield sp, ring.peek
            k, tf = ring.take()
            wqT, t_wqT = stage(A["WqT"].rearrange("(c p) n -> p c n", p=128), 128, 512, k, tf)
            wqT = two(wqT)
            yield pe, lambda: [t_k1, t_wqT, banks.peek()]
            n, tb = banks.take()
            for m_ in range(2):
                t = full(PB[n][:, m_ * 154:(m_ + 1) * 154],
                         [(wqT[:, c, m_ * 128:(m_ + 1) * 128], K1S[:, c, :]) for c in range(2)],
                         (t_k1, t_wqT, tb))
            ring.give(k, t)
            yield dve, lambda: t
            for m_ in range(2):
                t1 = dve.do(lambda e, m=m_, n=n: e.tensor_scalar(
                    M1[:, m, :, :], PB[n][:, m * 154:(m + 1) * 154].rearrange("p (b k) -> p b k", b=2),
                    col("g1", m), 0.0625, ALU.mult, ALU.mult), t, c=0.22)
            banks.give(n, t1)
            yield sp, ring.peek
            k, tf = ring.take()
            wqn, t_wqn = stage(A["Wq"].rearrange("(c p) n -> p c n", p=128), 128, 512, k, tf)
            wqn = two(wqn)
            yield pe, lambda: [t_wqn, banks.peek()]
            n, tb = banks.take()
            for m_ in range(2):
                t = full(PB[n][:, m_:m_ + 1], [(wqn[:, c, m_ * 128:(m_ + 1) * 128], col("be1", c)) for c in range(2)],
                         (t_wqn, t_cols, tb))
            ring.give(k, t)
            yield dve, lambda: t
            tq = dve.do(lambda e, n=n: e.tensor_tensor(PS[:, 3, :], PB[n][:, 0:2],
                                                       cols[:, COLS["bq1"]:COLS["bq1"] + 2], ALU.add), t, c=0.1)
            yield pe, lambda: tq
            for b in range(2):
                t = full(PB[n][0:NK, 4 + b:5 + b], [(K1S[:, c, b * NK:(b + 1) * NK], PS[:, 3, c:c + 1])
                                                    for c in range(2)], (tq,))
            yield dve, lambda: t
            tc = dve.do(lambda e, n=n: e.tensor_scalar(cT[:, :], PB[n][0:NK, 4:6], 0.0625, None, ALU.mult), t, c=0.1)
            banks.give(n, tc)
            t_w["m1"] = tc
            yield sp, ring.peek
            k, tf = ring.take()
            wo1, t_wo1 = stage(A["Wo"].rearrange("(c p) n -> p c n", p=128), 128, 512, k, tf)
            wo1 = two(wo1)
            yield pe, lambda: [t_v1, t_wo1, banks.peek()]
            n, tb = banks.take()
            for b in range(2):
                t = full(PB[n][0:NK, b * 256:(b + 1) * 256],
                         [(V1S[:, c, b * NK:(b + 1) * NK], wo1[:, c, :]) for c in range(2)],
                         (t_v1, t_wo1, tb))
            ring.give(k, t)
            yield dve, lambda: t
            tz = dve.do(lambda e: e.memset(M2[64:96, :, :], 0.0), c=0.3)
            t_w["pz"] = dve.do(lambda e: e.memset(PTT[64:96, :], 0.0), c=0.2)
            t = dve.do(lambda e, n=n: e.tensor_copy(M2[0:NK, :, :], PB[n][0:NK, :].rearrange("p (b n) -> p b n", b=2)),
                       t, tz, c=0.6)
            banks.give(n, t)
            t_w["m2"] = t


        def route():
            room = WD[:, 0, 0:512]
            RK, PI, SID = room[:, 0:128], room[:, 128:129], room[:, 136:144]
            mx, V, B, BE, zf = (room[:, o:o + a * n].rearrange("p (a n) -> p a n", a=a) for o, a, n in
                                ((144, 4, 8), (176, 2, 16), (208, 4, 16), (272, 16, 2), (304, 3, 8)))
            room2 = WD[:, 0, 512:1024]
            big = room2[:, 0:256].rearrange("p (a b) -> p a b", b=16)
            eq, tri, hoh = (r_[:, o:o + 64].rearrange("p (a b) -> p a b", b=8)
                            for r_, o in ((room, 328), (room, 392), (room2, 256)))
            half = WD[:, 1, 1024:1536].bitcast(BF16)
            LO = half[:, 0:1024].rearrange("p (j i) -> p j i", i=128)
            half = WD[:, 1, 1536:2048].bitcast(BF16)
            LT, ON = half[:, 0:128], half[:, 128:256]
            OHM = half[:, 256:320].rearrange("p (j t) -> p j t", t=8)
            HI = half[:, 320:448].rearrange("p (j t) -> p j t", t=16)
            yield dve, lambda: t_sg
            t = dve.do(lambda e: e.tensor_scalar(sg[:, 1, :], sg[:, 0, :], 0.0, None, ALU.is_gt), t_sg)
            t = dve.do(lambda e: e.tensor_scalar(sg[:, 2, :], sg[:, 0, :], 0.0, None, ALU.is_lt), t)
            t = dve.do(lambda e: e.tensor_tensor(sg[:, 1, :], sg[:, 1, :], sg[:, 2, :], ALU.subtract), t)
            to = dve.do(lambda e: e.memset(half[:, 0:256], 1.0))
            yield pe, lambda: [t, t_pe, banks.peek()]
            n1, tb = banks.take()
            for j in range(8):
                tp = pe.do(lambda e, j=j: e.matmul(PB[n1][:, j * 8:(j + 1) * 8], peT[:, j * 128:(j + 1) * 128],
                                                   sg[:, 1, :], start=True, stop=True), t, t_pe, tb, c=0.43)
            t_w["pe"] = tp
            yield pool, lambda: to
            tlt = pool.do(lambda e: e.affine_select(out=LT, in_=LT, compare_op=ALU.is_ge, fill=0.0, base=-1,
                                                    pattern=[[1, 128]], channel_multiplier=-1), to)
            ti = pool.do(lambda e: e.iota(RK[:, :], [[1, 128]], base=0, channel_multiplier=0,
                                          allow_small_or_imprecise_dtypes=True), c=0.3)
            ti = pool.do(lambda e: e.iota(PI[:, :], [[1, 1]], base=0, channel_multiplier=1,
                                          allow_small_or_imprecise_dtypes=True))
            ti = pool.do(lambda e: e.iota(SID[:, :], [[128, 8]], base=0, channel_multiplier=1,
                                          allow_small_or_imprecise_dtypes=True))
            sc = PB[n1][:, 0:64].rearrange("p (j t) -> p j t", t=8)

            def in1(a, w):
                return a.unsqueeze(2).to_broadcast([128, a.shape[1], w])

            def in0(a, w):
                return a.unsqueeze(1).to_broadcast([128, w, a.shape[1]])

            yield dve, lambda: ti
            rk = RK[:, 0:8]
            trv = dve.do(lambda e: e.tensor_scalar(mx[:, 2, :], rk, -1.0, 8.0, ALU.mult, ALU.add), ti)
            t2 = dve.do(lambda e: e.tensor_tensor(tri, in1(rk, 8), in0(rk, 8), ALU.is_gt), ti)
            tv = dve.do(lambda e: e.tensor_scalar(V[:, 0, 8:16], rk, 128.0, 128.0, ALU.mult, ALU.add), ti)
            yield dve, lambda: tp
            rev = in0(mx[:, 2, :], 8)
            t = dve.do(lambda e: e.tensor_reduce(mx[:, 0, :], sc, AX, ALU.max), tp)
            t = dve.do(lambda e: e.tensor_tensor(eq, sc, in1(mx[:, 0, :], 8), ALU.is_equal), t)
            banks.give(n1, t)
            t = dve.do(lambda e: e.tensor_tensor(eq, eq, rev, ALU.mult), t, trv)
            t = dve.do(lambda e: e.tensor_reduce(mx[:, 1, :], eq, AX, ALU.max), t)
            t = dve.do(lambda e: e.tensor_tensor(OHM, in1(mx[:, 1, :], 8), rev, ALU.is_equal), t)
            yield pe, lambda: [t, tlt, banks.peek()]
            n, tb = banks.take()
            pe.wait(t, tlt, tb)
            for j in range(8):
                for i in range(j + 1):
                    pe.go(lambda e, i=i, j=j: e.matmul(PB[n][:, j * 8:(j + 1) * 8], LT if i == j else ON, OHM[:, i, :],
                                                       start=i == 0, stop=i == j), c=0.03)
            for j in range(8):
                tp = pe.do(lambda e, j=j: e.matmul(PB[n][:, 64:72], ON, OHM[:, j, :], start=j == 0, stop=j == 7),
                           c=0.05)
            rank = PB[n][:, 0:64].rearrange("p (j t) -> p j t", t=8)
            yield dve, lambda: tp
            S = V[:, 0, 0:8]
            t = dve.do(lambda e: e.tensor_tensor(tri, tri, in0(PB[n][:, 64:72], 8), ALU.mult), tp, t2)
            ts = dve.do(lambda e: e.tensor_reduce(S, tri, AX, ALU.add), t, tv)
            t = dve.do(lambda e: e.tensor_tensor(eq, rank, in0(S, 8), ALU.add), ts)
            banks.give(n, t)
            t = dve.do(lambda e: e.tensor_tensor(eq, eq, OHM, ALU.mult), t)
            t = dve.do(lambda e: e.tensor_reduce(mx[:, 0, :], eq, AX, ALU.add), t)
            t = dve.do(lambda e: e.tensor_tensor(eq[:, :, 0:7], in1(mx[:, 0, :], 7), in0(V[:, 0, 8:15], 8),
                                                 ALU.is_ge), t, tv)
            t = dve.do(lambda e: e.tensor_reduce(mx[:, 1, :], eq[:, :, 0:7], AX, ALU.add), t)
            t = dve.do(lambda e: e.scalar_tensor_tensor(out=mx[:, 3, :], in0=mx[:, 1, :], scalar=-128.0,
                                                        in1=mx[:, 0, :], op0=ALU.mult, op1=ALU.add), t)
            tl = dve.do(lambda e: e.tensor_tensor(LO, in1(mx[:, 3, :], 128), in0(RK[:, :], 8), ALU.is_equal), t, c=1.1)
            t = dve.do(lambda e: e.tensor_tensor(hoh, in1(mx[:, 1, :], 8), in0(rk, 8), ALU.is_equal), t)
            t1 = dve.do(lambda e: e.tensor_scalar(HI[:, :, 0:8], hoh, PI[:, 0:1], None, ALU.mult), t)
            t = dve.do(lambda e: e.tensor_tensor(HI[:, :, 8:16], hoh, in1(rk, 8), ALU.mult), t)
            yield pe, lambda: [t, tl, banks.peek()]
            n2, tb = banks.take()
            pe.wait(t, tl, tb)
            for j in range(8):
                tp = pe.do(lambda e, j=j: e.matmul(PB[n2][:, 0:16], LO[:, j, :], HI[:, j, :], start=j == 0,
                                                        stop=j == 7), c=0.05)
            yield dve, lambda: tp
            t = dve.do(lambda e: e.tensor_copy(zf[:, 2, :], PB[n2][:, 0:8]), tp)
            t = dve.do(lambda e: e.scalar_tensor_tensor(out=zf[:, 0, :], in0=PB[n2][:, 8:16], scalar=128.0,
                                                             in1=zf[:, 2, :], op0=ALU.mult, op1=ALU.add), t)
            banks.give(n2, t)
            t = dve.do(lambda e: e.tensor_scalar(zf[:, 1, :], zf[:, 0, :], 1024.0, None, ALU.add), t)
            t = dve.do(lambda e: e.tensor_copy(SI[:, :], flat2(zf[:, 0:2, :])), t)
            t_w["route"] = t
            rest.append((ts, RK, PI, SID, mx, V, B, BE, big, eq, in0, in1))

        rest = []

        def stretches():
            yield dve, lambda: t_w["route"]
            ts, RK, PI, SID, mx, V, B, BE, big, eq, in0, in1 = rest[0]
            t = dve.do(lambda e: e.scalar_tensor_tensor(out=V[:, 1, :], in0=V[:, 0, :], scalar=16.0, in1=RK[:, 0:16],
                                                        op0=ALU.mult, op1=ALU.add), ts)
            t = dve.do(lambda e: e.tensor_tensor(big, in1(V[:, 1, :], 16), in0(V[:, 1, :], 16), ALU.is_gt), t, c=0.3)
            t = dve.do(lambda e: e.tensor_reduce(B[:, 0, :], big, AX, ALU.add), t, c=0.3)
            t = dve.do(lambda e: e.tensor_tensor(big, in0(B[:, 0, :], 16), in1(RK[:, 0:16], 16), ALU.is_equal), t,
                       c=0.3)
            t = dve.do(lambda e: e.tensor_tensor(big, big, in0(V[:, 0, :], 16), ALU.mult), t, c=0.3)
            t = dve.do(lambda e: e.tensor_reduce(B[:, 1, :], big, AX, ALU.add), t, c=0.3)
            t = dve.do(lambda e: e.tensor_tensor(big[:, :, 0:14], in1(B[:, 1, :], 14), in0(V[:, 0, 1:15], 16),
                                                 ALU.is_ge), t, c=0.3)
            for a in range(2):
                te = dve.do(lambda e, a=a: e.tensor_reduce(BE[:, :, a], big[:, :, 7 * a:7 * a + 7], AX, ALU.add), t,
                            c=0.2)
            t = dve.do(lambda e: e.scalar_tensor_tensor(out=B[:, 2, :], in0=BE[:, :, 1], scalar=-128.0,
                                                        in1=B[:, 1, :], op0=ALU.mult, op1=ALU.add), te)
            t = dve.do(lambda e: e.scalar_tensor_tensor(out=B[:, 3, 0:15], in0=BE[:, 0:15, 1], scalar=-128.0,
                                                        in1=B[:, 1, 1:16], op0=ALU.mult, op1=ALU.add), t)
            t = dve.do(lambda e: e.tensor_scalar(B[:, 2, :], B[:, 2, :], PI[:, 0:1], None, ALU.is_le), t)
            t = dve.do(lambda e: e.scalar_tensor_tensor(out=MK[:, 0:15], in0=B[:, 3, 0:15], scalar=PI[:, 0:1],
                                                        in1=B[:, 2, 0:15], op0=ALU.is_gt, op1=ALU.mult), t)
            for a, (r_, m_) in enumerate(((0, 256.0), (1, 256.0), (1, 128.0))):
                t = dve.do(lambda e, a=a, r_=r_, m_=m_: e.tensor_scalar(B[0:1, a, :], BE[0:1, :, r_], m_, None,
                                                                        ALU.mult), t)
            t = dve.do(lambda e: e.tensor_copy(EV[:, :, :], B[0:1, 0:3, :]), t)
            t_w["route2"] = t
            yield dve, lambda: t
            t = dve.do(lambda e: e.tensor_tensor(eq[:, :, 0:7], in1(SID[:, :], 7), in0(V[:, 0, 1:8], 8), ALU.is_ge), t)
            t = dve.do(lambda e: e.tensor_reduce(mx[:, 0, :], eq[:, :, 0:7], AX, ALU.add), t)
            t = dve.do(lambda e: e.tensor_copy(EI[:, :], mx[:, 0, :]), t)
            t_w["ei"] = t

        sms.open.pop()
        kv_done["kb", 0] = kv_done["vb", 0] = None

        def wds():
            for c in range(2):
                if c == 0:
                    yield sp, lambda: [t_w["ei"], t_w["m2"]]
                    sp.wait(t_w["ei"], t_w["m2"])
                t = load(WD[:, c, :], A["WD"][c * 128:(c + 1) * 128, :])
                t_w["wd"] = [t] if c == 0 else t_w["wd"] + [t]
            yield pool, lambda: [t_w["ei"], ring.peek(1)]
            w = [ring.take()[1], ring.take()[1], t_w["ei"]]
            s_bs = sem("s_bs")
            for q in range(8):
                if q:
                    yield pool, lambda: None
                pool.wait(w)
                pool.go(lambda e, q=q: e.indirect_dma_start(
                    BS[:, q, :], None, A["bD"][:, :],
                    bass.IndirectOffsetOnAxis(ap=EI[:, q:q + 1], axis=0)).then_inc(s_bs, 16), c=1.0)
            t_w["bs"] = (s_bs, 128, pool.now + 2)

        def early():
            for c in range(2):
                yield from halves(W1H[:, c, :], W1L[:, c, :], A["w1"][c * 128:(c + 1) * 128, :], 128, 1024, ("w1", c))
            for c in range(2):
                yield from halves(flat2(W2H[:, 4 * c:4 * c + 4, :]), flat2(W2L[:, 4 * c:4 * c + 4, :]),
                                  A["w2"][c * 512:(c + 1) * 512, :].rearrange("(j p) n -> p j n", p=128), 128, 1024,
                                  ("w2", c))
            yield from fold()
            yield from wds()

        work = [(hand.get("rt", 0.0), route()), (hand.get("r2", 0.0), stretches()), (hand.get("qw", 0.0), halves(flat2(WqH[:, :, :]), flat2(WqL[:, :, :]),
                           wq, 128, 512, "q", loaded=(kwq, t_wq))),
                (hand.get("k0", 0.0), keys0(0)), (hand.get("v0", 0.0), values0(0)),
                (hand.get("ea", 0.0), early())]
        for g in range(NG):
            def add(fn, *a, name):
                work.append((g * lag + hand.get(name, 0.0), fn(g, *a)))
            add(load_x, name="ld")
            if g == 4:
                work += [(g * lag + hand.get("k1", 0.0), keys0(1)), (g * lag + hand.get("v1", 0.0), values0(1))]
            add(a1, name="a1")
            add(a2, name="a2")
            for i in range(2):
                for a in range(2):
                    add(score, i, a, name="sc")
                    add(weigh, i, a, name="we")
            add(pv, name="pv")
            add(wo, name="wo")
            add(b1, name="b1")
            for j in range(4):
                add(w1, j, name="w1")
            add(w2, name="w2")
            add(b3, name="b3")
            add(c1, name="c1")
            add(c2, name="c2")
            if g < 4:
                add(sort_x, name="sx")
            add(d1, name="d1")
            work.append((g * lag + hand.get("put", 0.0), put(g)))
        for b in range(2):
            for r in range(8):
                work.append(((4 * b + min(r, 3)) * lag + hand["ex"], pairs(b, r)))
        schedule(work)
        sp.wait(*stored)

        block = ctx.enter_context(nc.Block())
        block.sync(sp.run)
        block.tensor(pe.run)
        block.vector(dve.run)
        block.scalar(act.run)
        block.gpsimd(pool.run)


def table():
    pos = np.arange(1024, dtype=np.float32)[:, None]
    div = np.exp(np.arange(0, 32, 2, dtype=np.float32) * np.float32(-np.log(10000.0) / 32))
    ang = (pos * div.astype(np.float32)).astype(np.float32)
    pe = np.zeros((1024, 32), np.float32)
    pe[:, 0::2] = np.sin(ang)
    pe[:, 1::2] = np.cos(ang)
    return np.ascontiguousarray(pe.T)


def laid_out(i):
    p = "L0_xattn_"
    q = "L1_xattn_"
    a = {
        "x": i["x"].reshape(2048, 256),
        "ctx": i["ctx_768"],
        "ctxT": i["ctx_768"].transpose(2, 0, 1).reshape(192, 154),
        "w_q": i[p + "w_q"], "w_k": i[p + "w_k"], "w_v": i[p + "w_v"], "w_o": i[p + "w_o"],
        "w1": i["L0_ffn_w1"][0], "w2": i["L0_ffn_w2"][0],
        "Wk": i[q + "Wk"], "Wv": i[q + "Wv"], "Wq": i[q + "Wq"], "WqT": i[q + "Wq"].T, "Wo": i[q + "Wo"],
        "WD": i["L1_ffn_W"].transpose(2, 0, 1).reshape(256, 2048),
        "bD": i["L1_ffn_b"],
        "sigT": i["L1_ffn_tile_sigs"].T,
        "peT": table(),
        "cols": np.concatenate([i[p + "b_q"], i[p + "b_k"], i[q + "bk"], i[q + "bq"], i[q + "bv"],
                                i[q + "ln1_g"], i[q + "ln1_b"], i["L0_ffn_b1"][0]]).reshape(22, 128).T,
        "rows": np.stack([i[p + "b_o"], i["L0_ffn_b2"][0], i["L0_ffn_beta"], i["L0_ffn_gamma"],
                          i[q + "bo"], i[p + "b_v"]]),
        "rows2": np.stack([i[q + "ln2_g"], i[q + "ln2_b"]]),
    }
    return {k: np.ascontiguousarray(v) for k, v in a.items()}


def kernel(**inputs):
    import concourse.bacc as bacc
    from concourse.bass_utils import run_bass_kernel_spmd

    nc = bacc.Bacc("TRN2", target_bir_lowering=False, num_devices=1)
    arrays = laid_out({k: np.asarray(v) for k, v in inputs.items()})
    A = {k: nc.dram_tensor(f"in_{k}", a.shape, mybir.dt.from_np(a.dtype), kind="ExternalInput").ap()
         for k, a in arrays.items()}
    out = nc.dram_tensor("out_x", (2048, 256), F32, kind="ExternalOutput").ap()
    program(nc, A, out)
    r = run_bass_kernel_spmd(nc, [{f"in_{k}": a for k, a in arrays.items()}], core_ids=[0])
    return r.results[0]["out_x"].reshape(2, 1024, 256)
```
